# Optimizing a Trainium2 kernel written in Bass

```python
import numpy as np
import jax
import jax.numpy as jnp

def _softmax(x, axis=-1):
    return jax.nn.softmax(x, axis=axis)

def _gelu(x):
    return jax.nn.gelu(x, approximate=True)

def _silu(x):
    return jax.nn.silu(x)

def _sigmoid(x):
    return jax.nn.sigmoid(x)

def _layernorm(x, axis=-1, eps=1e-05):
    m = jnp.mean(x, axis=axis, keepdims=True)
    v = jnp.var(x, axis=axis, keepdims=True)
    return (x - m) / jnp.sqrt(v + eps)

def _scatter_add(tgt, idx, src, axis=0):
    return tgt.at[idx].add(src)

def _segment_sum(src, seg, n):
    return jax.ops.segment_sum(src, seg, n)
kernel_name = 'mk_adj_resnorm_d4_adj_r2_78206c'

def setup_inputs(seed: int=0):
    np.random.seed(seed)
    _w = jnp.asarray

    def _rec_inputs():
        import jax
        import jax.numpy as jnp
        _gk = jax.random.key(seed)
        x = 7.22e-05 + 1 * jax.random.normal(jax.random.fold_in(_gk, 1), (64, 128, 128), jnp.float32)
        _w = (1.0 + jnp.arange(128, dtype=jnp.float32)) ** (-0.5)
        _w = _w / _w.mean()
        _pij = jnp.clip(0.125 * _w[:, None] * _w[None, :], 0.0, 1.0)
        _a = jax.random.uniform(jax.random.fold_in(_gk, 2), (64, 128, 128)) < _pij
        _af = _a.astype(jnp.float32)
        adj = _af
        _nm = jnp.ones((64, 128), dtype=bool)
        nodemask = jnp.where(_nm, 1.0, 0.0).astype(jnp.float32)
        return (x, adj, nodemask)
    x, adj, nodemask = _rec_inputs()

    def _L0_gnn_setup():
        import jax, jax.numpy as jnp
        import numpy as np
        B, N, D, C, L = (64, 256, 128, 128, 5)
        EDGE_P = 0.02

        def _gru_cell(m, h, w_ih, w_hh, b_ih, b_hh):
            gi = m @ w_ih.T + b_ih
            gh = h @ w_hh.T + b_hh
            i_r, i_z, i_n = jnp.split(gi, 3, axis=-1)
            h_r, h_z, h_n = jnp.split(gh, 3, axis=-1)
            r = jax.nn.sigmoid(i_r + h_r)
            z = jax.nn.sigmoid(i_z + h_z)
            n = jnp.tanh(i_n + r * h_n)
            return (1.0 - z) * n + z * h
        key = jax.random.key(seed)
        ks = jax.random.split(key, 8)
        x = jax.random.normal(ks[0], (B, N, D), dtype=jnp.float32)
        adj = (jax.random.uniform(ks[1], (B, N, N)) < EDGE_P).astype(jnp.float32)
        mask = jnp.ones((B, N), dtype=jnp.float32)
        s = 1.0 / np.sqrt(C).astype(np.float32)
        weight = jax.random.uniform(ks[2], (L, C, C), minval=-s, maxval=s, dtype=jnp.float32)
        w_ih = jax.random.uniform(ks[3], (3 * C, C), minval=-s, maxval=s, dtype=jnp.float32)
        w_hh = jax.random.uniform(ks[4], (3 * C, C), minval=-s, maxval=s, dtype=jnp.float32)
        b_ih = jax.random.uniform(ks[5], (3 * C,), minval=-s, maxval=s, dtype=jnp.float32)
        b_hh = jax.random.uniform(ks[6], (3 * C,), minval=-s, maxval=s, dtype=jnp.float32)
        return dict(x=x, adj=adj, mask=mask, weight=weight, w_ih=w_ih, w_hh=w_hh, b_ih=b_ih, b_hh=b_hh)
    _L0_gnn_all = _L0_gnn_setup()
    _L0_gnn_in = {k: v for k, v in _L0_gnn_all.items() if k in ('weight', 'w_ih', 'w_hh', 'b_ih', 'b_hh')}
    del _L0_gnn_all

    def _L1_gnn_setup():
        import jax, jax.numpy as jnp
        import numpy as np
        GROUPS = [list(range(25)), [0, 1, 2, 3, 4, 5, 6, 7, 8], [0, 9, 10, 11, 12, 13, 14], [6, 7, 8, 12, 13, 14], [3, 4, 5, 9, 10, 11]]
        B, N, D_IN, D_HID = (4096, 25, 128, 256)

        def _graph_conv(x, adj, W, b):
            n = adj.shape[-1]
            A = adj + jnp.eye(n, dtype=adj.dtype)
            deg = jnp.sum(A, axis=-1)
            deg_safe = jnp.where(deg == 0, 1.0, deg)
            dinv = jnp.where(deg == 0, 0.0, deg_safe ** (-0.5))
            norm_adj = dinv[:, :, None] * A * dinv[:, None, :]
            support = jnp.einsum('bnd,de->bne', x, W)
            out = jnp.einsum('bnm,bme->bne', norm_adj, support) + b
            return jax.nn.relu(out)
        key = jax.random.key(seed)
        ks = jax.random.split(key, 7)
        s1 = float(np.sqrt(6.0 / (D_IN + D_HID)))
        s2 = float(np.sqrt(6.0 / (D_HID + D_IN)))
        return {'x': jax.random.normal(ks[0], (B, N, D_IN), dtype=jnp.float32), 'adj': jax.random.uniform(ks[1], (B, N, N), dtype=jnp.float32), 'W1': jax.random.uniform(ks[2], (5, D_IN, D_HID), jnp.float32, -s1, s1), 'b1': jnp.zeros((5, D_HID), dtype=jnp.float32), 'W2': jax.random.uniform(ks[3], (5, D_HID, D_IN), jnp.float32, -s2, s2), 'b2': jnp.zeros((5, D_IN), dtype=jnp.float32), 'fusion_w': jnp.ones((5,), dtype=jnp.float32)}
    _L1_gnn_all = _L1_gnn_setup()
    _L1_gnn_in = {k: v for k, v in _L1_gnn_all.items() if k in ('W1', 'b1', 'W2', 'b2', 'fusion_w')}
    del _L1_gnn_all

    def _L2_gnn_setup():
        import jax, jax.numpy as jnp
        import numpy as np
        ALPHA = 0.2
        EPS = 1e-05
        NEG = -9000000000000000.0
        key = jax.random.key(seed)
        k1, k2, k3, k4 = jax.random.split(key, 4)
        B, N, F_in, F_out = (8, 1024, 128, 128)
        h = jax.random.normal(k1, (B, N, F_in), dtype=jnp.float32)
        adj = jax.random.randint(k2, (B, N, N), 0, 2).astype(jnp.float32)
        W = jax.random.normal(k3, (F_in, F_out), dtype=jnp.float32) * (1.414 * np.sqrt(2.0 / (F_in + F_out)))
        a = jax.random.normal(k4, (2 * F_out, 1), dtype=jnp.float32) * (1.414 * np.sqrt(2.0 / (2 * F_out + 1)))
        gamma = jnp.ones((F_out,), dtype=jnp.float32)
        beta = jnp.zeros((F_out,), dtype=jnp.float32)
        return {'h': h, 'adj': adj, 'W': W, 'a': a, 'gamma': gamma, 'beta': beta}
    _L2_gnn_all = _L2_gnn_setup()
    _L2_gnn_in = {k: v for k, v in _L2_gnn_all.items() if k in ('W', 'a', 'gamma', 'beta')}
    del _L2_gnn_all

    def _L3_gnn_setup():
        import jax, jax.numpy as jnp
        import numpy as np
        B, N, D = (8, 256, 128)
        key = jax.random.key(seed)
        ks = jax.random.split(key, 10)
        s = 1.0 / np.sqrt(D)
        u = lambda k, shape: jax.random.uniform(k, shape, jnp.float32, -s, s)
        return {'h_e': jax.random.normal(ks[0], (B, N, D), jnp.float32), 'adj': jax.random.uniform(ks[1], (B, N, N), jnp.float32), 'W_ioux': u(ks[2], (2 * D, D)), 'b_ioux': u(ks[3], (2 * D,)), 'W_iouh': u(ks[4], (2 * D, D)), 'b_iouh': u(ks[5], (2 * D,)), 'W_coux': u(ks[6], (D, D)), 'b_coux': u(ks[7], (D,)), 'W_couh': u(ks[8], (D, D)), 'b_couh': u(ks[9], (D,))}
    _L3_gnn_all = _L3_gnn_setup()
    _L3_gnn_in = {k: v for k, v in _L3_gnn_all.items() if k in ('W_ioux', 'b_ioux', 'W_iouh', 'b_iouh', 'W_coux', 'b_coux', 'W_couh', 'b_couh')}
    del _L3_gnn_all
    return {'x': x, 'adj': adj, 'nodemask': nodemask, 'L0_gnn_weight': _L0_gnn_in['weight'], 'L0_gnn_w_ih': _L0_gnn_in['w_ih'], 'L0_gnn_w_hh': _L0_gnn_in['w_hh'], 'L0_gnn_b_ih': _L0_gnn_in['b_ih'], 'L0_gnn_b_hh': _L0_gnn_in['b_hh'], 'L1_gnn_W1': _L1_gnn_in['W1'], 'L1_gnn_b1': _L1_gnn_in['b1'], 'L1_gnn_W2': _L1_gnn_in['W2'], 'L1_gnn_b2': _L1_gnn_in['b2'], 'L1_gnn_fusion_w': _L1_gnn_in['fusion_w'], 'L2_gnn_W': _L2_gnn_in['W'], 'L2_gnn_a': _L2_gnn_in['a'], 'L2_gnn_gamma': _L2_gnn_in['gamma'], 'L2_gnn_beta': _L2_gnn_in['beta'], 'L3_gnn_W_ioux': _L3_gnn_in['W_ioux'], 'L3_gnn_b_ioux': _L3_gnn_in['b_ioux'], 'L3_gnn_W_iouh': _L3_gnn_in['W_iouh'], 'L3_gnn_b_iouh': _L3_gnn_in['b_iouh'], 'L3_gnn_W_coux': _L3_gnn_in['W_coux'], 'L3_gnn_b_coux': _L3_gnn_in['b_coux'], 'L3_gnn_W_couh': _L3_gnn_in['W_couh'], 'L3_gnn_b_couh': _L3_gnn_in['b_couh']}

def reference(x, adj, nodemask, L0_gnn_weight, L0_gnn_w_ih, L0_gnn_w_hh, L0_gnn_b_ih, L0_gnn_b_hh, L1_gnn_W1, L1_gnn_b1, L1_gnn_W2, L1_gnn_b2, L1_gnn_fusion_w, L2_gnn_W, L2_gnn_a, L2_gnn_gamma, L2_gnn_beta, L3_gnn_W_ioux, L3_gnn_b_ioux, L3_gnn_W_iouh, L3_gnn_b_iouh, L3_gnn_W_coux, L3_gnn_b_coux, L3_gnn_W_couh, L3_gnn_b_couh):
    import jax
    import jax.numpy as jnp

    def _L0_gnn_ref(x, adj, mask, weight, w_ih, w_hh, b_ih, b_hh):
        import jax, jax.numpy as jnp
        import numpy as np
        B, N, D, C, L = (64, 256, 128, 128, 5)
        EDGE_P = 0.02

        def _gru_cell(m, h, w_ih, w_hh, b_ih, b_hh):
            gi = m @ w_ih.T + b_ih
            gh = h @ w_hh.T + b_hh
            i_r, i_z, i_n = jnp.split(gi, 3, axis=-1)
            h_r, h_z, h_n = jnp.split(gh, 3, axis=-1)
            r = jax.nn.sigmoid(i_r + h_r)
            z = jax.nn.sigmoid(i_z + h_z)
            n = jnp.tanh(i_n + r * h_n)
            return (1.0 - z) * n + z * h
        A = (adj != 0).astype(x.dtype)
        h = x
        for l in range(weight.shape[0]):
            m = jnp.einsum('bnd,de->bne', h, weight[l])
            agg = jnp.einsum('bij,bid->bjd', A, m)
            h = _gru_cell(agg, h, w_ih, w_hh, b_ih, b_hh)
        return h * mask[..., None]

    def _L1_gnn_ref(x, adj, W1, b1, W2, b2, fusion_w):
        import jax, jax.numpy as jnp
        import numpy as np
        GROUPS = [list(range(25)), [0, 1, 2, 3, 4, 5, 6, 7, 8], [0, 9, 10, 11, 12, 13, 14], [6, 7, 8, 12, 13, 14], [3, 4, 5, 9, 10, 11]]
        B, N, D_IN, D_HID = (4096, 25, 128, 256)

        def _graph_conv(x, adj, W, b):
            n = adj.shape[-1]
            A = adj + jnp.eye(n, dtype=adj.dtype)
            deg = jnp.sum(A, axis=-1)
            deg_safe = jnp.where(deg == 0, 1.0, deg)
            dinv = jnp.where(deg == 0, 0.0, deg_safe ** (-0.5))
            norm_adj = dinv[:, :, None] * A * dinv[:, None, :]
            support = jnp.einsum('bnd,de->bne', x, W)
            out = jnp.einsum('bnm,bme->bne', norm_adj, support) + b
            return jax.nn.relu(out)
        norm_w = jax.nn.softmax(fusion_w)
        fused = jnp.zeros_like(x)
        for g, idx_list in enumerate(GROUPS):
            idx = jnp.asarray(idx_list)
            x_g = x[:, idx, :]
            adj_g = adj[:, idx][:, :, idx]
            h = _graph_conv(x_g, adj_g, W1[g], b1[g])
            out_g = _graph_conv(h, adj_g, W2[g], b2[g])
            fused = fused.at[:, idx, :].add(norm_w[g] * out_g)
        return fused

    def _L2_gnn_ref(h, adj, W, a, gamma, beta):
        import jax, jax.numpy as jnp
        import numpy as np
        ALPHA = 0.2
        EPS = 1e-05
        NEG = -9000000000000000.0
        F_out = W.shape[1]
        Wh = jnp.matmul(h, W)
        a1 = a[:F_out, 0]
        a2 = a[F_out:, 0]
        s1 = jnp.einsum('bnf,f->bn', Wh, a1)
        s2 = jnp.einsum('bnf,f->bn', Wh, a2)
        e = s1[:, :, None] + s2[:, None, :]
        e = jnp.where(e > 0, e, ALPHA * e)
        e = jnp.where(adj > 0, e, NEG)
        attention = jax.nn.softmax(e, axis=2)
        h_prime = jnp.matmul(attention, Wh)
        mu = jnp.mean(h_prime, axis=-1, keepdims=True)
        var = jnp.mean(jnp.square(h_prime - mu), axis=-1, keepdims=True)
        hn = (h_prime - mu) / jnp.sqrt(var + EPS) * gamma + beta
        return jax.nn.gelu(hn, approximate=False)

    def _L3_gnn_ref(h_e, adj, W_ioux, b_ioux, W_iouh, b_iouh, W_coux, b_coux, W_couh, b_couh):
        import jax, jax.numpy as jnp
        import numpy as np
        B, N, D = (8, 256, 128)
        n = h_e.shape[1]
        d = jnp.sum(adj, axis=-1)
        dinv = jnp.where(d != 0, 1.0 / jnp.where(d != 0, d, 1.0), 0.0)
        norm_adjT = jnp.swapaxes(adj, 1, 2) * dinv[:, :, None]

        def step(h, i):
            x = jnp.take(h_e, i, axis=1)
            row = jnp.take(norm_adjT, i, axis=1)
            x_par = jnp.einsum('bj,bjd->bd', row, h)
            iou = x @ W_ioux.T + b_ioux + x_par @ W_iouh.T + b_iouh
            r, z = jnp.split(iou, 2, axis=1)
            r, z = (jax.nn.sigmoid(r), jax.nn.sigmoid(z))
            hc = jnp.tanh(x @ W_coux.T + b_coux + x_par * r @ W_couh.T + b_couh)
            h_new = z * x_par + (1.0 - z) * hc
            h = jax.lax.dynamic_update_slice(h, h_new[:, None, :], (0, i, 0))
            return (h, None)
        h_out, _ = jax.lax.scan(step, h_e, jnp.arange(n))
        return h_out
    x = _layernorm(x + _L0_gnn_ref(x, adj, nodemask, L0_gnn_weight, L0_gnn_w_ih, L0_gnn_w_hh, L0_gnn_b_ih, L0_gnn_b_hh), axis=-1)
    x = _layernorm(x + _L1_gnn_ref(x, adj, L1_gnn_W1, L1_gnn_b1, L1_gnn_W2, L1_gnn_b2, L1_gnn_fusion_w), axis=-1)
    x = _layernorm(x + _L2_gnn_ref(x, adj, L2_gnn_W, L2_gnn_a, L2_gnn_gamma, L2_gnn_beta), axis=-1)
    x = _layernorm(x + _L3_gnn_ref(x, adj, L3_gnn_W_ioux, L3_gnn_b_ioux, L3_gnn_W_iouh, L3_gnn_b_iouh, L3_gnn_W_coux, L3_gnn_b_coux, L3_gnn_W_couh, L3_gnn_b_couh), axis=-1)
    return x

_drawn_inputs = setup_inputs


def setup_inputs(seed=0):
    import zlib

    import numpy as np

    out = dict(_drawn_inputs(seed))
    spreads = {'L1_gnn_b1': (0.0, 0.8),
     'L1_gnn_b2': (0.0, 0.694),
     'L1_gnn_fusion_w': (1.0, 0.6),
     'L2_gnn_gamma': (1.0, 0.2),
     'L2_gnn_beta': (0.0, 0.1)}
    factors = {'L3_gnn_b_ioux': 7.923, 'L3_gnn_b_iouh': 6.954}
    for name, (base, spread) in spreads.items():
        noise = np.random.default_rng([zlib.crc32(name.encode()), seed]).standard_normal(out[name].shape)
        drawn = base * np.exp(spread * noise) if base else spread * noise
        out[name] = jnp.asarray(drawn.astype(out[name].dtype))
    for name, factor in factors.items():
        out[name] = (out[name] * factor).astype(out[name].dtype)
    return out
```

```python
from contextlib import ExitStack

import concourse.bass as bass
from concourse import mybir

F32 = mybir.dt.float32
BF16 = mybir.dt.bfloat16
ALU = mybir.AluOpType
ACT = mybir.ActivationFunctionType
AX_X = mybir.AxisListType.X

P = 128
B = 64
LAYERS = 5
TILE = 4
COLS = TILE * P
PAIRS = B // (2 * TILE)
S = 8
PARTS = (0, 64, 96)
EPS = 1e-5
ALPHA = 0.2
NEG = -9e15


GROUPS = (list(range(25)), list(range(9)), [0, *range(9, 15)], [6, 7, 8, 12, 13, 14], [3, 4, 5, 9, 10, 11])
JOINTS = 25
ROWS = [n for nodes in GROUPS for n in nodes]
Q = len(ROWS)
FIRST = [sum(len(nodes) for nodes in GROUPS[:g]) for g in range(len(GROUPS))]
HALVES = 2
T1 = 8


def runs(nodes):
    found, at = [], 0
    while at < len(nodes):
        k = 1
        while at + k < len(nodes) and nodes[at + k] == nodes[at] + k:
            k += 1
        found.append((at, nodes[at], k))
        at += k
    return found


def alone(eng, met):
    eng.wait_ge(met, 1)


def gated_convolution(nc, dram, X, adj, consts, norm_t, root_diag, groups_ready, node_degree, degrees_ready):
    with nc.cleanup_on_exit(), ExitStack() as ctx:
        def sb(name, shape):
            return ctx.enter_context(nc.sbuf_tensor(name, shape, F32))

        def sem(name):
            return nc.alloc_semaphore(name)

        w_msg = sb("w_msg", [P, LAYERS, P])
        w_ih = sb("w_ih", [P, 3, P])
        w_hh = sb("w_hh", [P, 3, P])
        b_ih = sb("b_ih", [P, 3])
        b_hh = sb("b_hh", [P, 3])
        b_rz = sb("b_rz", [P, 2])
        mask = sb("mask", [P, B])
        h_in = sb("h_in", [P, 2, COLS])
        h = sb("h", [P, 2, COLS])
        h_last = sb("h_last", [P, 2, COLS])
        edges = sb("edges", [P, 2, COLS])
        m_sb = sb("m_sb", [P, 2, COLS])
        agg_sb = sb("agg_sb", [P, 2, COLS])
        r = sb("r", [P, 2, COLS])
        z = sb("z", [P, 2, COLS])
        n_pre = sb("n_pre", [P, 2, COLS])
        n = sb("n", [P, 2, COLS])
        zh = sb("zh", [P, 2, COLS])
        stats = sb("stats", [P, TILE, 6])
        mv = sb("mv", [P, 2, TILE, 2])
        rstd = sb("rstd", [P, 2, TILE])
        adj_groups = sb("adj_groups", [Q, B, Q])
        eye_q = sb("eye_q", [Q, Q])
        degree = sb("degree", [Q, 2 * TILE])
        root = sb("root", [Q, 2 * TILE])
        ps = ctx.enter_context(nc.psum_tensor("ps0", [P, 8, COLS], F32))
        R, Z, HN, SHARED = (0, 1), (2, 3), (4, 5), (6, 7)

        weights_in = sem("weights_in")
        small_in = sem("small_in")
        h_loaded = [sem(f"h_loaded{s}") for s in range(2)]
        nodes_loaded = sem("nodes_loaded")
        adj_loaded = sem("adj_loaded")
        edges_ready = sem("edges_ready")
        m_done = sem("m_done")
        m_copied = sem("m_copied")
        agg_done = sem("agg_done")
        agg_copied = sem("agg_copied")
        r_done = sem("r_done")
        z_done = sem("z_done")
        n_done = sem("n_done")
        r_ready = sem("r_ready")
        z_ready = sem("z_ready")
        n_pre_ready = sem("n_pre_ready")
        n_ready = sem("n_ready")
        chain = sem("gru_chain")
        zh_ready = sem("zh_ready")
        h_ready = sem("h_ready")
        turned = sem("turned")
        summed = sem("summed")
        moments_ready = sem("moments_ready")
        var_eps = sem("var_eps")
        rstd_ready = sem("rstd_ready")
        normed = sem("normed")
        const_ready = sem("const_ready")

        groups_in = sem("groups_in")
        eye_added = sem("eye_added")
        degree_step = sem("degree_step")
        guarded = sem("guarded")
        powered = sem("powered")
        root_ready = sem("root_ready")
        rows_scaled = sem("rows_scaled")

        def graphs(it):
            return bass.ds(it * 2 * TILE, 2 * TILE)

        STEPS = 2 * LAYERS

        def pairs(eng, body):
            body(0)
            with eng.Fori(1, PAIRS) as it:
                body(it)

        block = ctx.enter_context(nc.Block())

        @block.sync
        def _(sp):
            def pair_in(it):
                for s in range(2):
                    if it is not 0:
                        sp.wait_ge(h_ready, (it - 1) * STEPS + s + 1)
                    sp.dma_start(h_in[:, s, :], dram["x_fm"][:, bass.ds((it * 2 + s) * COLS, COLS)]).then_inc(h_loaded[s], 16)
                    if s == 0:
                        sp.dma_start(adj[:, bass.ds(it * 2 * TILE, 2 * TILE), :],
                                     dram["adj_nm"][:, bass.ds(it * 2 * TILE, 2 * TILE), :]).then_inc(adj_loaded, 16)
                if it is 0:
                    sp.dma_start(norm_t[:], dram["adj_groups_t"]).then_inc(groups_in, 16)
                    sp.dma_start(adj_groups[:], dram["adj_groups"]).then_inc(groups_in, 16)
                    sp.dma_start(eye_q[:], dram["identity"][0:Q, 0:Q]).then_inc(groups_in, 16)
                sp.dma_start(X[:, bass.ds(it * 2 * TILE, 2 * TILE), :],
                             dram["x_nm"][:, bass.ds(it * 2 * TILE, 2 * TILE), :]).then_inc(nodes_loaded, 16)

            sp.dma_start(w_msg[:], dram["L0_weight"]).then_inc(weights_in, 16)
            pairs(sp, pair_in)

        @block.scalar
        def _(act):
            act.dma_start(w_hh[:], dram["L0_w_hh"]).then_inc(weights_in, 16)
            act.dma_start(w_ih[:], dram["L0_w_ih"]).then_inc(weights_in, 16)
            act.dma_start(b_ih[:], dram["L0_b_ih"]).then_inc(small_in, 16)
            act.dma_start(b_hh[:], dram["L0_b_hh"]).then_inc(small_in, 16)
            act.dma_start(mask[:], dram["mask"]).then_inc(small_in, 16)
            act.dma_start(consts["identity"][:], dram["identity"]).then_inc(consts["identity_in"], 16)
            act.wait_ge(const_ready, 2)

            def pair(it):
                for u in range(STEPS):
                    s, turn = u % 2, it * STEPS + u
                    act.wait_ge(m_done, turn + 1)
                    nc.scalar.copy(m_sb[:, s, :], ps[:, SHARED[s], :]).then_inc(m_copied, 1)
                    act.wait_ge(r_done, turn + 1)
                    nc.scalar.activation(r[:, s, :], ps[:, R[s], :], ACT.Sigmoid, bias=b_rz[:, 0:1]).then_inc(r_ready, 1)
                    act.wait_ge(z_done, turn + 1)
                    nc.scalar.activation(z[:, s, :], ps[:, Z[s], :], ACT.Sigmoid, bias=b_rz[:, 1:2]).then_inc(z_ready, 1)
                    act.wait_ge(n_pre_ready, turn + 1)
                    nc.scalar.activation(n[:, s, :], n_pre[:, s, :], ACT.Tanh, bias=b_ih[:, 2:3]).then_inc(n_ready, 1)

            pairs(act, pair)

        @block.gpsimd
        def _(pool):
            nc.gpsimd.memset(consts["minus_half"][:], -0.5)
            nc.gpsimd.memset(consts["eps"][:], EPS).then_inc(const_ready, 1)

            def reciprocal_root(it, s):
                pool.wait_ge(moments_ready, it * 2 + s + 1)
                nc.gpsimd.tensor_tensor(mv[:, s, :, 1], mv[:, s, :, 1], consts["eps"][:, 0:TILE],
                                        ALU.add).then_inc(var_eps, 1)
                pool.wait_ge(var_eps, it * 2 + s + 1)
                nc.gpsimd.tensor_tensor(rstd[:, s, :], mv[:, s, :, 1], consts["minus_half"][:, 0:TILE],
                                        ALU.pow).then_inc(rstd_ready, 1)

            pool.wait_ge(const_ready, 1)

            def pair(it):
                for u in range(STEPS):
                    s, turn = u % 2, it * STEPS + u
                    if u < 2:
                        pool.wait_ge(h_loaded[s], (it + 1) * 16)
                    pool.wait_ge(z_ready, turn + 1)
                    src = h_in if u < 2 else h
                    nc.gpsimd.tensor_tensor(zh[:, s, :], z[:, s, :], src[:, s, :], ALU.mult).then_inc(zh_ready, 1)
                    if u == 3:
                        pool.wait_ge(groups_in, 48)
                        nc.gpsimd.tensor_tensor(norm_t[:, graphs(it), :], norm_t[:, graphs(it), :],
                                                eye_q[:].unsqueeze(1).broadcast_to([Q, 2 * TILE, Q]),
                                                ALU.add).then_inc(eye_added, 1)
                    if u == 5:
                        pool.wait_ge(guarded, it + 1)
                        nc.gpsimd.tensor_tensor(root[:], root[:], consts["minus_half"][0:Q, 0:2 * TILE],
                                                ALU.pow).then_inc(powered, 1)
                    if u == 7:
                        alone(pool, consts["identity_in"])
                        pool.wait_ge(eye_added, it + 1)
                        pool.wait_ge(root_ready, it + 1)
                        nc.gpsimd.tensor_tensor(norm_t[:, graphs(it), :], norm_t[:, graphs(it), :],
                                                root[:].unsqueeze(2).broadcast_to([Q, 2 * TILE, Q]),
                                                ALU.mult).then_inc(rows_scaled, 1)
                    if u == 8:
                        nc.gpsimd.tensor_tensor(root_diag[:, graphs(it), :],
                                                eye_q[:].unsqueeze(1).broadcast_to([Q, 2 * TILE, Q]),
                                                root[:].unsqueeze(2).broadcast_to([Q, 2 * TILE, Q]),
                                                ALU.mult).then_inc(groups_ready, 1)
                    if u == 1 and it is not 0:
                        reciprocal_root(it - 1, 0)
                    if u == 2 and it is not 0:
                        reciprocal_root(it - 1, 1)

            pairs(pool, pair)
            reciprocal_root(PAIRS - 1, 0)
            reciprocal_root(PAIRS - 1, 1)

        @block.vector
        def _(dve):
            dve.wait_ge(small_in, 48)
            nc.vector.tensor_tensor(b_rz[:], b_ih[:, 0:2], b_hh[:, 0:2], ALU.add).then_inc(const_ready, 1)

            def residual(it, s):
                dve.wait_ge(nodes_loaded, (it + 1) * 16)
                dve.wait_ge(turned, it * 2 + s + 1)
                for g in range(TILE):
                    b = it * 2 * TILE + s * TILE + g
                    one = nc.vector.scalar_tensor_tensor(
                        out=X[:, bass.ds(b, 1), :], in0=ps[:, HN[s], g * P:(g + 1) * P].unsqueeze(1), scalar=mask[:, bass.ds(b, 1)],
                        in1=X[:, bass.ds(b, 1), :], op0=ALU.mult, op1=ALU.add)
                one.then_inc(summed, 1)
                alone(dve, consts["identity_in"])
                dve.wait_ge(summed, it * 2 + s + 1)
                for g in range(TILE):
                    b = it * 2 * TILE + s * TILE + g
                    one = nc.vector.bn_stats(stats[:, g, :], X[:, bass.ds(b, 1), :])
                one.then_inc(chain, 1)
                alone(dve, consts["identity_in"])
                dve.wait_ge(chain, it * 2 + s + 1)
                for g in range(TILE):
                    one = nc.vector.bn_aggr(mv[:, s, g, :], stats[:, g, :])
                one.then_inc(moments_ready, 1)

            def normalise(it, s):
                dve.wait_ge(rstd_ready, it * 2 + s + 1)
                for g in range(TILE):
                    b = it * 2 * TILE + s * TILE + g
                    one = nc.vector.tensor_scalar(X[:, bass.ds(b, 1), :], X[:, bass.ds(b, 1), :], mv[:, s, g, 0:1],
                                                  rstd[:, s, g:g + 1], ALU.subtract, ALU.mult)
                one.then_inc(normed, 1)

            def pair(it):
                dve.wait_ge(adj_loaded, (it + 1) * 16)
                for u in range(STEPS):
                    s, turn = u % 2, it * STEPS + u
                    if u < 2:
                        if it is not 0:
                            dve.wait_ge(agg_done, it * STEPS - 1 + s)
                        nc.vector.tensor_scalar(edges[:, s, :].rearrange("p (b n) -> p b n", b=TILE),
                                                adj[:, bass.ds(it * 2 * TILE + s * TILE, TILE), :],
                                                0.0, None, ALU.not_equal).then_inc(edges_ready, 1)
                    if u < 2 and it is not 0:
                        residual(it - 1, s)
                    dve.wait_ge(agg_done, turn + 1)
                    nc.vector.tensor_copy(agg_sb[:, s, :], ps[:, SHARED[1 - s], :]).then_inc(agg_copied, 1)
                    dve.wait_ge(r_ready, turn + 1)
                    nc.vector.scalar_tensor_tensor(out=n_pre[:, s, :], in0=ps[:, HN[s], :], scalar=b_hh[:, 2:3],
                                                   in1=r[:, s, :], op0=ALU.add, op1=ALU.mult).then_inc(r_used, 1)
                    dve.wait_ge(r_used, turn + 1)
                    dve.wait_ge(n_done, turn + 1)
                    nc.vector.tensor_tensor(n_pre[:, s, :], n_pre[:, s, :], ps[:, SHARED[s], :],
                                            ALU.add).then_inc(n_pre_ready, 1)
                    dve.wait_ge(z_ready, turn + 1)
                    nc.vector.tensor_scalar(z1[:, s, :], z[:, s, :], -1.0, 1.0, ALU.mult, ALU.add).then_inc(z1_ready, 1)
                    dve.wait_ge(z1_ready, turn + 1)
                    dve.wait_ge(n_ready, turn + 1)
                    nc.vector.tensor_tensor(n[:, s, :], n[:, s, :], z1[:, s, :], ALU.mult).then_inc(n_scaled, 1)
                    dve.wait_ge(n_scaled, turn + 1)
                    dve.wait_ge(zh_ready, turn + 1)
                    dst = h_last if u >= STEPS - 2 else h
                    nc.vector.tensor_tensor(dst[:, s, :], n[:, s, :], zh[:, s, :], ALU.add).then_inc(h_ready, 1)
                    if u in (2, 3) and it is not 0:
                        normalise(it - 1, u % 2)
                    if u == 3:
                        dve.wait_ge(groups_in, 48)
                        if it is not 0:
                            dve.wait_ge(groups_ready, it)
                        nc.vector.tensor_reduce(degree[:], adj_groups[:, graphs(it), :], AX_X,
                                                ALU.add).then_inc(degree_step, 1)
                        dve.wait_ge(degree_step, 2 * it + 1)
                        nc.vector.tensor_scalar(degree[:], degree[:], 1.0, None, ALU.add).then_inc(degree_step, 1)
                        dve.wait_ge(degree_step, 2 * it + 2)
                        nc.vector.scalar_tensor_tensor(out=root[:], in0=degree[:], scalar=0.0, in1=degree[:],
                                                       op0=ALU.is_equal, op1=ALU.add).then_inc(guarded, 1)
                    if u == 4:
                        nc.vector.tensor_reduce(node_degree[:, graphs(it)], adj[:, graphs(it), :], AX_X,
                                                ALU.add).then_inc(degrees_ready, 1)
                    if u == 6:
                        dve.wait_ge(powered, it + 1)
                        nc.vector.scalar_tensor_tensor(out=root[:], in0=degree[:], scalar=0.0, in1=root[:],
                                                       op0=ALU.is_equal, op1=ALU.subtract).then_inc(root_ready, 1)

            z1 = sb("z1", [P, 2, COLS])
            r_used, z1_ready, n_scaled = sem("r_used"), sem("z1_ready"), sem("n_scaled")
            pairs(dve, pair)
            for s in range(2):
                residual(PAIRS - 1, s)
            for s in range(2):
                normalise(PAIRS - 1, s)

        @block.tensor
        def _(pe):
            pe.wait_ge(weights_in, 48)
            pe.wait_ge(consts["identity_in"], 16)

            def turn_back(it, s):
                pe.wait_ge(h_ready, it * STEPS + STEPS - 1 + s)
                for g in range(TILE):
                    one = nc.tensor.transpose(ps[:, HN[s], g * P:(g + 1) * P], h_last[:, s, g * P:(g + 1) * P],
                                              consts["identity"][:])
                one.then_inc(turned, 1)

            def pair(it):
                for u in range(STEPS):
                    s, layer, turn = u % 2, u // 2, it * STEPS + u
                    state = h_in if u < 2 else h
                    if u < 2:
                        pe.wait_ge(h_loaded[s], (it + 1) * 16)
                        if it is not 0:
                            pe.wait_ge(h_ready, turn - 1)
                    else:
                        pe.wait_ge(h_ready, turn - 1)
                    for g in range(TILE):
                        one = nc.tensor.matmul(ps[:, SHARED[s], g * P:(g + 1) * P], state[:, s, g * P:(g + 1) * P],
                                               w_msg[:, layer, :], start=True, stop=True)
                    one.then_inc(m_done, 1)
                    for bank, k in ((R, 0), (Z, 1)):
                        nc.tensor.matmul(ps[:, bank[s], :], w_hh[:, k, :], state[:, s, :], start=True, stop=False)
                    pe.wait_ge(m_copied, turn + 1)
                    if u < 2:
                        pe.wait_ge(edges_ready, it * 2 + s + 1)
                    for g in range(TILE):
                        one = nc.tensor.matmul(ps[:, SHARED[1 - s], g * P:(g + 1) * P], m_sb[:, s, g * P:(g + 1) * P],
                                               edges[:, s, g * P:(g + 1) * P], start=True, stop=True)
                    one.then_inc(agg_done, 1)
                    if u < 2 and it is not 0:
                        pe.wait_ge(summed, (it - 1) * 2 + s + 1)
                    nc.tensor.matmul(ps[:, HN[s], :], w_hh[:, 2, :], state[:, s, :], start=True, stop=True)
                    pe.wait_ge(agg_copied, turn + 1)
                    for bank, k, done in ((R, 0, r_done), (Z, 1, z_done)):
                        nc.tensor.matmul(ps[:, bank[s], :], w_ih[:, k, :], agg_sb[:, s, :], start=False,
                                         stop=True).then_inc(done, 1)
                    nc.tensor.matmul(ps[:, SHARED[s], :], w_ih[:, 2, :], agg_sb[:, s, :], start=True,
                                     stop=True).then_inc(n_done, 1)
                    if u == 0 and it is not 0:
                        turn_back(it - 1, 1)
                turn_back(it, 0)

            pairs(pe, pair)
            turn_back(PAIRS - 1, 1)


def group_convolution(nc, dram, X, consts, norm_t, root_diag, groups_ready, node_degree, inverse_t, inverse_stored):
    with ExitStack() as ctx:
        def sb(name, shape):
            return ctx.enter_context(nc.sbuf_tensor(name, shape, F32))

        def sem(name):
            return ctx.enter_context(nc.semaphore(name))

        G, SLOTS = len(GROUPS), 4
        ROUNDS = B // T1 // SLOTS
        mix = sb("mix", [JOINTS, B, Q])
        ones_q = sb("ones_q", [Q, Q])
        to_joint = sb("to_joint", [Q, JOINTS])
        w1 = sb("w1", [P, G, HALVES, P])
        w2 = sb("w2", [P, G, HALVES, P])
        b1 = sb("b1", [P, G, HALVES])
        b2 = sb("b2", [P, G])
        fusion = sb("fusion", [P, G])
        weight = sb("weight", [P, G])
        b2w = sb("b2w", [P, G])
        top = sb("top", [P, 1])
        total = sb("total", [P, 1])
        spare = sb("spare", [P, 1])
        x_in = sb("x_in", [JOINTS, SLOTS, T1, P])
        u_sb = sb("u_sb", [P, SLOTS, T1, Q])
        hid = sb("hid", [P, SLOTS, HALVES, T1, Q])
        sup = sb("sup", [P, SLOTS, T1, Q])
        sup_nm = sb("sup_nm", [Q, SLOTS, T1 * P])
        out_w = sb("out_w", [P, SLOTS, T1, Q])
        stats = sb("stats1", [P, SLOTS, T1, 6])
        mv = sb("mv1", [P, SLOTS, T1, 2])
        rstd = sb("rstd1", [P, SLOTS, T1])
        ps = ctx.enter_context(nc.psum_tensor("ps1", [P, 8, 512], F32))
        identity = consts["identity"]

        small_in = sem("small1_in")
        w_in = sem("w12_in")
        ones_set = sem("ones_set")
        root_done = sem("root_done")
        norm_ready = sem("norm_ready")
        mix_done = sem("mix_done")
        mix_ready = sem("mix_ready")
        mix_ready_act = sem("mix_ready_act")
        fuse_step = sem("fuse_step")
        fuse_exp = sem("fuse_exp")
        fuse_ready = sem("fuse_ready")
        x_ready = [sem(f"x_ready{s}") for s in range(SLOTS)]
        u_done = sem("u_done")
        u_ready = sem("u_ready")
        hid_done = sem("hid_done")
        hid0_ready = sem("hid0_ready")
        hid1_ready = sem("hid1_ready")
        sup_done = sem("sup_done")
        sup_ready = sem("sup_ready")
        sup_turned = sem("sup_turned")
        sup_nm0_ready = sem("sup_nm0_ready")
        sup_nm1_ready = sem("sup_nm1_ready")
        out_done = sem("out_done")
        out_ready = sem("out_ready")
        fused_step = sem("fused_step")
        fused_ready = sem("fused_ready")
        fused_turned = sem("fused_turned")
        summed = sem("summed1")
        stats_ready = sem("stats1_ready")
        moments_ready = sem("moments1_ready")
        var_eps = sem("var_eps1")
        rstd_ready = sem("rstd1_ready")
        normed = sem("normed1")

        inverse_step = sem("inverse_step")
        inverse_turned = sem("inverse_turned")
        guard = sb("guard", [P, B])
        turned = sb("inverse_turned_sb", [B, P])

        def bank(k):
            return ps[:, k, 0:T1 * Q].rearrange("p (b q) -> p b q", b=T1)

        def group(ap, g):
            return ap[:, :, FIRST[g]:FIRST[g] + len(GROUPS[g])]

        PLACES = [(FIRST[g] + at, node, k) for g in range(1, G) for at, node, k in runs(GROUPS[g])]

        def first(it, s):
            return it * SLOTS * T1 + s * T1

        block = ctx.enter_context(nc.Block())

        @block.sync
        def _(sp):
            sp.dma_start(w1[:], dram["L1_W1"]).then_inc(w_in, 16)
            sp.dma_start(w2[:], dram["L1_W2"]).then_inc(w_in, 16)
            sp.wait_ge(inverse_step, 5)
            sp.dma_start(inverse_t, turned[:]).then_inc(inverse_stored, 16)
            with sp.Fori(0, ROUNDS) as it:
                for s in range(SLOTS):
                    sp.wait_ge(u_done, it * SLOTS + s + 1)
                    sp.dma_start(x_in[:, s], X[0:JOINTS, bass.ds(first(it, s), T1), :]).then_inc(x_ready[s], 16)
            sp.wait_ge(inverse_stored, 16)

        @block.scalar
        def _(act):
            act.dma_start(to_joint[:], dram["to_joint"]).then_inc(small_in, 16)
            act.dma_start(b1[:], dram["L1_b1"]).then_inc(small_in, 16)
            act.dma_start(b2[:], dram["L1_b2"]).then_inc(small_in, 16)
            act.dma_start(fusion[:], dram["L1_fusion_w"]).then_inc(small_in, 16)
            act.wait_ge(fuse_step, 2)
            nc.scalar.activation(weight[:], fusion[:], ACT.Exp, accum_out=total[:]).then_inc(fuse_exp, 1)
            for k in range(1, 8, 2):
                act.wait_ge(mix_done, k + 1)
                nc.scalar.copy(mix[:, k * T1:(k + 1) * T1, :], bank(k)[0:JOINTS]).then_inc(mix_ready_act, 1)
            act.wait_ge(fuse_ready, 1)
            with act.Fori(0, ROUNDS) as it:
                for s in range(SLOTS):
                    act.wait_ge(u_done, it * SLOTS + s + 1 + SLOTS)
                    nc.scalar.copy(u_sb[:, s], bank(2 * s)).then_inc(u_ready, 1)
                for s in range(SLOTS):
                    act.wait_ge(hid_done, it * SLOTS + s + 1)
                    for g in range(G):
                        one = nc.scalar.activation(group(hid[:, s, 0], g), group(bank(2 * s), g), ACT.Relu,
                                                   bias=b1[:, g, 0:1])
                    one.then_inc(hid0_ready, 1)
                for s in range(SLOTS):
                    act.wait_ge(sup_done, it * SLOTS + s + 1)
                    nc.scalar.copy(sup[:, s], bank(2 * s)).then_inc(sup_ready, 1)
                for s in range(SLOTS):
                    act.wait_ge(sup_turned, it * SLOTS + s + 1)
                    nc.scalar.copy(sup_nm[:, s, 0:512], ps[0:Q, 2 * s, :]).then_inc(sup_nm0_ready, 1)
                for s in range(SLOTS):
                    act.wait_ge(out_done, it * SLOTS + s + 1)
                    for g in range(G):
                        one = nc.scalar.activation(group(out_w[:, s], g), group(bank(2 * s), g), ACT.Relu,
                                                   bias=b2w[:, g:g + 1], scale=weight[:, g:g + 1])
                    one.then_inc(out_ready, 1)

        @block.gpsimd
        def _(pool):
            nc.gpsimd.memset(ones_q[:], 1.0).then_inc(ones_set, 1)
            with pool.Fori(0, ROUNDS) as it:
                for s in range(SLOTS):
                    pool.wait_ge(out_ready, it * SLOTS + s + 1)
                    for n, (q, node, k) in enumerate(PLACES):
                        if n:
                            pool.wait_ge(fused_step, (it * SLOTS + s) * (len(PLACES) - 1) + n)
                        part = out_w[:, s, :, node:node + k]
                        one = nc.gpsimd.tensor_tensor(part, part, out_w[:, s, :, q:q + k], ALU.add)
                        one.then_inc(fused_step if n + 1 < len(PLACES) else fused_ready, 1)
                for s in range(SLOTS):
                    pool.wait_ge(moments_ready, it * SLOTS + s + 1)
                    nc.gpsimd.tensor_tensor(mv[:, s, :, 1], mv[:, s, :, 1], consts["eps"][:, 0:T1],
                                            ALU.add).then_inc(var_eps, 1)
                    pool.wait_ge(var_eps, it * SLOTS + s + 1)
                    nc.gpsimd.tensor_tensor(rstd[:, s, :], mv[:, s, :, 1], consts["minus_half"][:, 0:T1],
                                            ALU.pow).then_inc(rstd_ready, 1)

        @block.vector
        def _(dve):
            dve.sem_inc(summed, SLOTS)
            nc.vector.tensor_scalar(guard[:], node_degree[:], 0.0, None, ALU.not_equal).then_inc(inverse_step, 1)
            nc.vector.scalar_tensor_tensor(out=node_degree[:], in0=node_degree[:], scalar=0.0, in1=node_degree[:],
                                           op0=ALU.is_equal, op1=ALU.add).then_inc(inverse_step, 1)
            dve.wait_ge(inverse_step, 2)
            nc.vector.reciprocal(node_degree[:], node_degree[:]).then_inc(inverse_step, 1)
            dve.wait_ge(inverse_step, 3)
            nc.vector.tensor_tensor(node_degree[:], node_degree[:], guard[:], ALU.mult).then_inc(inverse_step, 1)
            dve.wait_ge(inverse_turned, 1)
            nc.vector.tensor_copy(turned[:], ps[0:B, 7, 0:P]).then_inc(inverse_step, 1)
            dve.wait_ge(small_in, 64)
            nc.vector.tensor_reduce(top[:], fusion[:], AX_X, ALU.max).then_inc(fuse_step, 1)
            dve.wait_ge(fuse_step, 1)
            nc.vector.tensor_scalar(fusion[:], fusion[:], top[:, 0:1], None, ALU.subtract).then_inc(fuse_step, 1)
            for k in range(8):
                dve.wait_ge(root_done, k + 1)
                part = norm_t[:, k * T1:(k + 1) * T1, :]
                nc.vector.tensor_tensor(part, part, bank(k)[0:Q], ALU.mult).then_inc(norm_ready, 1)
            dve.wait_ge(fuse_exp, 1)
            nc.vector.reciprocal(total[:], total[:]).then_inc(fuse_step, 1)
            dve.wait_ge(fuse_step, 3)
            nc.vector.tensor_scalar(weight[:], weight[:], total[:, 0:1], None, ALU.mult).then_inc(fuse_step, 1)
            dve.wait_ge(fuse_step, 4)
            nc.vector.tensor_tensor(b2w[:], b2[:], weight[:], ALU.mult).then_inc(fuse_ready, 1)
            for k in range(0, 8, 2):
                dve.wait_ge(mix_done, k + 1)
                nc.vector.tensor_copy(mix[:, k * T1:(k + 1) * T1, :], bank(k)[0:JOINTS]).then_inc(mix_ready, 1)

            with dve.Fori(0, ROUNDS) as it:
                for s in range(SLOTS):
                    dve.wait_ge(hid_done, it * SLOTS + s + 1)
                    for g in range(G):
                        one = nc.vector.tensor_scalar(group(hid[:, s, 1], g), group(bank(2 * s + 1), g),
                                                      b1[:, g, 1:2], 0.0, ALU.add, ALU.max)
                    one.then_inc(hid1_ready, 1)
                for s in range(SLOTS):
                    dve.wait_ge(sup_turned, it * SLOTS + s + 1)
                    nc.vector.tensor_copy(sup_nm[:, s, 512:1024], ps[0:Q, 2 * s + 1, :]).then_inc(sup_nm1_ready, 1)
                for s in range(SLOTS):
                    dve.wait_ge(fused_turned, it * SLOTS + s + 1)
                    for k in range(2):
                        part = X[0:JOINTS, bass.ds(first(it, s) + 4 * k, 4), :]
                        one = nc.vector.tensor_tensor(part, part, ps[0:JOINTS, 2 * s + k, :].rearrange(
                            "p (b d) -> p b d", b=4), ALU.add)
                    one.then_inc(summed, 1)
                    dve.wait_ge(summed, it * SLOTS + s + 1 + SLOTS)
                    nc.vector.memset(spare[:], 0.0)
                    for b in range(T1):
                        one = nc.vector.bn_stats(stats[:, s, b, :], X[:, bass.ds(first(it, s) + b, 1), :])
                    one.then_inc(stats_ready, 1)
                    alone(dve, consts["identity_in"])
                    dve.wait_ge(stats_ready, it * SLOTS + s + 1)
                    for b in range(T1):
                        one = nc.vector.bn_aggr(mv[:, s, b, :], stats[:, s, b, :])
                    one.then_inc(moments_ready, 1)
                for s in range(SLOTS):
                    dve.wait_ge(rstd_ready, it * SLOTS + s + 1)
                    for b in range(T1):
                        part = X[:, bass.ds(first(it, s) + b, 1), :]
                        one = nc.vector.tensor_scalar(part, part, mv[:, s, b, 0:1], rstd[:, s, b:b + 1],
                                                      ALU.subtract, ALU.mult)
                    one.then_inc(normed, 1)

        @block.tensor
        def _(pe):
            pe.sem_inc(u_done, SLOTS)
            pe.wait_ge(inverse_step, 4)
            nc.tensor.transpose(ps[0:B, 7, 0:P], node_degree[:], identity[:]).then_inc(inverse_turned, 1)
            pe.wait_ge(ones_set, 1)
            pe.wait_ge(groups_ready, B // T1)
            for k in range(8):
                if k == 7:
                    pe.wait_ge(inverse_step, 5)
                nc.tensor.matmul(bank(k)[0:Q], ones_q[:], root_diag[:, k * T1:(k + 1) * T1, :], start=True,
                                 stop=True).then_inc(root_done, 1)
            pe.wait_ge(small_in, 64)
            for k in range(8):
                pe.wait_ge(norm_ready, k + 1)
                nc.tensor.matmul(bank(k)[0:JOINTS], to_joint[:], norm_t[:, k * T1:(k + 1) * T1, :], start=True,
                                 stop=True).then_inc(mix_done, 1)
            pe.wait_ge(mix_ready, 4)
            pe.wait_ge(mix_ready_act, 4)
            pe.wait_ge(w_in, 32)
            with pe.Fori(0, ROUNDS) as it:
                for s in range(SLOTS):
                    pe.wait_ge(x_ready[s], it * 16 + 16)
                    pe.wait_ge(summed, it * SLOTS + s + 1)
                    for b in range(T1):
                        one = nc.tensor.matmul(bank(2 * s)[:, b, :], x_in[:, s, b, :],
                                               mix[:, bass.ds(first(it, s) + b, 1), :].squeeze(1), start=True, stop=True)
                    one.then_inc(u_done, 1)
                for s in range(SLOTS):
                    pe.wait_ge(u_ready, it * SLOTS + s + 1)
                    for half in range(HALVES):
                        for g in range(G):
                            one = nc.tensor.matmul(group(bank(2 * s + half), g), w1[:, g, half, :],
                                                   group(u_sb[:, s], g), start=True, stop=True)
                    one.then_inc(hid_done, 1)
                for s in range(SLOTS):
                    pe.wait_ge(hid0_ready, it * SLOTS + s + 1)
                    pe.wait_ge(hid1_ready, it * SLOTS + s + 1)
                    for g in range(G):
                        for half in range(HALVES):
                            one = nc.tensor.matmul(group(bank(2 * s), g), w2[:, g, half, :],
                                                   group(hid[:, s, half], g), start=half == 0, stop=half == 1)
                    one.then_inc(sup_done, 1)
                for s in range(SLOTS):
                    alone(pe, consts["identity_in"])
                    pe.wait_ge(sup_ready, it * SLOTS + s + 1)
                    for b in range(T1):
                        one = nc.tensor.transpose(ps[0:Q, 2 * s + b // 4, (b % 4) * P:(b % 4 + 1) * P],
                                                  sup[:, s, b, :], identity[:])
                    one.then_inc(sup_turned, 1)
                for s in range(SLOTS):
                    pe.wait_ge(sup_nm0_ready, it * SLOTS + s + 1)
                    pe.wait_ge(sup_nm1_ready, it * SLOTS + s + 1)
                    for b in range(T1):
                        one = nc.tensor.matmul(bank(2 * s)[:, b, :], sup_nm[:, s, b * P:(b + 1) * P],
                                               norm_t[:, bass.ds(first(it, s) + b, 1), :].squeeze(1), start=True, stop=True)
                    one.then_inc(out_done, 1)
                for s in range(SLOTS):
                    alone(pe, consts["identity_in"])
                    pe.wait_ge(fused_ready, it * SLOTS + s + 1)
                    for b in range(T1):
                        one = nc.tensor.transpose(ps[0:JOINTS, 2 * s + b // 4, (b % 4) * P:(b % 4 + 1) * P],
                                                  out_w[:, s, b, 0:JOINTS], identity[:])
                    one.then_inc(fused_turned, 1)


def graph_attention(nc, dram, X, adj, hn, consts):
    with ExitStack() as ctx:
        def sb(name, shape):
            return ctx.enter_context(nc.sbuf_tensor(name, shape, F32))

        def sem(name):
            return ctx.enter_context(nc.semaphore(name))

        SLOTS = 4
        ROUNDS = B // TILE // SLOTS
        w = sb("w_att", [P, P])
        w_t = sb("w_att_t", [P, P])
        a1 = sb("a1", [P, P])
        a2 = sb("a2", [P, P])
        wa1 = sb("wa1", [P, P])
        wa2 = sb("wa2", [P, P])
        gamma = sb("gamma", [P, P])
        beta = sb("beta", [P, P])
        x_in = sb("x2_in", [P, SLOTS, COLS])
        bars = sb("bars", [P, SLOTS, COLS])
        xt = sb("xt", [P, SLOTS, COLS])
        wh = sb("wh", [P, SLOTS, COLS])
        score = sb("score", [P, SLOTS, COLS])
        att = sb("att", [P, SLOTS, COLS])
        att_t = xt
        top = sb("top2", [P, SLOTS, TILE])
        total = sb("total2", [P, SLOTS, TILE])
        scale = sb("scale2", [P, SLOTS, TILE])
        stats = sb("stats2", [P, SLOTS, TILE, 6])
        mv = sb("mv2", [P, SLOTS, TILE, 2])
        ps = ctx.enter_context(nc.psum_tensor("ps2", [P, 8, COLS], F32))
        identity = consts["identity"]

        w_in = sem("w_att_in")
        wa_done = sem("wa_done")
        wa_ready = sem("wa_ready")
        x_loaded = [sem(f"x2_loaded{s}") for s in range(SLOTS)]
        x_turned = sem("x2_turned")
        xt_ready = sem("xt_ready")
        wh_done = sem("wh_done")
        wh_ready = sem("wh_ready")
        score_done = sem("score_done")
        score_copied = sem("score_copied")
        barred = sem("barred")
        leaked = sem("leaked")
        masked = sem("masked")
        top_found = sem("top_found")
        top_ready = sem("top_ready")
        exp_ready = sem("exp_ready")
        att_turned = sem("att_turned")
        att_t_ready = sem("att_t_ready")
        head_done = sem("head_done")
        head_ready = sem("head_ready")
        stats_ready = sem("stats2_ready")
        moments_ready = sem("moments2_ready")
        total_inverted = sem("total_inverted")
        scale_step = sem("scale_step")
        scale_ready = sem("scale_ready")
        head_normed = sem("head_normed")
        gained = sem("gained")
        hn_ready = sem("hn_ready")

        def graph(ap, s, g):
            return ap[:, s, g * P:(g + 1) * P]

        def graphs(ap):
            return ap.rearrange("p (b d) -> p b d", b=TILE)

        block = ctx.enter_context(nc.Block())

        @block.sync
        def _(sp):
            with sp.Fori(0, ROUNDS) as it:
                for s in range(SLOTS):
                    tile = bass.ds((it * SLOTS + s) * TILE, TILE)
                    sp.wait_ge(x_turned, it * SLOTS + s + 1)
                    sp.dma_start(graphs(x_in[:, s]), X[:, tile, :]).then_inc(x_loaded[s], 16)

        @block.scalar
        def _(act):
            for k, dst in enumerate((w, w_t, a1, a2, gamma, beta)):
                act.dma_start(dst[:], dram[("L2_W", "L2_W_t", "L2_a1", "L2_a2", "L2_gamma", "L2_beta")[k]]).then_inc(w_in, 16)
            act.wait_ge(wa_done, 1)
            nc.scalar.copy(wa1[:], ps[:, 0, 0:P])
            nc.scalar.copy(wa2[:], ps[:, 0, P:2 * P]).then_inc(wa_ready, 1)
            with act.Fori(0, ROUNDS) as it:
                def turn(s):
                    return it * SLOTS + s + 1
                for s in range(SLOTS):
                    act.wait_ge(x_turned, it * SLOTS + s + 1 + SLOTS)
                    nc.scalar.copy(xt[:, s], ps[:, 2 * s, :]).then_inc(xt_ready, 1)
                for s in range(SLOTS):
                    act.wait_ge(score_done, turn(s))
                    nc.scalar.copy(score[:, s], ps[:, 2 * s, :]).then_inc(score_copied, 1)
                for s in range(SLOTS):
                    act.wait_ge(top_ready, turn(s))
                    act.wait_ge(hn_ready, turn(s))
                    for g in range(TILE):
                        one = nc.scalar.activation(graph(att, s, g), graph(score, s, g), ACT.Exp,
                                                   bias=top[:, s, g:g + 1], accum_out=total[:, s, g:g + 1])
                    one.then_inc(exp_ready, 1)
                for s in range(SLOTS):
                    act.wait_ge(att_turned, turn(s))
                    nc.scalar.copy(att_t[:, s], ps[:, 2 * s, :]).then_inc(att_t_ready, 1)
                for s in range(SLOTS):
                    act.wait_ge(head_done, turn(s))
                    nc.scalar.copy(att[:, s], ps[:, 2 * s + 1, :]).then_inc(head_ready, 1)

        @block.gpsimd
        def _(pool):
            pool.sem_inc(hn_ready, SLOTS)
            with pool.Fori(0, ROUNDS) as it:
                def turn(s):
                    return it * SLOTS + s + 1
                for s in range(SLOTS):
                    pool.wait_ge(total_inverted, turn(s))
                    steps = ((scale, total, total, ALU.mult), (scale, scale, None, ALU.mult),
                             (scale, scale, "eps", ALU.add), (scale, scale, "minus_half", ALU.pow),
                             (scale, scale, total, ALU.mult))
                    pool.wait_ge(moments_ready, turn(s))
                    for k, (dst, one, other, op) in enumerate(steps):
                        if k:
                            pool.wait_ge(scale_step, (it * SLOTS + s) * 4 + k)
                        if other is None:
                            second = mv[:, s, :, 1]
                        elif isinstance(other, str):
                            second = consts[other][:, 0:TILE]
                        else:
                            second = other[:, s]
                        nc.gpsimd.tensor_tensor(dst[:, s], one[:, s], second, op).then_inc(
                            scale_step if k < 4 else scale_ready, 1)
                for s in range(SLOTS):
                    pool.wait_ge(head_normed, turn(s))
                    nc.gpsimd.tensor_tensor(graphs(att[:, s]), graphs(att[:, s]),
                                            gamma[:].unsqueeze(1).broadcast_to([P, TILE, P]), ALU.mult).then_inc(gained, 1)
                    alone(pool, consts["identity_in"])
                    pool.wait_ge(gained, turn(s))
                    nc.gpsimd.tensor_tensor(hn[:, bass.ds((it * SLOTS + s) * TILE, TILE), :], graphs(att[:, s]),
                                            beta[:].unsqueeze(1).broadcast_to([P, TILE, P]), ALU.add).then_inc(hn_ready, 1)

        @block.vector
        def _(dve):
            with dve.Fori(0, ROUNDS) as it:
                def turn(s):
                    return it * SLOTS + s + 1
                for s in range(SLOTS):
                    nc.vector.tensor_scalar(graphs(bars[:, s]), adj[:, bass.ds((it * SLOTS + s) * TILE, TILE), :],
                                            0.0, NEG, ALU.is_le, ALU.mult).then_inc(barred, 1)
                for s in range(SLOTS):
                    dve.wait_ge(wh_done, turn(s))
                    nc.vector.tensor_copy(wh[:, s], ps[:, 2 * s + 1, :]).then_inc(wh_ready, 1)
                for s in range(SLOTS):
                    dve.wait_ge(score_copied, turn(s))
                    nc.vector.scalar_tensor_tensor(out=score[:, s], in0=score[:, s], scalar=ALPHA,
                                                   in1=ps[:, 2 * s, :], op0=ALU.mult, op1=ALU.max).then_inc(leaked, 1)
                    dve.wait_ge(leaked, turn(s))
                    dve.wait_ge(barred, turn(s))
                    nc.vector.tensor_tensor(score[:, s], score[:, s], bars[:, s], ALU.add).then_inc(masked, 1)
                    dve.wait_ge(masked, turn(s))
                    nc.vector.tensor_reduce(top[:, s], graphs(score[:, s]), AX_X, ALU.max).then_inc(top_found, 1)
                    dve.wait_ge(top_found, turn(s))
                    nc.vector.tensor_scalar(top[:, s], top[:, s], -1.0, None, ALU.mult).then_inc(top_ready, 1)
                for s in range(SLOTS):
                    dve.wait_ge(exp_ready, turn(s))
                    nc.vector.reciprocal(total[:, s], total[:, s]).then_inc(total_inverted, 1)
                for s in range(SLOTS):
                    dve.wait_ge(head_ready, turn(s))
                    for g in range(TILE):
                        one = nc.vector.bn_stats(stats[:, s, g, :], graph(att, s, g))
                    one.then_inc(stats_ready, 1)
                    alone(dve, consts["identity_in"])
                    dve.wait_ge(stats_ready, turn(s))
                    for g in range(TILE):
                        one = nc.vector.bn_aggr(mv[:, s, g, :], stats[:, s, g, :])
                    one.then_inc(moments_ready, 1)
                for s in range(SLOTS):
                    dve.wait_ge(scale_ready, turn(s))
                    for g in range(TILE):
                        one = nc.vector.tensor_scalar(graph(att, s, g), graph(att, s, g), mv[:, s, g, 0:1],
                                                      scale[:, s, g:g + 1], ALU.subtract, ALU.mult)
                    one.then_inc(head_normed, 1)

        @block.tensor
        def _(pe):
            pe.sem_inc(x_turned, SLOTS)
            pe.wait_ge(w_in, 96)
            nc.tensor.matmul(ps[:, 0, 0:P], w_t[:], a1[:], start=True, stop=True)
            nc.tensor.matmul(ps[:, 0, P:2 * P], w_t[:], a2[:], start=True, stop=True).then_inc(wa_done, 1)
            pe.wait_ge(wa_ready, 1)
            with pe.Fori(0, ROUNDS) as it:
                def turn(s):
                    return it * SLOTS + s + 1
                for s in range(SLOTS):
                    pe.wait_ge(x_loaded[s], it * 16 + 16)
                    for g in range(TILE):
                        one = nc.tensor.transpose(ps[:, 2 * s, g * P:(g + 1) * P], graph(x_in, s, g), identity[:])
                    one.then_inc(x_turned, 1)
                for s in range(SLOTS):
                    pe.wait_ge(xt_ready, turn(s))
                    for g in range(TILE):
                        one = nc.tensor.matmul(ps[:, 2 * s + 1, g * P:(g + 1) * P], graph(xt, s, g), w[:],
                                               start=True, stop=True)
                    one.then_inc(wh_done, 1)
                    nc.tensor.matmul(ps[:, 2 * s, :], wa2[:], xt[:, s], start=True, stop=False)
                    for g in range(TILE):
                        one = nc.tensor.matmul(ps[:, 2 * s, g * P:(g + 1) * P], graph(xt, s, g), wa1[:],
                                               start=False, stop=g == TILE - 1)
                    one.then_inc(score_done, 1)
                for s in range(SLOTS):
                    pe.wait_ge(exp_ready, turn(s))
                    for g in range(TILE):
                        one = nc.tensor.transpose(ps[:, 2 * s, g * P:(g + 1) * P], graph(att, s, g), identity[:])
                    one.then_inc(att_turned, 1)
                for s in range(SLOTS):
                    pe.wait_ge(att_t_ready, turn(s))
                    pe.wait_ge(wh_ready, turn(s))
                    for g in range(TILE):
                        one = nc.tensor.matmul(ps[:, 2 * s + 1, g * P:(g + 1) * P], graph(att_t, s, g), graph(wh, s, g),
                                               start=True, stop=True)
                    one.then_inc(head_done, 1)


def finish_attention(nc, dram, X, adj, hn, x_fm, consts, inverse_t):
    with ExitStack() as ctx:
        def sb(name, shape):
            return ctx.enter_context(nc.sbuf_tensor(name, shape, F32))

        def sem(name):
            return ctx.enter_context(nc.semaphore(name))

        CHUNK = 8
        stats = sb("stats3", [P, 2, CHUNK, 6])
        mv = sb("mv3", [P, 2, CHUNK, 2])
        rstd = sb("rstd3", [P, 2, CHUNK])
        staged = sb("staged", [P, 2, CHUNK, P])
        inverse = sb("inverse", [P, 2, CHUNK, P])
        ps = ctx.enter_context(nc.psum_tensor("ps3", [P, 4, 512], F32))

        gelu_ready = sem("gelu_ready")
        added = sem("added2")
        stats_ready = sem("stats3_ready")
        moments_ready = sem("moments3_ready")
        var_eps = sem("var_eps3")
        rstd_ready = sem("rstd3_ready")
        normed = sem("normed3")
        staged_in = [sem(f"staged_in{s}") for s in range(2)]
        kept = sem("kept")
        turned = sem("turned3")
        laid = sem("laid3")
        inverse_in = [sem(f"inverse_in{s}") for s in range(2)]
        divided = sem("divided")
        ROUNDS = B // CHUNK // 2

        block = ctx.enter_context(nc.Block())

        @block.sync
        def _(sp):
            with sp.Fori(0, ROUNDS) as it:
                for s in range(2):
                    part = bass.ds((it * 2 + s) * CHUNK, CHUNK)
                    alone(sp, consts["identity_in"])
                    sp.wait_ge(divided, it * 2 + s + 1)
                    sp.dma_start(inverse[:, s], inverse_t[part, :].unsqueeze(0).broadcast_to([P, CHUNK, P])).then_inc(
                        inverse_in[s], 16)
                for s in range(2):
                    part = bass.ds((it * 2 + s) * CHUNK, CHUNK)
                    alone(sp, consts["identity_in"])
                    sp.wait_ge(normed, it * 2 + s + 1)
                    alone(sp, consts["identity_in"])
                    sp.wait_ge(turned, it * 2 + s + 1)
                    sp.dma_start(staged[:, s], X[:, part, :]).then_inc(staged_in[s], 16)
                    sp.dma_start(hn[:, part, :], X[:, part, :]).then_inc(kept, 16)
            sp.wait_ge(kept, 16 * 2 * ROUNDS)

        @block.scalar
        def _(act):
            act.sem_inc(laid, 4)
            with act.Fori(0, ROUNDS) as it:
                for s in range(2):
                    part = hn[:, bass.ds((it * 2 + s) * CHUNK, CHUNK), :]
                    nc.scalar.activation(part, part, ACT.Gelu).then_inc(gelu_ready, 1)
                for s in range(2):
                    for k in range(2):
                        alone(act, consts["identity_in"])
                        act.wait_ge(turned, it * 2 + s + 3)
                        nc.scalar.copy(x_fm[:, :, bass.ds((it * 2 + s) * CHUNK + k * 4, 4)],
                                       ps[:, 2 * s + k, :].rearrange("p (b n) -> p n b", b=4)).then_inc(laid, 1)

        @block.gpsimd
        def _(pool):
            pool.sem_inc(divided, 2)
            with pool.Fori(0, ROUNDS) as it:
                for s in range(2):
                    pool.wait_ge(moments_ready, it * 2 + s + 1)
                    nc.gpsimd.tensor_tensor(mv[:, s, :, 1], mv[:, s, :, 1], consts["eps"][:, 0:CHUNK],
                                            ALU.add).then_inc(var_eps, 1)
                    pool.wait_ge(var_eps, it * 2 + s + 1)
                    nc.gpsimd.tensor_tensor(rstd[:, s, :], mv[:, s, :, 1], consts["minus_half"][:, 0:CHUNK],
                                            ALU.pow).then_inc(rstd_ready, 1)
                for s in range(2):
                    part = adj[:, bass.ds((it * 2 + s) * CHUNK, CHUNK), :]
                    alone(pool, consts["identity_in"])
                    pool.wait_ge(inverse_in[s], it * 16 + 16)
                    nc.gpsimd.tensor_tensor(part, part, inverse[:, s], ALU.mult).then_inc(divided, 1)

        @block.vector
        def _(dve):
            with dve.Fori(0, ROUNDS) as it:
                for s in range(2):
                    at = (it * 2 + s) * CHUNK
                    dve.wait_ge(gelu_ready, it * 2 + s + 1)
                    part = X[:, bass.ds(at, CHUNK), :]
                    nc.vector.tensor_tensor(part, part, hn[:, bass.ds(at, CHUNK), :], ALU.add).then_inc(added, 1)
                    alone(dve, consts["identity_in"])
                    dve.wait_ge(added, it * 2 + s + 1)
                    for b in range(CHUNK):
                        one = nc.vector.bn_stats(stats[:, s, b, :], X[:, bass.ds(at + b, 1), :])
                    one.then_inc(stats_ready, 1)
                    alone(dve, consts["identity_in"])
                    dve.wait_ge(stats_ready, it * 2 + s + 1)
                    for b in range(CHUNK):
                        one = nc.vector.bn_aggr(mv[:, s, b, :], stats[:, s, b, :])
                    one.then_inc(moments_ready, 1)
                for s in range(2):
                    dve.wait_ge(rstd_ready, it * 2 + s + 1)
                    for b in range(CHUNK):
                        part = X[:, bass.ds((it * 2 + s) * CHUNK + b, 1), :]
                        one = nc.vector.tensor_scalar(part, part, mv[:, s, b, 0:1], rstd[:, s, b:b + 1],
                                                      ALU.subtract, ALU.mult)
                    one.then_inc(normed, 1)

        @block.tensor
        def _(pe):
            pe.sem_inc(turned, 2)
            with pe.Fori(0, ROUNDS) as it:
                for s in range(2):
                    pe.wait_ge(staged_in[s], it * 16 + 16)
                    pe.wait_ge(laid, it * 4 + 2 * s + 1)
                    for b in range(CHUNK):
                        one = nc.tensor.transpose(ps[:, 2 * s + b // 4, (b % 4) * P:(b % 4 + 1) * P],
                                                  staged[:, s, b, :], consts["identity"][:])
                    one.then_inc(turned, 1)


def gated_scan(nc, dram, X, adj, x_fm, consts, inverse_t, inverse):
    with ExitStack() as ctx:
        def sb(name, shape, dt=F32):
            return ctx.enter_context(nc.sbuf_tensor(name, shape, dt))

        def sem(name):
            return ctx.enter_context(nc.semaphore(name))

        BLOCKS = P // S
        GB = P // S
        NG = B // GB
        wx = sb("wx", [P, 3, P])
        wh = sb("wh3", [P, 3, P])
        bias_x = sb("bias_x", [P, 3])
        bias_h = sb("bias_h", [P, 3])
        bias = sb("bias3", [P, 3])
        parts = sb("parts", [PARTS[-1] + S, BLOCKS, S, B], BF16)
        select_f = sb("select_f", [PARTS[-1] + S, S, P])
        select = sb("select", [PARTS[-1] + S, S, P], BF16)
        same_graph = sb("same_graph", [P, GB, S])
        nexts = sb("nexts", [P, BLOCKS - 1, NG, S])
        step_mat = sb("step_mat", [P, NG, GB, S])
        with ExitStack() as preparing:
            spread_coefficients(nc, dram, consts, preparing, inverse_t, inverse, parts, nexts)

        sums = sb("sums", [P, S, B])
        delta = sb("delta", [P, S, B])
        h_new = sb("h_new", [P, S, B])
        delta_nm = sb("delta_nm", [P, NG, P])
        h_nm = sb("h_nm", [P, NG, P])
        r = sb("r3", [P, B])
        z = sb("z3", [P, 2, B])
        hc = sb("hc", [P, 2, B])
        x_par = sb("x_par", [P, 2, B])
        xr = sb("xr", [P, B])
        early = sb("early", [P, B])
        late = sb("late", [P, B])
        near_z = sb("near_z", [P, B])
        zx = sb("zx", [P, B])
        kept = sb("kept3", [P, 2, B])
        near_kept = sb("near_kept", [P, B])
        fresh = sb("fresh", [P, B])
        far = sb("far", [P, S, B])
        ps = ctx.enter_context(nc.psum_tensor("ps4", [P, 8, 512], F32))
        R, Z, C, BASE, TURN, COEF = 0, 1, 2, 3, 4, (5, 6)
        identity = consts["identity"]

        w_in, small_in, select_in = sem("w3_in"), sem("small3_in"), sem("select_in")
        bias_ready, select_ready = sem("bias_ready"), sem("select_ready")
        step_ready = sem("step_mat_ready")
        base_done, base_full, sums_ready = sem("base_done"), sem("base_full"), sem("sums_ready")
        r_done, z_done, c_done, coef_done = sem("r3_done"), sem("z3_done"), sem("c3_done"), sem("coef_done")
        r_ready, z_ready, hc_ready = sem("r3_ready"), sem("z3_ready"), sem("hc_ready")
        x_ready, late_ready, xr_ready, early_ready = sem("x_par_ready"), sem("late_ready"), sem("xr_ready"), sem("early_ready")
        fresh_ready, delta_ready, far_ready = sem("fresh_ready"), sem("delta_ready"), sem("far_ready")
        near_z_ready, near_kept_ready = sem("near_z_ready"), sem("near_kept_ready")
        zx_ready, kept_ready, h_ready, far_added = sem("zx_ready"), sem("kept_ready"), sem("h3_ready"), sem("far_added")
        delta_turned, delta_nm_ready = sem("delta_turned"), sem("delta_nm_ready")
        h_turned, h_nm_ready, rows_in = sem("h_turned"), sem("h_nm_ready"), sem("rows_in")

        def blocks(eng, body):
            with eng.Fori(0, BLOCKS - 1) as m:
                body(m, False)
            body(BLOCKS - 1, True)

        def old(m, s):
            return x_fm[:, bass.ds(m * S + s, 1), :].squeeze(1)

        block = ctx.enter_context(nc.Block())

        @block.sync
        def _(sp):
            sp.sem_inc(rows_in, 16)
            sp.dma_start(wx[:], dram["L3_wx"]).then_inc(w_in, 16)
            sp.dma_start(wh[:], dram["L3_wh"]).then_inc(w_in, 16)
            sp.dma_start(select_f[:], dram["select"]).then_inc(select_in, 16)

            for m in range(BLOCKS):
                sp.wait_ge(h_nm_ready, m + 2)
                if m + 1 < BLOCKS:
                    sp.wait_ge(base_done, m + 2)
                sp.dma_start(X[m * S:(m + 1) * S].rearrange("n (b g) d -> n b (g d)", g=NG),
                             h_nm[:].rearrange("p g d -> p (g d)")).then_inc(rows_in, 16)
            sp.wait_ge(rows_in, 16 * BLOCKS + 16)

        @block.scalar
        def _(act):
            act.dma_start(bias_x[:], dram["L3_bx"]).then_inc(small_in, 16)
            act.dma_start(bias_h[:], dram["L3_bh"]).then_inc(small_in, 16)
            act.dma_start(same_graph[:], dram["same_graph"]).then_inc(small_in, 16)
            act.sem_inc(h_nm_ready, 1)
            act.wait_ge(select_in, 16)
            nc.scalar.copy(select[:], select_f[:]).then_inc(select_ready, 1)
            act.wait_ge(bias_ready, 1)

            def body(m, last):
                for s in range(S):
                    turn = m * S + s + 1
                    act.wait_ge(r_done, turn)
                    nc.scalar.activation(r[:], ps[:, R, 0:B], ACT.Sigmoid, bias=bias[:, 0:1]).then_inc(r_ready, 1)
                    act.wait_ge(z_done, turn)
                    nc.scalar.activation(z[:, s % 2], ps[:, Z, 0:B], ACT.Sigmoid, bias=bias[:, 1:2]).then_inc(z_ready, 1)
                    act.wait_ge(c_done, turn)
                    nc.scalar.activation(hc[:, s % 2], ps[:, C, 0:B], ACT.Tanh, bias=bias[:, 2:3]).then_inc(hc_ready, 1)
                act.wait_ge(h_turned, m + 1)
                act.wait_ge(rows_in, m * 16 + 16)
                nc.scalar.copy(h_nm[:].rearrange("p g d -> p (g d)"), ps[:, TURN, :]).then_inc(h_nm_ready, 1)

            blocks(act, body)

        @block.gpsimd
        def _(pool):
            pool.wait_ge(small_in, 48)

            def after(m, s):
                if s + 2 < S:
                    pool.wait_ge(far_ready, m * (S - 2) + s + 1)
                    nc.gpsimd.tensor_tensor(sums[:, s + 2:S, :], sums[:, s + 2:S, :], far[:, s + 2:S, :],
                                            ALU.add).then_inc(far_added, 1)
                alone(pool, consts["identity_in"])
                pool.wait_ge(delta_ready, m * S + s + 1)
                nc.gpsimd.tensor_tensor(h_new[:, s], delta[:, s], old(m, s), ALU.add).then_inc(h_ready, 1)

            def body(m, last):
                for s in range(S):
                    turn = m * S + s + 1
                    if s == 2 and not last:
                        alone(pool, consts["identity_in"])
                        pool.wait_ge(base_full, m + 1)
                        nc.gpsimd.tensor_tensor(
                            step_mat[:], nexts[:, bass.ds(m, 1)].squeeze(1).unsqueeze(2).broadcast_to([P, NG, GB, S]),
                            same_graph[:].unsqueeze(1).broadcast_to([P, NG, GB, S]), ALU.mult).then_inc(step_ready, 1)
                    pool.wait_ge(x_ready, turn)
                    pool.wait_ge(z_ready, turn)
                    nc.gpsimd.tensor_tensor(zx[:], z[:, s % 2], x_par[:, s % 2], ALU.mult).then_inc(zx_ready, 1)
                    alone(pool, consts["identity_in"])
                    pool.wait_ge(zx_ready, turn)
                    nc.gpsimd.tensor_tensor(kept[:, s % 2], zx[:], old(m, s), ALU.subtract).then_inc(kept_ready, 1)
                    if s:
                        after(m, s - 1)
                after(m, S - 1)

            blocks(pool, body)

        @block.vector
        def _(dve):
            dve.wait_ge(small_in, 48)
            nc.vector.tensor_tensor(bias[:], bias_x[:], bias_h[:], ALU.add).then_inc(bias_ready, 1)

            def after(m, s):
                dve.wait_ge(hc_ready, m * S + s + 1)
                if s + 1 < S:
                    step = m * (S - 1) + s + 1
                    dve.wait_ge(near_z_ready, step)
                    nc.vector.tensor_tensor(late[:], near_z[:], hc[:, s % 2], ALU.mult).then_inc(late_ready, 1)
                nc.vector.scalar_tensor_tensor(out=fresh[:], in0=z[:, s % 2], scalar=1.0, in1=hc[:, s % 2],
                                               op0=ALU.subtract, op1=ALU.mult, reverse0=True).then_inc(fresh_ready, 1)
                if s + 1 < S:
                    dve.wait_ge(early_ready, step)
                    dve.wait_ge(late_ready, step)
                    nc.vector.tensor_tensor(x_par[:, (s + 1) % 2], early[:], late[:], ALU.add).then_inc(x_ready, 1)
                dve.wait_ge(fresh_ready, m * S + s + 1)
                dve.wait_ge(kept_ready, m * S + s + 1)
                nc.vector.tensor_tensor(delta[:, s], fresh[:], kept[:, s % 2], ALU.add).then_inc(delta_ready, 1)

            def body(m, last):
                dve.wait_ge(base_full, m + 1)
                base = ps[:, BASE, :].rearrange("p (b i) -> p i b", i=S)
                nc.vector.tensor_copy(x_par[:, 0], base[:, 0]).then_inc(x_ready, 1)
                nc.vector.tensor_copy(sums[:, 1:S], base[:, 1:S]).then_inc(sums_ready, 1)
                for s in range(S):
                    turn, step = m * S + s + 1, m * (S - 1) + s + 1
                    if s:
                        after(m, s - 1)
                    dve.wait_ge(r_ready, turn)
                    dve.wait_ge(x_ready, turn)
                    nc.vector.tensor_tensor(xr[:], x_par[:, s % 2], r[:], ALU.mult).then_inc(xr_ready, 1)
                    if s and s + 1 < S:
                        dve.wait_ge(delta_ready, m * S + s)
                        coef = ps[:, COEF[(s - 1) % 2], :].rearrange("p (i b) -> p i b", b=B)
                        nc.vector.tensor_tensor(far[:, s + 1:S], coef[:, s + 1:S],
                                                delta[:, s - 1].unsqueeze(1).broadcast_to([P, S - s - 1, B]),
                                                ALU.mult).then_inc(far_ready, 1)
                    if s + 1 < S:
                        near = ps[:, COEF[s % 2], (s + 1) * B:(s + 2) * B]
                        dve.wait_ge(coef_done, step)
                        dve.wait_ge(z_ready, turn)
                        nc.vector.scalar_tensor_tensor(out=near_z[:], in0=z[:, s % 2], scalar=1.0, in1=near,
                                                       op0=ALU.subtract, op1=ALU.mult, reverse0=True).then_inc(near_z_ready, 1)
                        dve.wait_ge(kept_ready, turn)
                        nc.vector.tensor_tensor(near_kept[:], kept[:, s % 2], near, ALU.mult).then_inc(near_kept_ready, 1)
                        dve.wait_ge(sums_ready, m + 1)
                        if s:
                            dve.wait_ge(far_added, m * (S - 2) + s)
                        dve.wait_ge(near_kept_ready, step)
                        nc.vector.tensor_tensor(early[:], sums[:, s + 1], near_kept[:], ALU.add).then_inc(early_ready, 1)
                after(m, S - 1)
                if not last:
                    dve.wait_ge(delta_turned, m + 1)
                    nc.vector.tensor_copy(delta_nm[:].rearrange("p g d -> p (g d)"), ps[:, TURN, :]).then_inc(delta_nm_ready, 1)

            blocks(dve, body)

        @block.tensor
        def _(pe):
            pe.sem_inc(base_done, 1)
            pe.wait_ge(w_in, 32)
            pe.wait_ge(select_ready, 1)

            def base(m, graphs, done):
                for b in graphs:
                    one = nc.tensor.matmul(ps[:, BASE, b * S:(b + 1) * S], X[:, b, :], adj[:, b, bass.ds(m * S, S)],
                                           start=b == 0, stop=False, skip_group_check=True)
                if b == B - 1:
                    one.then_inc(done, 1)

            def turn_block(slab):
                for g in range(NG):
                    one = nc.tensor.transpose(ps[:, TURN, g * P:(g + 1) * P], slab[:].rearrange("p n (b g) -> p g n b", g=NG)[:, g], identity[:])
                return one

            base(0, range(B), base_full)

            def body(m, last):
                for s in range(S):
                    turn, step = m * S + s + 1, m * (S - 1) + s
                    x = old(m, s)
                    nc.tensor.matmul(ps[:, R, 0:B], wx[:, 0, :], x, start=True, stop=False)
                    if s:
                        pe.wait_ge(early_ready, step)
                        nc.tensor.matmul(ps[:, R, 0:B], wh[:, 0, :], early[:], start=False, stop=False)
                    nc.tensor.matmul(ps[:, Z, 0:B], wx[:, 1, :], x, start=True, stop=False)
                    if s:
                        pe.wait_ge(late_ready, step)
                        nc.tensor.matmul(ps[:, R, 0:B], wh[:, 0, :], late[:], start=False, stop=True).then_inc(r_done, 1)
                        pe.wait_ge(x_ready, turn)
                    else:
                        pe.wait_ge(x_ready, turn)
                        nc.tensor.matmul(ps[:, R, 0:B], wh[:, 0, :], x_par[:, 0], start=False, stop=True).then_inc(r_done, 1)
                    nc.tensor.matmul(ps[:, Z, 0:B], wh[:, 1, :], x_par[:, s % 2], start=False, stop=True).then_inc(z_done, 1)
                    if s + 1 < S:
                        if s > 1:
                            pe.wait_ge(far_ready, m * (S - 2) + s - 1)
                        nc.tensor.matmul(ps[:, COEF[s % 2], (s + 1) * B:S * B], select[:, s, :],
                                         parts[:, bass.ds(m, 1), s + 1:S, :].squeeze(1), start=True, stop=True).then_inc(coef_done, 1)
                    nc.tensor.matmul(ps[:, C, 0:B], wx[:, 2, :], x, start=True, stop=False)
                    if not last:
                        if s == 0:
                            pe.wait_ge(sums_ready, m + 1)
                            pe.wait_ge(rows_in, m * 16 + 16)
                        base(m + 1, range(s * B // S, s * B // S + B // S // 2), base_done)
                    pe.wait_ge(xr_ready, turn)
                    nc.tensor.matmul(ps[:, C, 0:B], wh[:, 2, :], xr[:], start=False, stop=True).then_inc(c_done, 1)
                    if not last:
                        base(m + 1, range(s * B // S + B // S // 2, (s + 1) * B // S), base_done)
                if not last:
                    pe.wait_ge(h_nm_ready, m + 1)
                    pe.wait_ge(delta_ready, (m + 1) * S)
                    turn_block(delta).then_inc(delta_turned, 1)
                    pe.wait_ge(step_ready, m + 1)
                    pe.wait_ge(delta_nm_ready, m + 1)
                    for g in range(NG):
                        one = nc.tensor.matmul(ps[:, BASE, :].rearrange("p (b g i) -> p g b i", g=NG, i=S)[:, g], delta_nm[:, g, :],
                                               step_mat[:, g], start=False, stop=True,
                                               skip_group_check=True)
                    one.then_inc(base_full, 1)
                else:
                    pe.wait_ge(h_nm_ready, BLOCKS)
                pe.wait_ge(h_ready, (m + 1) * S)
                turn_block(h_new).then_inc(h_turned, 1)

            blocks(pe, body)


def spread_coefficients(nc, dram, consts, ctx, inverse_t, inverse, parts, nexts):
    def sb(name, shape, dt=F32):
        return ctx.enter_context(nc.sbuf_tensor(name, shape, dt))

    def sem(name):
        return ctx.enter_context(nc.semaphore(name))

    NG = B * S // P
    diag = sb("diag", [P, B, S])
    low = sb("low", [P, B, S])
    parts_bf = sb("parts_bf", [P, 3, S, B], BF16)
    inverse_8 = sb("inverse_8", [P, B, S])
    eye_8 = sb("eye_8", [P, S])
    same_block = sb("same_block", [P, P])
    inverse_n = sb("inverse_n", [P, NG, P])
    ps = ctx.enter_context(nc.psum_tensor("ps5", [P, 512], F32))
    nexts_in, diag_in, cleared = sem("nexts_in"), sem("diag_in"), sem("cleared")
    diagonal_ready, inverse_done, split, nexts_ready = sem("diagonal_ready"), sem("inverse_done"), sem("split"), sem("nexts_ready")
    parts_out, parts_in = sem("parts_out"), sem("parts_in")

    block = ctx.enter_context(nc.Block())

    @block.sync
    def _(sp):
        sp.dma_start(diag[:], dram["adj_diag"]).then_inc(diag_in, 16)
        sp.dma_start(eye_8[:], dram["eye_8"]).then_inc(diag_in, 16)
        sp.dma_start(same_block[:], dram["same_block"]).then_inc(diag_in, 16)
        for n in range(S):
            sp.dma_start(inverse_n[n * P // S:(n + 1) * P // S],
                         inverse_t.rearrange("(b g) i -> b g i", g=NG)).then_inc(nexts_in, 16)
        sp.dma_start(nexts[:], dram["adj_next"]).then_inc(nexts_in, 16)
        sp.wait_ge(split, 6)
        sp.dma_start(dram["parts"], parts_bf[:].rearrange("p k i b -> p k (i b)")).then_inc(parts_out, 16)
        sp.wait_ge(parts_out, 16)
        sp.wait_ge(cleared, 1)
        for k, at in enumerate(PARTS):
            sp.dma_start(parts[at:at + S].rearrange("n m i b -> n m (i b)"),
                         dram["parts"][:, k, :].rearrange("(m n) f -> n m f", n=S)).then_inc(parts_in, 16)
        sp.wait_ge(parts_in, 16 * len(PARTS))

    @block.gpsimd
    def _(pool):
        nc.gpsimd.memset(parts[:], 0.0).then_inc(cleared, 1)

    @block.vector
    def _(dve):
        dve.wait_ge(diag_in, 48)
        nc.vector.tensor_tensor(inverse_8[:], inverse[:].unsqueeze(2).broadcast_to([P, B, S]),
                                eye_8[:].unsqueeze(1).broadcast_to([P, B, S]), ALU.mult).then_inc(diagonal_ready, 1)
        dve.wait_ge(inverse_done, 1)
        nc.vector.tensor_tensor(diag[:], diag[:], ps[:].rearrange("p (b i) -> p b i", i=S), ALU.mult).then_inc(split, 1)

        def part(k):
            return parts_bf[:, k].rearrange("p i b -> p b i")

        for k in range(3):
            rest = diag if k == 0 else low
            dve.wait_ge(split, 2 * k + 1)
            nc.vector.tensor_copy(part(k), rest[:]).then_inc(split, 1)
            if k < 2:
                dve.wait_ge(split, 2 * k + 2)
                nc.vector.tensor_tensor(low[:], rest[:], part(k), ALU.subtract).then_inc(split, 1)
        dve.wait_ge(nexts_in, 16 * (S + 1))
        nc.vector.tensor_tensor(nexts[:], nexts[:], inverse_n[:, :, S:P].rearrange("p g (m i) -> p m g i", i=S),
                                ALU.mult).then_inc(nexts_ready, 1)

    @block.tensor
    def _(pe):
        pe.wait_ge(diagonal_ready, 1)
        nc.tensor.matmul(ps[:], same_block[:], inverse_8[:].rearrange("p b i -> p (b i)"), start=True,
                         stop=True).then_inc(inverse_done, 1)


def final_norm(nc, X, x_kept, consts, out):
    with ExitStack() as ctx:
        def sb(name, shape):
            return ctx.enter_context(nc.sbuf_tensor(name, shape, F32))

        def sem(name):
            return ctx.enter_context(nc.semaphore(name))

        CHUNK = 8
        stats = sb("stats6", [P, 2, CHUNK, 6])
        mv = sb("mv6", [P, 2, CHUNK, 2])
        rstd = sb("rstd6", [P, 2, CHUNK])
        spare = sb("spare6", [P, 1])
        summed, stats_ready, moments_ready = sem("summed6"), sem("stats6_ready"), sem("moments6_ready")
        var_eps, rstd_ready, normed, stored = sem("var_eps6"), sem("rstd6_ready"), sem("normed6"), sem("stored")
        ROUNDS = B // CHUNK // 2
        block = ctx.enter_context(nc.Block())

        @block.sync
        def _(sp):
            with sp.Fori(0, ROUNDS) as it:
                for s in range(2):
                    part = bass.ds((it * 2 + s) * CHUNK, CHUNK)
                    sp.wait_ge(normed, it * 2 + s + 1)
                    sp.dma_start(out[:, part, :], X[:, part, :]).then_inc(stored, 16)
            sp.wait_ge(stored, 16 * 2 * ROUNDS)

        @block.gpsimd
        def _(pool):
            with pool.Fori(0, ROUNDS) as it:
                for s in range(2):
                    pool.wait_ge(moments_ready, it * 2 + s + 1)
                    nc.gpsimd.tensor_tensor(mv[:, s, :, 1], mv[:, s, :, 1], consts["eps"][:, 0:CHUNK],
                                            ALU.add).then_inc(var_eps, 1)
                    pool.wait_ge(var_eps, it * 2 + s + 1)
                    nc.gpsimd.tensor_tensor(rstd[:, s, :], mv[:, s, :, 1], consts["minus_half"][:, 0:CHUNK],
                                            ALU.pow).then_inc(rstd_ready, 1)

        @block.vector
        def _(dve):
            with dve.Fori(0, ROUNDS) as it:
                for s in range(2):
                    at = (it * 2 + s) * CHUNK
                    part = X[:, bass.ds(at, CHUNK), :]
                    nc.vector.tensor_tensor(part, part, x_kept[:, bass.ds(at, CHUNK), :], ALU.add).then_inc(summed, 1)
                    dve.wait_ge(summed, it * 2 + s + 1)
                    nc.vector.memset(spare[:], 0.0)
                    for b in range(CHUNK):
                        one = nc.vector.bn_stats(stats[:, s, b, :], X[:, bass.ds(at + b, 1), :])
                    one.then_inc(stats_ready, 1)
                    alone(dve, consts["identity_in"])
                    dve.wait_ge(stats_ready, it * 2 + s + 1)
                    for b in range(CHUNK):
                        one = nc.vector.bn_aggr(mv[:, s, b, :], stats[:, s, b, :])
                    one.then_inc(moments_ready, 1)
                for s in range(2):
                    dve.wait_ge(rstd_ready, it * 2 + s + 1)
                    for b in range(CHUNK):
                        part = X[:, bass.ds((it * 2 + s) * CHUNK + b, 1), :]
                        one = nc.vector.tensor_scalar(part, part, mv[:, s, b, 0:1], rstd[:, s, b:b + 1],
                                                      ALU.subtract, ALU.mult)
                    one.then_inc(normed, 1)


def graph_layers(nc, dram, out):
    with ExitStack() as ctx:
        def sb(name, shape):
            return ctx.enter_context(nc.sbuf_tensor(name, shape, F32))

        def sem(name):
            return ctx.enter_context(nc.semaphore(name))

        X = sb("X", [P, B, P])
        adj = sb("adj", [P, B, P])
        node_degree = sb("node_degree", [P, B])
        degrees_ready = sem("degrees_ready")
        inverse_stored = sem("inverse_stored")
        consts = {"identity": sb("identity", [P, P]), "minus_half": sb("minus_half", [P, B]), "eps": sb("eps", [P, B]),
                  "identity_in": sem("identity_in")}
        with ExitStack() as groups:
            norm_t = groups.enter_context(nc.sbuf_tensor("norm_t", [Q, B, Q], F32))
            root_diag = groups.enter_context(nc.sbuf_tensor("root_diag", [Q, B, Q], F32))
            groups_ready = groups.enter_context(nc.semaphore("groups_ready"))
            gated_convolution(nc, dram, X, adj, consts, norm_t, root_diag, groups_ready, node_degree,
                              degrees_ready)
            group_convolution(nc, dram, X, consts, norm_t, root_diag, groups_ready, node_degree,
                              dram["inverse_t"], inverse_stored)
        hn = ctx.enter_context(nc.sbuf_tensor("hn", [P, B, P], F32))
        graph_attention(nc, dram, X, adj, hn, consts)
        x_fm = ctx.enter_context(nc.sbuf_tensor("x_fm", [P, P, B], F32))
        finish_attention(nc, dram, X, adj, hn, x_fm, consts, dram["inverse_t"])
        gated_scan(nc, dram, X, adj, x_fm, consts, dram["inverse_t"], node_degree)
        final_norm(nc, X, hn, consts, out)


def kernel(**inputs):
    import numpy as np
    import concourse.bacc as bacc
    from concourse.bass_utils import run_bass_kernel_spmd

    def lay(a):
        return np.ascontiguousarray(a)

    a = {k: np.asarray(v) for k, v in inputs.items()}
    x, adj = a["x"], a["adj"]
    group_of = [g for g, nodes in enumerate(GROUPS) for _ in nodes]
    blocks = np.zeros((Q, B, Q), adj.dtype)
    blocks_t = np.zeros((Q, B, Q), adj.dtype)
    to_joint = np.zeros((Q, JOINTS), np.float32)
    for q, n in enumerate(ROWS):
        to_joint[q, n] = 1.0
        for p, m in enumerate(ROWS):
            if group_of[p] == group_of[q]:
                blocks[q, :, p] = adj[:, n, m]
                blocks_t[q, :, p] = adj[:, m, n]
    G = len(GROUPS)
    blocks_of = P // S
    by_block = adj.reshape(B, blocks_of, S, blocks_of, S)
    own = np.stack([by_block[:, m, :, m] for m in range(blocks_of)])
    following = np.stack([by_block[:, m, :, m + 1] for m in range(blocks_of - 1)])
    select = np.zeros((PARTS[-1] + S, S, P), np.float32)
    for s in range(S):
        for at in PARTS:
            select[at + s, s] = 1.0
    node = np.arange(P)
    gate = a["L3_gnn_W_ioux"].reshape(2, P, P).transpose(2, 0, 1), a["L3_gnn_W_iouh"].reshape(2, P, P).transpose(2, 0, 1)
    wide = (P, P)
    arrays = {
        "adj_diag": lay(own.transpose(0, 2, 1, 3).reshape(P, B, S)),
        "adj_next": lay(following.reshape(blocks_of - 1, P // S, B * S // P, S, S).transpose(3, 1, 0, 2, 4).reshape(
            P, blocks_of - 1, B * S // P, S)),
        "eye_8": (node[:, None] % S == np.arange(S)).astype(np.float32),
        "same_block": (node[:, None] // S == node // S).astype(np.float32),
        "same_graph": lay(np.broadcast_to((node[:, None] % (P // S) == np.arange(P // S))[:, :, None],
                                          (P, P // S, S)).astype(np.float32)),
        "select": select,
        "L3_wx": lay(np.concatenate([gate[0], a["L3_gnn_W_coux"].T[:, None]], axis=1)),
        "L3_wh": lay(np.concatenate([gate[1], a["L3_gnn_W_couh"].T[:, None]], axis=1)),
        "L3_bx": lay(np.stack([*a["L3_gnn_b_ioux"].reshape(2, P), a["L3_gnn_b_coux"]], axis=1)),
        "L3_bh": lay(np.stack([*a["L3_gnn_b_iouh"].reshape(2, P), a["L3_gnn_b_couh"]], axis=1)),
        "L2_W": a["L2_gnn_W"],
        "L2_W_t": lay(a["L2_gnn_W"].T),
        "L2_a1": lay(np.broadcast_to(a["L2_gnn_a"][:P], wide)),
        "L2_a2": lay(np.broadcast_to(a["L2_gnn_a"][P:], wide)),
        "L2_gamma": lay(np.broadcast_to(a["L2_gnn_gamma"], wide)),
        "L2_beta": lay(np.broadcast_to(a["L2_gnn_beta"], wide)),
        "adj_groups": blocks,
        "adj_groups_t": blocks_t,
        "to_joint": to_joint,
        "L1_W1": lay(a["L1_gnn_W1"].reshape(G, P, HALVES, P).transpose(1, 0, 2, 3)),
        "L1_W2": lay(a["L1_gnn_W2"].reshape(G, HALVES, P, P).transpose(2, 0, 1, 3)),
        "L1_b1": lay(a["L1_gnn_b1"].reshape(G, HALVES, P).transpose(2, 0, 1)),
        "L1_b2": lay(a["L1_gnn_b2"].T),
        "L1_fusion_w": lay(np.broadcast_to(a["L1_gnn_fusion_w"], (P, G))),
        "x_nm": lay(x.transpose(1, 0, 2)),
        "x_fm": lay(x.transpose(2, 0, 1).reshape(P, B * P)),
        "adj_nm": lay(adj.transpose(1, 0, 2)),
        "mask": lay(a["nodemask"].T),
        "identity": np.eye(P, dtype=np.float32),
        "L0_weight": lay(a["L0_gnn_weight"].transpose(1, 0, 2)),
        "L0_w_ih": lay(a["L0_gnn_w_ih"].reshape(3, P, P).transpose(2, 0, 1)),
        "L0_w_hh": lay(a["L0_gnn_w_hh"].reshape(3, P, P).transpose(2, 0, 1)),
        "L0_b_ih": lay(a["L0_gnn_b_ih"].reshape(3, P).T),
        "L0_b_hh": lay(a["L0_gnn_b_hh"].reshape(3, P).T),
    }
    nc = bacc.Bacc("TRN2", target_bir_lowering=False, num_devices=1)
    dram = {name: nc.dram_tensor(f"in_{name}", v.shape, F32, kind="ExternalInput").ap() for name, v in arrays.items()}
    dram["inverse_t"] = nc.dram_tensor("inverse_t", (B, P), F32, kind="Internal").ap()
    dram["parts"] = nc.dram_tensor("parts_scratch", (P, 3, S * B), BF16, kind="Internal").ap()
    out = nc.dram_tensor("out_nm", (P, B, P), F32, kind="ExternalOutput").ap()
    graph_layers(nc, dram, out)
    result = run_bass_kernel_spmd(nc, [{f"in_{name}": v for name, v in arrays.items()}], core_ids=[0])
    return lay(result.results[0]["out_nm"].transpose(1, 0, 2))
```

```python
from contextlib import ExitStack

import concourse.bass as bass
from concourse import mybir

F32 = mybir.dt.float32
BF16 = mybir.dt.bfloat16
ALU = mybir.AluOpType
ACT = mybir.ActivationFunctionType
AX_X = mybir.AxisListType.X

P = 128
B = 64
LAYERS = 5
TILE = 4
COLS = TILE * P
PAIRS = B // (2 * TILE)
S = 8
SPAN = 32
BLOCK_PAIRS = [(k, target) for target in range(1, SPAN // S) for k in range(target)]
PAIRS_UP_TO = [sum(target <= p for _, target in BLOCK_PAIRS) for p in range(SPAN // S)]
PARTS = (0, 64, 96)
EPS = 1e-5
ALPHA = 0.2
NEG = -9e15


GROUPS = (list(range(25)), list(range(9)), [0, *range(9, 15)], [6, 7, 8, 12, 13, 14], [3, 4, 5, 9, 10, 11])
JOINTS = 25
ROWS = [n for nodes in GROUPS for n in nodes]
Q = len(ROWS)
FIRST = [sum(len(nodes) for nodes in GROUPS[:g]) for g in range(len(GROUPS))]
HALVES = 2
T1 = 8


def runs(nodes):
    found, at = [], 0
    while at < len(nodes):
        k = 1
        while at + k < len(nodes) and nodes[at + k] == nodes[at] + k:
            k += 1
        found.append((at, nodes[at], k))
        at += k
    return found


def alone(eng, met):
    eng.wait_ge(met, 1)


def gated_convolution(nc, dram, X, adj, consts, norm_t, root_diag, groups_ready, node_degree, degrees_ready):
    with nc.cleanup_on_exit(), ExitStack() as ctx:
        def sb(name, shape):
            return ctx.enter_context(nc.sbuf_tensor(name, shape, F32))

        def sem(name):
            return nc.alloc_semaphore(name)

        w_msg = sb("w_msg", [P, LAYERS, P])
        w_ih = sb("w_ih", [P, 3, P])
        w_hh = sb("w_hh", [P, 3, P])
        b_ih = sb("b_ih", [P, 3])
        b_hh = sb("b_hh", [P, 3])
        b_rz = sb("b_rz", [P, 2])
        mask = sb("mask", [P, B])
        h_in = sb("h_in", [P, 2, COLS])
        h = sb("h", [P, 2, COLS])
        h_last = sb("h_last", [P, 2, COLS])
        edges = sb("edges", [P, 2, COLS])
        m_sb = sb("m_sb", [P, 2, COLS])
        agg_sb = sb("agg_sb", [P, 2, COLS])
        r = sb("r", [P, 2, COLS])
        z = sb("z", [P, 2, COLS])
        n_pre = sb("n_pre", [P, 2, COLS])
        n = sb("n", [P, 2, COLS])
        zh = sb("zh", [P, 2, COLS])
        stats = sb("stats", [P, TILE, 6])
        mv = sb("mv", [P, 2, TILE, 2])
        rstd = sb("rstd", [P, 2, TILE])
        adj_groups = sb("adj_groups", [Q, B, Q])
        eye_q = sb("eye_q", [Q, Q])
        degree = sb("degree", [Q, 2 * TILE])
        root = sb("root", [Q, 2 * TILE])
        ps = ctx.enter_context(nc.psum_tensor("ps0", [P, 8, COLS], F32))
        R, Z, HN, SHARED = (0, 1), (2, 3), (4, 5), (6, 7)

        weights_in = sem("weights_in")
        small_in = sem("small_in")
        h_loaded = [sem(f"h_loaded{s}") for s in range(2)]
        nodes_loaded = sem("nodes_loaded")
        adj_loaded = sem("adj_loaded")
        edges_ready = sem("edges_ready")
        m_done = sem("m_done")
        m_copied = sem("m_copied")
        agg_done = sem("agg_done")
        agg_copied = sem("agg_copied")
        r_done = sem("r_done")
        z_done = sem("z_done")
        n_done = sem("n_done")
        r_ready = sem("r_ready")
        z_ready = sem("z_ready")
        n_pre_ready = sem("n_pre_ready")
        n_ready = sem("n_ready")
        chain = sem("gru_chain")
        zh_ready = sem("zh_ready")
        h_ready = sem("h_ready")
        turned = sem("turned")
        summed = sem("summed")
        moments_ready = sem("moments_ready")
        var_eps = sem("var_eps")
        rstd_ready = sem("rstd_ready")
        normed = sem("normed")
        const_ready = sem("const_ready")

        groups_in = sem("groups_in")
        eye_added = sem("eye_added")
        degree_step = sem("degree_step")
        guarded = sem("guarded")
        powered = sem("powered")
        root_ready = sem("root_ready")
        rows_scaled = sem("rows_scaled")

        def graphs(it):
            return bass.ds(it * 2 * TILE, 2 * TILE)

        STEPS = 2 * LAYERS

        def pairs(eng, body):
            body(0)
            with eng.Fori(1, PAIRS) as it:
                body(it)

        block = ctx.enter_context(nc.Block())

        @block.sync
        def _(sp):
            def pair_in(it):
                for s in range(2):
                    if it is not 0:
                        sp.wait_ge(h_ready, (it - 1) * STEPS + s + 1)
                    sp.dma_start(h_in[:, s, :], dram["x_fm"][:, bass.ds((it * 2 + s) * COLS, COLS)]).then_inc(h_loaded[s], 16)
                    if s == 0:
                        sp.dma_start(adj[:, bass.ds(it * 2 * TILE, 2 * TILE), :],
                                     dram["adj_nm"][:, bass.ds(it * 2 * TILE, 2 * TILE), :]).then_inc(adj_loaded, 16)
                if it is 0:
                    sp.dma_start(norm_t[:], dram["adj_groups_t"]).then_inc(groups_in, 16)
                    sp.dma_start(adj_groups[:], dram["adj_groups"]).then_inc(groups_in, 16)
                    sp.dma_start(eye_q[:], dram["identity"][0:Q, 0:Q]).then_inc(groups_in, 16)
                sp.dma_start(X[:, bass.ds(it * 2 * TILE, 2 * TILE), :],
                             dram["x_nm"][:, bass.ds(it * 2 * TILE, 2 * TILE), :]).then_inc(nodes_loaded, 16)

            sp.dma_start(w_msg[:], dram["L0_weight"]).then_inc(weights_in, 16)
            pairs(sp, pair_in)

        @block.scalar
        def _(act):
            act.dma_start(w_hh[:], dram["L0_w_hh"]).then_inc(weights_in, 16)
            act.dma_start(w_ih[:], dram["L0_w_ih"]).then_inc(weights_in, 16)
            act.dma_start(b_ih[:], dram["L0_b_ih"]).then_inc(small_in, 16)
            act.dma_start(b_hh[:], dram["L0_b_hh"]).then_inc(small_in, 16)
            act.dma_start(mask[:], dram["mask"]).then_inc(small_in, 16)
            act.dma_start(consts["identity"][:], dram["identity"]).then_inc(consts["identity_in"], 16)
            act.wait_ge(const_ready, 2)

            def pair(it):
                for u in range(STEPS):
                    s, turn = u % 2, it * STEPS + u
                    act.wait_ge(m_done, turn + 1)
                    nc.scalar.copy(m_sb[:, s, :], ps[:, SHARED[s], :]).then_inc(m_copied, 1)
                    act.wait_ge(r_done, turn + 1)
                    nc.scalar.activation(r[:, s, :], ps[:, R[s], :], ACT.Sigmoid, bias=b_rz[:, 0:1]).then_inc(r_ready, 1)
                    act.wait_ge(z_done, turn + 1)
                    nc.scalar.activation(z[:, s, :], ps[:, Z[s], :], ACT.Sigmoid, bias=b_rz[:, 1:2]).then_inc(z_ready, 1)
                    act.wait_ge(n_pre_ready, turn + 1)
                    nc.scalar.activation(n[:, s, :], n_pre[:, s, :], ACT.Tanh, bias=b_ih[:, 2:3]).then_inc(n_ready, 1)

            pairs(act, pair)

        @block.gpsimd
        def _(pool):
            nc.gpsimd.memset(consts["minus_half"][:], -0.5)
            nc.gpsimd.memset(consts["eps"][:], EPS).then_inc(const_ready, 1)

            def reciprocal_root(it, s):
                pool.wait_ge(moments_ready, it * 2 + s + 1)
                nc.gpsimd.tensor_tensor(mv[:, s, :, 1], mv[:, s, :, 1], consts["eps"][:, 0:TILE],
                                        ALU.add).then_inc(var_eps, 1)
                pool.wait_ge(var_eps, it * 2 + s + 1)
                nc.gpsimd.tensor_tensor(rstd[:, s, :], mv[:, s, :, 1], consts["minus_half"][:, 0:TILE],
                                        ALU.pow).then_inc(rstd_ready, 1)

            pool.wait_ge(const_ready, 1)

            def pair(it):
                for u in range(STEPS):
                    s, turn = u % 2, it * STEPS + u
                    if u < 2:
                        pool.wait_ge(h_loaded[s], (it + 1) * 16)
                    pool.wait_ge(z_ready, turn + 1)
                    src = h_in if u < 2 else h
                    nc.gpsimd.tensor_tensor(zh[:, s, :], z[:, s, :], src[:, s, :], ALU.mult).then_inc(zh_ready, 1)
                    if u == 3:
                        pool.wait_ge(groups_in, 48)
                        nc.gpsimd.tensor_tensor(norm_t[:, graphs(it), :], norm_t[:, graphs(it), :],
                                                eye_q[:].unsqueeze(1).broadcast_to([Q, 2 * TILE, Q]),
                                                ALU.add).then_inc(eye_added, 1)
                    if u == 5:
                        pool.wait_ge(guarded, it + 1)
                        nc.gpsimd.tensor_tensor(root[:], root[:], consts["minus_half"][0:Q, 0:2 * TILE],
                                                ALU.pow).then_inc(powered, 1)
                    if u == 7:
                        alone(pool, consts["identity_in"])
                        pool.wait_ge(eye_added, it + 1)
                        pool.wait_ge(root_ready, it + 1)
                        nc.gpsimd.tensor_tensor(norm_t[:, graphs(it), :], norm_t[:, graphs(it), :],
                                                root[:].unsqueeze(2).broadcast_to([Q, 2 * TILE, Q]),
                                                ALU.mult).then_inc(rows_scaled, 1)
                    if u == 8:
                        nc.gpsimd.tensor_tensor(root_diag[:, graphs(it), :],
                                                eye_q[:].unsqueeze(1).broadcast_to([Q, 2 * TILE, Q]),
                                                root[:].unsqueeze(2).broadcast_to([Q, 2 * TILE, Q]),
                                                ALU.mult).then_inc(groups_ready, 1)
                    if u == 1 and it is not 0:
                        reciprocal_root(it - 1, 0)
                    if u == 2 and it is not 0:
                        reciprocal_root(it - 1, 1)

            pairs(pool, pair)
            reciprocal_root(PAIRS - 1, 0)
            reciprocal_root(PAIRS - 1, 1)

        @block.vector
        def _(dve):
            dve.wait_ge(small_in, 48)
            nc.vector.tensor_tensor(b_rz[:], b_ih[:, 0:2], b_hh[:, 0:2], ALU.add).then_inc(const_ready, 1)

            def residual(it, s):
                dve.wait_ge(nodes_loaded, (it + 1) * 16)
                dve.wait_ge(turned, it * 2 + s + 1)
                for g in range(TILE):
                    b = it * 2 * TILE + s * TILE + g
                    one = nc.vector.scalar_tensor_tensor(
                        out=X[:, bass.ds(b, 1), :], in0=ps[:, HN[s], g * P:(g + 1) * P].unsqueeze(1), scalar=mask[:, bass.ds(b, 1)],
                        in1=X[:, bass.ds(b, 1), :], op0=ALU.mult, op1=ALU.add)
                one.then_inc(summed, 1)
                alone(dve, consts["identity_in"])
                dve.wait_ge(summed, it * 2 + s + 1)
                for g in range(TILE):
                    b = it * 2 * TILE + s * TILE + g
                    one = nc.vector.bn_stats(stats[:, g, :], X[:, bass.ds(b, 1), :])
                one.then_inc(chain, 1)
                alone(dve, consts["identity_in"])
                dve.wait_ge(chain, it * 2 + s + 1)
                for g in range(TILE):
                    one = nc.vector.bn_aggr(mv[:, s, g, :], stats[:, g, :])
                one.then_inc(moments_ready, 1)

            def normalise(it, s):
                dve.wait_ge(rstd_ready, it * 2 + s + 1)
                for g in range(TILE):
                    b = it * 2 * TILE + s * TILE + g
                    one = nc.vector.tensor_scalar(X[:, bass.ds(b, 1), :], X[:, bass.ds(b, 1), :], mv[:, s, g, 0:1],
                                                  rstd[:, s, g:g + 1], ALU.subtract, ALU.mult)
                one.then_inc(normed, 1)

            def pair(it):
                dve.wait_ge(adj_loaded, (it + 1) * 16)
                for u in range(STEPS):
                    s, turn = u % 2, it * STEPS + u
                    if u < 2:
                        if it is not 0:
                            dve.wait_ge(agg_done, it * STEPS - 1 + s)
                        nc.vector.tensor_scalar(edges[:, s, :].rearrange("p (b n) -> p b n", b=TILE),
                                                adj[:, bass.ds(it * 2 * TILE + s * TILE, TILE), :],
                                                0.0, None, ALU.not_equal).then_inc(edges_ready, 1)
                    if u < 2 and it is not 0:
                        residual(it - 1, s)
                    dve.wait_ge(agg_done, turn + 1)
                    nc.vector.tensor_copy(agg_sb[:, s, :], ps[:, SHARED[1 - s], :]).then_inc(agg_copied, 1)
                    dve.wait_ge(r_ready, turn + 1)
                    nc.vector.scalar_tensor_tensor(out=n_pre[:, s, :], in0=ps[:, HN[s], :], scalar=b_hh[:, 2:3],
                                                   in1=r[:, s, :], op0=ALU.add, op1=ALU.mult).then_inc(r_used, 1)
                    dve.wait_ge(r_used, turn + 1)
                    dve.wait_ge(n_done, turn + 1)
                    nc.vector.tensor_tensor(n_pre[:, s, :], n_pre[:, s, :], ps[:, SHARED[s], :],
                                            ALU.add).then_inc(n_pre_ready, 1)
                    dve.wait_ge(z_ready, turn + 1)
                    nc.vector.tensor_scalar(z1[:, s, :], z[:, s, :], -1.0, 1.0, ALU.mult, ALU.add).then_inc(z1_ready, 1)
                    dve.wait_ge(z1_ready, turn + 1)
                    dve.wait_ge(n_ready, turn + 1)
                    nc.vector.tensor_tensor(n[:, s, :], n[:, s, :], z1[:, s, :], ALU.mult).then_inc(n_scaled, 1)
                    dve.wait_ge(n_scaled, turn + 1)
                    dve.wait_ge(zh_ready, turn + 1)
                    dst = h_last if u >= STEPS - 2 else h
                    nc.vector.tensor_tensor(dst[:, s, :], n[:, s, :], zh[:, s, :], ALU.add).then_inc(h_ready, 1)
                    if u in (2, 3) and it is not 0:
                        normalise(it - 1, u % 2)
                    if u == 3:
                        dve.wait_ge(groups_in, 48)
                        if it is not 0:
                            dve.wait_ge(groups_ready, it)
                        nc.vector.tensor_reduce(degree[:], adj_groups[:, graphs(it), :], AX_X,
                                                ALU.add).then_inc(degree_step, 1)
                        dve.wait_ge(degree_step, 2 * it + 1)
                        nc.vector.tensor_scalar(degree[:], degree[:], 1.0, None, ALU.add).then_inc(degree_step, 1)
                        dve.wait_ge(degree_step, 2 * it + 2)
                        nc.vector.scalar_tensor_tensor(out=root[:], in0=degree[:], scalar=0.0, in1=degree[:],
                                                       op0=ALU.is_equal, op1=ALU.add).then_inc(guarded, 1)
                    if u == 4:
                        nc.vector.tensor_reduce(node_degree[:, graphs(it)], adj[:, graphs(it), :], AX_X,
                                                ALU.add).then_inc(degrees_ready, 1)
                    if u == 6:
                        dve.wait_ge(powered, it + 1)
                        nc.vector.scalar_tensor_tensor(out=root[:], in0=degree[:], scalar=0.0, in1=root[:],
                                                       op0=ALU.is_equal, op1=ALU.subtract).then_inc(root_ready, 1)

            z1 = sb("z1", [P, 2, COLS])
            r_used, z1_ready, n_scaled = sem("r_used"), sem("z1_ready"), sem("n_scaled")
            pairs(dve, pair)
            for s in range(2):
                residual(PAIRS - 1, s)
            for s in range(2):
                normalise(PAIRS - 1, s)

        @block.tensor
        def _(pe):
            pe.wait_ge(weights_in, 48)
            pe.wait_ge(consts["identity_in"], 16)

            def turn_back(it, s):
                pe.wait_ge(h_ready, it * STEPS + STEPS - 1 + s)
                for g in range(TILE):
                    one = nc.tensor.transpose(ps[:, HN[s], g * P:(g + 1) * P], h_last[:, s, g * P:(g + 1) * P],
                                              consts["identity"][:])
                one.then_inc(turned, 1)

            def pair(it):
                for u in range(STEPS):
                    s, layer, turn = u % 2, u // 2, it * STEPS + u
                    state = h_in if u < 2 else h
                    if u < 2:
                        pe.wait_ge(h_loaded[s], (it + 1) * 16)
                        if it is not 0:
                            pe.wait_ge(h_ready, turn - 1)
                    else:
                        pe.wait_ge(h_ready, turn - 1)
                    for g in range(TILE):
                        one = nc.tensor.matmul(ps[:, SHARED[s], g * P:(g + 1) * P], state[:, s, g * P:(g + 1) * P],
                                               w_msg[:, layer, :], start=True, stop=True)
                    one.then_inc(m_done, 1)
                    for bank, k in ((R, 0), (Z, 1)):
                        nc.tensor.matmul(ps[:, bank[s], :], w_hh[:, k, :], state[:, s, :], start=True, stop=False)
                    pe.wait_ge(m_copied, turn + 1)
                    if u < 2:
                        pe.wait_ge(edges_ready, it * 2 + s + 1)
                    for g in range(TILE):
                        one = nc.tensor.matmul(ps[:, SHARED[1 - s], g * P:(g + 1) * P], m_sb[:, s, g * P:(g + 1) * P],
                                               edges[:, s, g * P:(g + 1) * P], start=True, stop=True)
                    one.then_inc(agg_done, 1)
                    if u < 2 and it is not 0:
                        pe.wait_ge(summed, (it - 1) * 2 + s + 1)
                    nc.tensor.matmul(ps[:, HN[s], :], w_hh[:, 2, :], state[:, s, :], start=True, stop=True)
                    pe.wait_ge(agg_copied, turn + 1)
                    for bank, k, done in ((R, 0, r_done), (Z, 1, z_done)):
                        nc.tensor.matmul(ps[:, bank[s], :], w_ih[:, k, :], agg_sb[:, s, :], start=False,
                                         stop=True).then_inc(done, 1)
                    nc.tensor.matmul(ps[:, SHARED[s], :], w_ih[:, 2, :], agg_sb[:, s, :], start=True,
                                     stop=True).then_inc(n_done, 1)
                    if u == 0 and it is not 0:
                        turn_back(it - 1, 1)
                turn_back(it, 0)

            pairs(pe, pair)
            turn_back(PAIRS - 1, 1)


def group_convolution(nc, dram, X, consts, norm_t, root_diag, groups_ready, node_degree, inverse_t, inverse_stored):
    with ExitStack() as ctx:
        def sb(name, shape):
            return ctx.enter_context(nc.sbuf_tensor(name, shape, F32))

        def sem(name):
            return ctx.enter_context(nc.semaphore(name))

        G, SLOTS = len(GROUPS), 4
        ROUNDS = B // T1 // SLOTS
        mix = sb("mix", [JOINTS, B, Q])
        ones_q = sb("ones_q", [Q, Q])
        to_joint = sb("to_joint", [Q, JOINTS])
        w1 = sb("w1", [P, G, HALVES, P])
        w2 = sb("w2", [P, G, HALVES, P])
        b1 = sb("b1", [P, G, HALVES])
        b2 = sb("b2", [P, G])
        fusion = sb("fusion", [P, G])
        weight = sb("weight", [P, G])
        b2w = sb("b2w", [P, G])
        top = sb("top", [P, 1])
        total = sb("total", [P, 1])
        spare = sb("spare", [P, 1])
        x_in = sb("x_in", [JOINTS, SLOTS, T1, P])
        u_sb = sb("u_sb", [P, SLOTS, T1, Q])
        hid = sb("hid", [P, SLOTS, HALVES, T1, Q])
        sup = sb("sup", [P, SLOTS, T1, Q])
        sup_nm = sb("sup_nm", [Q, SLOTS, T1 * P])
        out_w = sb("out_w", [P, SLOTS, T1, Q])
        stats = sb("stats1", [P, SLOTS, T1, 6])
        mv = sb("mv1", [P, SLOTS, T1, 2])
        rstd = sb("rstd1", [P, SLOTS, T1])
        ps = ctx.enter_context(nc.psum_tensor("ps1", [P, 8, 512], F32))
        identity = consts["identity"]

        small_in = sem("small1_in")
        w_in = sem("w12_in")
        ones_set = sem("ones_set")
        root_done = sem("root_done")
        norm_ready = sem("norm_ready")
        mix_done = sem("mix_done")
        mix_ready = sem("mix_ready")
        mix_ready_act = sem("mix_ready_act")
        fuse_step = sem("fuse_step")
        fuse_exp = sem("fuse_exp")
        fuse_ready = sem("fuse_ready")
        x_ready = [sem(f"x_ready{s}") for s in range(SLOTS)]
        u_done = sem("u_done")
        u_ready = sem("u_ready")
        hid_done = sem("hid_done")
        hid0_ready = sem("hid0_ready")
        hid1_ready = sem("hid1_ready")
        sup_done = sem("sup_done")
        sup_ready = sem("sup_ready")
        sup_turned = sem("sup_turned")
        sup_nm0_ready = sem("sup_nm0_ready")
        sup_nm1_ready = sem("sup_nm1_ready")
        out_done = sem("out_done")
        out_ready = sem("out_ready")
        fused_step = sem("fused_step")
        fused_ready = sem("fused_ready")
        fused_turned = sem("fused_turned")
        summed = sem("summed1")
        stats_ready = sem("stats1_ready")
        moments_ready = sem("moments1_ready")
        var_eps = sem("var_eps1")
        rstd_ready = sem("rstd1_ready")
        normed = sem("normed1")

        inverse_step = sem("inverse_step")
        inverse_turned = sem("inverse_turned")
        guard = sb("guard", [P, B])
        turned = sb("inverse_turned_sb", [B, P])

        def bank(k):
            return ps[:, k, 0:T1 * Q].rearrange("p (b q) -> p b q", b=T1)

        def group(ap, g):
            return ap[:, :, FIRST[g]:FIRST[g] + len(GROUPS[g])]

        PLACES = [(FIRST[g] + at, node, k) for g in range(1, G) for at, node, k in runs(GROUPS[g])]

        def first(it, s):
            return it * SLOTS * T1 + s * T1

        block = ctx.enter_context(nc.Block())

        @block.sync
        def _(sp):
            sp.dma_start(w1[:], dram["L1_W1"]).then_inc(w_in, 16)
            sp.dma_start(w2[:], dram["L1_W2"]).then_inc(w_in, 16)
            sp.wait_ge(inverse_step, 5)
            sp.dma_start(inverse_t, turned[:]).then_inc(inverse_stored, 16)
            with sp.Fori(0, ROUNDS) as it:
                for s in range(SLOTS):
                    sp.wait_ge(u_done, it * SLOTS + s + 1)
                    sp.dma_start(x_in[:, s], X[0:JOINTS, bass.ds(first(it, s), T1), :]).then_inc(x_ready[s], 16)
            sp.wait_ge(inverse_stored, 16)

        @block.scalar
        def _(act):
            act.dma_start(to_joint[:], dram["to_joint"]).then_inc(small_in, 16)
            act.dma_start(b1[:], dram["L1_b1"]).then_inc(small_in, 16)
            act.dma_start(b2[:], dram["L1_b2"]).then_inc(small_in, 16)
            act.dma_start(fusion[:], dram["L1_fusion_w"]).then_inc(small_in, 16)
            act.wait_ge(fuse_step, 2)
            nc.scalar.activation(weight[:], fusion[:], ACT.Exp, accum_out=total[:]).then_inc(fuse_exp, 1)
            for k in range(1, 8, 2):
                act.wait_ge(mix_done, k + 1)
                nc.scalar.copy(mix[:, k * T1:(k + 1) * T1, :], bank(k)[0:JOINTS]).then_inc(mix_ready_act, 1)
            act.wait_ge(fuse_ready, 1)
            with act.Fori(0, ROUNDS) as it:
                for s in range(SLOTS):
                    act.wait_ge(u_done, it * SLOTS + s + 1 + SLOTS)
                    nc.scalar.copy(u_sb[:, s], bank(2 * s)).then_inc(u_ready, 1)
                for s in range(SLOTS):
                    act.wait_ge(hid_done, it * SLOTS + s + 1)
                    for g in range(G):
                        one = nc.scalar.activation(group(hid[:, s, 0], g), group(bank(2 * s), g), ACT.Relu,
                                                   bias=b1[:, g, 0:1])
                    one.then_inc(hid0_ready, 1)
                for s in range(SLOTS):
                    act.wait_ge(sup_done, it * SLOTS + s + 1)
                    nc.scalar.copy(sup[:, s], bank(2 * s)).then_inc(sup_ready, 1)
                for s in range(SLOTS):
                    act.wait_ge(sup_turned, it * SLOTS + s + 1)
                    nc.scalar.copy(sup_nm[:, s, 0:512], ps[0:Q, 2 * s, :]).then_inc(sup_nm0_ready, 1)
                for s in range(SLOTS):
                    act.wait_ge(out_done, it * SLOTS + s + 1)
                    for g in range(G):
                        one = nc.scalar.activation(group(out_w[:, s], g), group(bank(2 * s), g), ACT.Relu,
                                                   bias=b2w[:, g:g + 1], scale=weight[:, g:g + 1])
                    one.then_inc(out_ready, 1)

        @block.gpsimd
        def _(pool):
            nc.gpsimd.memset(ones_q[:], 1.0).then_inc(ones_set, 1)
            with pool.Fori(0, ROUNDS) as it:
                for s in range(SLOTS):
                    pool.wait_ge(out_ready, it * SLOTS + s + 1)
                    for n, (q, node, k) in enumerate(PLACES):
                        if n:
                            pool.wait_ge(fused_step, (it * SLOTS + s) * (len(PLACES) - 1) + n)
                        part = out_w[:, s, :, node:node + k]
                        one = nc.gpsimd.tensor_tensor(part, part, out_w[:, s, :, q:q + k], ALU.add)
                        one.then_inc(fused_step if n + 1 < len(PLACES) else fused_ready, 1)
                for s in range(SLOTS):
                    pool.wait_ge(moments_ready, it * SLOTS + s + 1)
                    nc.gpsimd.tensor_tensor(mv[:, s, :, 1], mv[:, s, :, 1], consts["eps"][:, 0:T1],
                                            ALU.add).then_inc(var_eps, 1)
                    pool.wait_ge(var_eps, it * SLOTS + s + 1)
                    nc.gpsimd.tensor_tensor(rstd[:, s, :], mv[:, s, :, 1], consts["minus_half"][:, 0:T1],
                                            ALU.pow).then_inc(rstd_ready, 1)

        @block.vector
        def _(dve):
            dve.sem_inc(summed, SLOTS)
            nc.vector.tensor_scalar(guard[:], node_degree[:], 0.0, None, ALU.not_equal).then_inc(inverse_step, 1)
            nc.vector.scalar_tensor_tensor(out=node_degree[:], in0=node_degree[:], scalar=0.0, in1=node_degree[:],
                                           op0=ALU.is_equal, op1=ALU.add).then_inc(inverse_step, 1)
            dve.wait_ge(inverse_step, 2)
            nc.vector.reciprocal(node_degree[:], node_degree[:]).then_inc(inverse_step, 1)
            dve.wait_ge(inverse_step, 3)
            nc.vector.tensor_tensor(node_degree[:], node_degree[:], guard[:], ALU.mult).then_inc(inverse_step, 1)
            dve.wait_ge(inverse_turned, 1)
            nc.vector.tensor_copy(turned[:], ps[0:B, 7, 0:P]).then_inc(inverse_step, 1)
            dve.wait_ge(small_in, 64)
            nc.vector.tensor_reduce(top[:], fusion[:], AX_X, ALU.max).then_inc(fuse_step, 1)
            dve.wait_ge(fuse_step, 1)
            nc.vector.tensor_scalar(fusion[:], fusion[:], top[:, 0:1], None, ALU.subtract).then_inc(fuse_step, 1)
            for k in range(8):
                dve.wait_ge(root_done, k + 1)
                part = norm_t[:, k * T1:(k + 1) * T1, :]
                nc.vector.tensor_tensor(part, part, bank(k)[0:Q], ALU.mult).then_inc(norm_ready, 1)
            dve.wait_ge(fuse_exp, 1)
            nc.vector.reciprocal(total[:], total[:]).then_inc(fuse_step, 1)
            dve.wait_ge(fuse_step, 3)
            nc.vector.tensor_scalar(weight[:], weight[:], total[:, 0:1], None, ALU.mult).then_inc(fuse_step, 1)
            dve.wait_ge(fuse_step, 4)
            nc.vector.tensor_tensor(b2w[:], b2[:], weight[:], ALU.mult).then_inc(fuse_ready, 1)
            for k in range(0, 8, 2):
                dve.wait_ge(mix_done, k + 1)
                nc.vector.tensor_copy(mix[:, k * T1:(k + 1) * T1, :], bank(k)[0:JOINTS]).then_inc(mix_ready, 1)

            with dve.Fori(0, ROUNDS) as it:
                for s in range(SLOTS):
                    dve.wait_ge(hid_done, it * SLOTS + s + 1)
                    for g in range(G):
                        one = nc.vector.tensor_scalar(group(hid[:, s, 1], g), group(bank(2 * s + 1), g),
                                                      b1[:, g, 1:2], 0.0, ALU.add, ALU.max)
                    one.then_inc(hid1_ready, 1)
                for s in range(SLOTS):
                    dve.wait_ge(sup_turned, it * SLOTS + s + 1)
                    nc.vector.tensor_copy(sup_nm[:, s, 512:1024], ps[0:Q, 2 * s + 1, :]).then_inc(sup_nm1_ready, 1)
                for s in range(SLOTS):
                    dve.wait_ge(fused_turned, it * SLOTS + s + 1)
                    for k in range(2):
                        part = X[0:JOINTS, bass.ds(first(it, s) + 4 * k, 4), :]
                        one = nc.vector.tensor_tensor(part, part, ps[0:JOINTS, 2 * s + k, :].rearrange(
                            "p (b d) -> p b d", b=4), ALU.add)
                    one.then_inc(summed, 1)
                    dve.wait_ge(summed, it * SLOTS + s + 1 + SLOTS)
                    nc.vector.memset(spare[:], 0.0)
                    for b in range(T1):
                        one = nc.vector.bn_stats(stats[:, s, b, :], X[:, bass.ds(first(it, s) + b, 1), :])
                    one.then_inc(stats_ready, 1)
                    alone(dve, consts["identity_in"])
                    dve.wait_ge(stats_ready, it * SLOTS + s + 1)
                    for b in range(T1):
                        one = nc.vector.bn_aggr(mv[:, s, b, :], stats[:, s, b, :])
                    one.then_inc(moments_ready, 1)
                for s in range(SLOTS):
                    dve.wait_ge(rstd_ready, it * SLOTS + s + 1)
                    for b in range(T1):
                        part = X[:, bass.ds(first(it, s) + b, 1), :]
                        one = nc.vector.tensor_scalar(part, part, mv[:, s, b, 0:1], rstd[:, s, b:b + 1],
                                                      ALU.subtract, ALU.mult)
                    one.then_inc(normed, 1)

        @block.tensor
        def _(pe):
            pe.sem_inc(u_done, SLOTS)
            pe.wait_ge(inverse_step, 4)
            nc.tensor.transpose(ps[0:B, 7, 0:P], node_degree[:], identity[:]).then_inc(inverse_turned, 1)
            pe.wait_ge(ones_set, 1)
            pe.wait_ge(groups_ready, B // T1)
            for k in range(8):
                if k == 7:
                    pe.wait_ge(inverse_step, 5)
                nc.tensor.matmul(bank(k)[0:Q], ones_q[:], root_diag[:, k * T1:(k + 1) * T1, :], start=True,
                                 stop=True).then_inc(root_done, 1)
            pe.wait_ge(small_in, 64)
            for k in range(8):
                pe.wait_ge(norm_ready, k + 1)
                nc.tensor.matmul(bank(k)[0:JOINTS], to_joint[:], norm_t[:, k * T1:(k + 1) * T1, :], start=True,
                                 stop=True).then_inc(mix_done, 1)
            pe.wait_ge(mix_ready, 4)
            pe.wait_ge(mix_ready_act, 4)
            pe.wait_ge(w_in, 32)
            with pe.Fori(0, ROUNDS) as it:
                for s in range(SLOTS):
                    pe.wait_ge(x_ready[s], it * 16 + 16)
                    pe.wait_ge(summed, it * SLOTS + s + 1)
                    for b in range(T1):
                        one = nc.tensor.matmul(bank(2 * s)[:, b, :], x_in[:, s, b, :],
                                               mix[:, bass.ds(first(it, s) + b, 1), :].squeeze(1), start=True, stop=True)
                    one.then_inc(u_done, 1)
                for s in range(SLOTS):
                    pe.wait_ge(u_ready, it * SLOTS + s + 1)
                    for half in range(HALVES):
                        for g in range(G):
                            one = nc.tensor.matmul(group(bank(2 * s + half), g), w1[:, g, half, :],
                                                   group(u_sb[:, s], g), start=True, stop=True)
                    one.then_inc(hid_done, 1)
                for s in range(SLOTS):
                    pe.wait_ge(hid0_ready, it * SLOTS + s + 1)
                    pe.wait_ge(hid1_ready, it * SLOTS + s + 1)
                    for g in range(G):
                        for half in range(HALVES):
                            one = nc.tensor.matmul(group(bank(2 * s), g), w2[:, g, half, :],
                                                   group(hid[:, s, half], g), start=half == 0, stop=half == 1)
                    one.then_inc(sup_done, 1)
                for s in range(SLOTS):
                    alone(pe, consts["identity_in"])
                    pe.wait_ge(sup_ready, it * SLOTS + s + 1)
                    for b in range(T1):
                        one = nc.tensor.transpose(ps[0:Q, 2 * s + b // 4, (b % 4) * P:(b % 4 + 1) * P],
                                                  sup[:, s, b, :], identity[:])
                    one.then_inc(sup_turned, 1)
                for s in range(SLOTS):
                    pe.wait_ge(sup_nm0_ready, it * SLOTS + s + 1)
                    pe.wait_ge(sup_nm1_ready, it * SLOTS + s + 1)
                    for b in range(T1):
                        one = nc.tensor.matmul(bank(2 * s)[:, b, :], sup_nm[:, s, b * P:(b + 1) * P],
                                               norm_t[:, bass.ds(first(it, s) + b, 1), :].squeeze(1), start=True, stop=True)
                    one.then_inc(out_done, 1)
                for s in range(SLOTS):
                    alone(pe, consts["identity_in"])
                    pe.wait_ge(fused_ready, it * SLOTS + s + 1)
                    for b in range(T1):
                        one = nc.tensor.transpose(ps[0:JOINTS, 2 * s + b // 4, (b % 4) * P:(b % 4 + 1) * P],
                                                  out_w[:, s, b, 0:JOINTS], identity[:])
                    one.then_inc(fused_turned, 1)


def graph_attention(nc, dram, X, adj, hn, consts):
    with ExitStack() as ctx:
        def sb(name, shape):
            return ctx.enter_context(nc.sbuf_tensor(name, shape, F32))

        def sem(name):
            return ctx.enter_context(nc.semaphore(name))

        SLOTS = 4
        ROUNDS = B // TILE // SLOTS
        w = sb("w_att", [P, P])
        w_t = sb("w_att_t", [P, P])
        a1 = sb("a1", [P, P])
        a2 = sb("a2", [P, P])
        wa1 = sb("wa1", [P, P])
        wa2 = sb("wa2", [P, P])
        gamma = sb("gamma", [P, P])
        beta = sb("beta", [P, P])
        x_in = sb("x2_in", [P, SLOTS, COLS])
        bars = sb("bars", [P, SLOTS, COLS])
        xt = sb("xt", [P, SLOTS, COLS])
        wh = sb("wh", [P, SLOTS, COLS])
        score = sb("score", [P, SLOTS, COLS])
        att = sb("att", [P, SLOTS, COLS])
        att_t = xt
        top = sb("top2", [P, SLOTS, TILE])
        total = sb("total2", [P, SLOTS, TILE])
        scale = sb("scale2", [P, SLOTS, TILE])
        stats = sb("stats2", [P, SLOTS, TILE, 6])
        mv = sb("mv2", [P, SLOTS, TILE, 2])
        ps = ctx.enter_context(nc.psum_tensor("ps2", [P, 8, COLS], F32))
        identity = consts["identity"]

        w_in = sem("w_att_in")
        wa_done = sem("wa_done")
        wa_ready = sem("wa_ready")
        x_loaded = [sem(f"x2_loaded{s}") for s in range(SLOTS)]
        x_turned = sem("x2_turned")
        xt_ready = sem("xt_ready")
        wh_done = sem("wh_done")
        wh_ready = sem("wh_ready")
        score_done = sem("score_done")
        score_copied = sem("score_copied")
        barred = sem("barred")
        leaked = sem("leaked")
        masked = sem("masked")
        top_found = sem("top_found")
        top_ready = sem("top_ready")
        exp_ready = sem("exp_ready")
        att_turned = sem("att_turned")
        att_t_ready = sem("att_t_ready")
        head_done = sem("head_done")
        head_ready = sem("head_ready")
        stats_ready = sem("stats2_ready")
        moments_ready = sem("moments2_ready")
        total_inverted = sem("total_inverted")
        scale_step = sem("scale_step")
        scale_ready = sem("scale_ready")
        head_normed = sem("head_normed")
        gained = sem("gained")
        hn_ready = sem("hn_ready")

        def graph(ap, s, g):
            return ap[:, s, g * P:(g + 1) * P]

        def graphs(ap):
            return ap.rearrange("p (b d) -> p b d", b=TILE)

        block = ctx.enter_context(nc.Block())

        @block.sync
        def _(sp):
            with sp.Fori(0, ROUNDS) as it:
                for s in range(SLOTS):
                    tile = bass.ds((it * SLOTS + s) * TILE, TILE)
                    sp.wait_ge(x_turned, it * SLOTS + s + 1)
                    sp.dma_start(graphs(x_in[:, s]), X[:, tile, :]).then_inc(x_loaded[s], 16)

        @block.scalar
        def _(act):
            for k, dst in enumerate((w, w_t, a1, a2, gamma, beta)):
                act.dma_start(dst[:], dram[("L2_W", "L2_W_t", "L2_a1", "L2_a2", "L2_gamma", "L2_beta")[k]]).then_inc(w_in, 16)
            act.wait_ge(wa_done, 1)
            nc.scalar.copy(wa1[:], ps[:, 0, 0:P])
            nc.scalar.copy(wa2[:], ps[:, 0, P:2 * P]).then_inc(wa_ready, 1)
            with act.Fori(0, ROUNDS) as it:
                def turn(s):
                    return it * SLOTS + s + 1
                for s in range(SLOTS):
                    act.wait_ge(x_turned, it * SLOTS + s + 1 + SLOTS)
                    nc.scalar.copy(xt[:, s], ps[:, 2 * s, :]).then_inc(xt_ready, 1)
                for s in range(SLOTS):
                    act.wait_ge(score_done, turn(s))
                    nc.scalar.copy(score[:, s], ps[:, 2 * s, :]).then_inc(score_copied, 1)
                for s in range(SLOTS):
                    act.wait_ge(top_ready, turn(s))
                    act.wait_ge(hn_ready, turn(s))
                    for g in range(TILE):
                        one = nc.scalar.activation(graph(att, s, g), graph(score, s, g), ACT.Exp,
                                                   bias=top[:, s, g:g + 1], accum_out=total[:, s, g:g + 1])
                    one.then_inc(exp_ready, 1)
                for s in range(SLOTS):
                    act.wait_ge(att_turned, turn(s))
                    nc.scalar.copy(att_t[:, s], ps[:, 2 * s, :]).then_inc(att_t_ready, 1)
                for s in range(SLOTS):
                    act.wait_ge(head_done, turn(s))
                    nc.scalar.copy(att[:, s], ps[:, 2 * s + 1, :]).then_inc(head_ready, 1)

        @block.gpsimd
        def _(pool):
            pool.sem_inc(hn_ready, SLOTS)
            with pool.Fori(0, ROUNDS) as it:
                def turn(s):
                    return it * SLOTS + s + 1
                for s in range(SLOTS):
                    pool.wait_ge(total_inverted, turn(s))
                    steps = ((scale, total, total, ALU.mult), (scale, scale, None, ALU.mult),
                             (scale, scale, "eps", ALU.add), (scale, scale, "minus_half", ALU.pow),
                             (scale, scale, total, ALU.mult))
                    pool.wait_ge(moments_ready, turn(s))
                    for k, (dst, one, other, op) in enumerate(steps):
                        if k:
                            pool.wait_ge(scale_step, (it * SLOTS + s) * 4 + k)
                        if other is None:
                            second = mv[:, s, :, 1]
                        elif isinstance(other, str):
                            second = consts[other][:, 0:TILE]
                        else:
                            second = other[:, s]
                        nc.gpsimd.tensor_tensor(dst[:, s], one[:, s], second, op).then_inc(
                            scale_step if k < 4 else scale_ready, 1)
                for s in range(SLOTS):
                    pool.wait_ge(head_normed, turn(s))
                    nc.gpsimd.tensor_tensor(graphs(att[:, s]), graphs(att[:, s]),
                                            gamma[:].unsqueeze(1).broadcast_to([P, TILE, P]), ALU.mult).then_inc(gained, 1)
                    alone(pool, consts["identity_in"])
                    pool.wait_ge(gained, turn(s))
                    nc.gpsimd.tensor_tensor(hn[:, bass.ds((it * SLOTS + s) * TILE, TILE), :], graphs(att[:, s]),
                                            beta[:].unsqueeze(1).broadcast_to([P, TILE, P]), ALU.add).then_inc(hn_ready, 1)

        @block.vector
        def _(dve):
            with dve.Fori(0, ROUNDS) as it:
                def turn(s):
                    return it * SLOTS + s + 1
                for s in range(SLOTS):
                    nc.vector.tensor_scalar(graphs(bars[:, s]), adj[:, bass.ds((it * SLOTS + s) * TILE, TILE), :],
                                            0.0, NEG, ALU.is_le, ALU.mult).then_inc(barred, 1)
                for s in range(SLOTS):
                    dve.wait_ge(wh_done, turn(s))
                    nc.vector.tensor_copy(wh[:, s], ps[:, 2 * s + 1, :]).then_inc(wh_ready, 1)
                for s in range(SLOTS):
                    dve.wait_ge(score_copied, turn(s))
                    nc.vector.scalar_tensor_tensor(out=score[:, s], in0=score[:, s], scalar=ALPHA,
                                                   in1=ps[:, 2 * s, :], op0=ALU.mult, op1=ALU.max).then_inc(leaked, 1)
                    dve.wait_ge(leaked, turn(s))
                    dve.wait_ge(barred, turn(s))
                    nc.vector.tensor_tensor(score[:, s], score[:, s], bars[:, s], ALU.add).then_inc(masked, 1)
                    dve.wait_ge(masked, turn(s))
                    nc.vector.tensor_reduce(top[:, s], graphs(score[:, s]), AX_X, ALU.max).then_inc(top_found, 1)
                    dve.wait_ge(top_found, turn(s))
                    nc.vector.tensor_scalar(top[:, s], top[:, s], -1.0, None, ALU.mult).then_inc(top_ready, 1)
                for s in range(SLOTS):
                    dve.wait_ge(exp_ready, turn(s))
                    nc.vector.reciprocal(total[:, s], total[:, s]).then_inc(total_inverted, 1)
                for s in range(SLOTS):
                    dve.wait_ge(head_ready, turn(s))
                    for g in range(TILE):
                        one = nc.vector.bn_stats(stats[:, s, g, :], graph(att, s, g))
                    one.then_inc(stats_ready, 1)
                    alone(dve, consts["identity_in"])
                    dve.wait_ge(stats_ready, turn(s))
                    for g in range(TILE):
                        one = nc.vector.bn_aggr(mv[:, s, g, :], stats[:, s, g, :])
                    one.then_inc(moments_ready, 1)
                for s in range(SLOTS):
                    dve.wait_ge(scale_ready, turn(s))
                    for g in range(TILE):
                        one = nc.vector.tensor_scalar(graph(att, s, g), graph(att, s, g), mv[:, s, g, 0:1],
                                                      scale[:, s, g:g + 1], ALU.subtract, ALU.mult)
                    one.then_inc(head_normed, 1)

        @block.tensor
        def _(pe):
            pe.sem_inc(x_turned, SLOTS)
            pe.wait_ge(w_in, 96)
            nc.tensor.matmul(ps[:, 0, 0:P], w_t[:], a1[:], start=True, stop=True)
            nc.tensor.matmul(ps[:, 0, P:2 * P], w_t[:], a2[:], start=True, stop=True).then_inc(wa_done, 1)
            pe.wait_ge(wa_ready, 1)
            with pe.Fori(0, ROUNDS) as it:
                def turn(s):
                    return it * SLOTS + s + 1
                for s in range(SLOTS):
                    pe.wait_ge(x_loaded[s], it * 16 + 16)
                    for g in range(TILE):
                        one = nc.tensor.transpose(ps[:, 2 * s, g * P:(g + 1) * P], graph(x_in, s, g), identity[:])
                    one.then_inc(x_turned, 1)
                for s in range(SLOTS):
                    pe.wait_ge(xt_ready, turn(s))
                    for g in range(TILE):
                        one = nc.tensor.matmul(ps[:, 2 * s + 1, g * P:(g + 1) * P], graph(xt, s, g), w[:],
                                               start=True, stop=True)
                    one.then_inc(wh_done, 1)
                    nc.tensor.matmul(ps[:, 2 * s, :], wa2[:], xt[:, s], start=True, stop=False)
                    for g in range(TILE):
                        one = nc.tensor.matmul(ps[:, 2 * s, g * P:(g + 1) * P], graph(xt, s, g), wa1[:],
                                               start=False, stop=g == TILE - 1)
                    one.then_inc(score_done, 1)
                for s in range(SLOTS):
                    pe.wait_ge(exp_ready, turn(s))
                    for g in range(TILE):
                        one = nc.tensor.transpose(ps[:, 2 * s, g * P:(g + 1) * P], graph(att, s, g), identity[:])
                    one.then_inc(att_turned, 1)
                for s in range(SLOTS):
                    pe.wait_ge(att_t_ready, turn(s))
                    pe.wait_ge(wh_ready, turn(s))
                    for g in range(TILE):
                        one = nc.tensor.matmul(ps[:, 2 * s + 1, g * P:(g + 1) * P], graph(att_t, s, g), graph(wh, s, g),
                                               start=True, stop=True)
                    one.then_inc(head_done, 1)


def finish_attention(nc, dram, X, adj, hn, x_fm, consts, inverse_t):
    with ExitStack() as ctx:
        def sb(name, shape):
            return ctx.enter_context(nc.sbuf_tensor(name, shape, F32))

        def sem(name):
            return ctx.enter_context(nc.semaphore(name))

        CHUNK = 8
        stats = sb("stats3", [P, 2, CHUNK, 6])
        mv = sb("mv3", [P, 2, CHUNK, 2])
        rstd = sb("rstd3", [P, 2, CHUNK])
        staged = sb("staged", [P, 2, CHUNK, P])
        inverse = sb("inverse", [P, 2, CHUNK, P])
        not_next = sb("not_next", [P, P])
        ps = ctx.enter_context(nc.psum_tensor("ps3", [P, 4, 512], F32))

        gelu_ready = sem("gelu_ready")
        added = sem("added2")
        stats_ready = sem("stats3_ready")
        moments_ready = sem("moments3_ready")
        var_eps = sem("var_eps3")
        rstd_ready = sem("rstd3_ready")
        normed = sem("normed3")
        staged_in = [sem(f"staged_in{s}") for s in range(2)]
        kept = sem("kept")
        turned = sem("turned3")
        laid = sem("laid3")
        inverse_in = [sem(f"inverse_in{s}") for s in range(2)]
        divided = sem("divided")
        not_next_in, cut = sem("not_next_in"), sem("cut")
        ROUNDS = B // CHUNK // 2

        block = ctx.enter_context(nc.Block())

        @block.sync
        def _(sp):
            sp.dma_start(not_next[:], dram["not_next"]).then_inc(not_next_in, 16)
            with sp.Fori(0, ROUNDS) as it:
                for s in range(2):
                    part = bass.ds((it * 2 + s) * CHUNK, CHUNK)
                    alone(sp, consts["identity_in"])
                    sp.wait_ge(divided, it * 2 + s + 1)
                    sp.dma_start(inverse[:, s], inverse_t[part, :].unsqueeze(0).broadcast_to([P, CHUNK, P])).then_inc(
                        inverse_in[s], 16)
                for s in range(2):
                    part = bass.ds((it * 2 + s) * CHUNK, CHUNK)
                    alone(sp, consts["identity_in"])
                    sp.wait_ge(normed, it * 2 + s + 1)
                    alone(sp, consts["identity_in"])
                    sp.wait_ge(turned, it * 2 + s + 1)
                    sp.dma_start(staged[:, s], X[:, part, :]).then_inc(staged_in[s], 16)
                    sp.dma_start(hn[:, part, :], X[:, part, :]).then_inc(kept, 16)
            sp.wait_ge(kept, 16 * 2 * ROUNDS)

        @block.scalar
        def _(act):
            act.sem_inc(laid, 4)
            with act.Fori(0, ROUNDS) as it:
                for s in range(2):
                    part = hn[:, bass.ds((it * 2 + s) * CHUNK, CHUNK), :]
                    nc.scalar.activation(part, part, ACT.Gelu).then_inc(gelu_ready, 1)
                for s in range(2):
                    for k in range(2):
                        alone(act, consts["identity_in"])
                        act.wait_ge(turned, it * 2 + s + 3)
                        nc.scalar.copy(x_fm[:, :, bass.ds((it * 2 + s) * CHUNK + k * 4, 4)],
                                       ps[:, 2 * s + k, :].rearrange("p (b n) -> p n b", b=4)).then_inc(laid, 1)

        @block.gpsimd
        def _(pool):
            pool.sem_inc(divided, 2)
            with pool.Fori(0, ROUNDS) as it:
                for s in range(2):
                    pool.wait_ge(moments_ready, it * 2 + s + 1)
                    nc.gpsimd.tensor_tensor(mv[:, s, :, 1], mv[:, s, :, 1], consts["eps"][:, 0:CHUNK],
                                            ALU.add).then_inc(var_eps, 1)
                    pool.wait_ge(var_eps, it * 2 + s + 1)
                    nc.gpsimd.tensor_tensor(rstd[:, s, :], mv[:, s, :, 1], consts["minus_half"][:, 0:CHUNK],
                                            ALU.pow).then_inc(rstd_ready, 1)
                for s in range(2):
                    part = adj[:, bass.ds((it * 2 + s) * CHUNK, CHUNK), :]
                    alone(pool, consts["identity_in"])
                    pool.wait_ge(inverse_in[s], it * 16 + 16)
                    alone(pool, consts["identity_in"])
                    pool.wait_ge(cut, it * 2 + s + 1)
                    nc.gpsimd.tensor_tensor(part, part, inverse[:, s], ALU.mult).then_inc(divided, 1)

        @block.vector
        def _(dve):
            dve.wait_ge(not_next_in, 16)
            with dve.Fori(0, ROUNDS) as it:
                for s in range(2):
                    part = adj[:, bass.ds((it * 2 + s) * CHUNK, CHUNK), :]
                    nc.vector.tensor_tensor(part, part, not_next[:].unsqueeze(1).broadcast_to([P, CHUNK, P]),
                                            ALU.mult).then_inc(cut, 1)
                for s in range(2):
                    at = (it * 2 + s) * CHUNK
                    dve.wait_ge(gelu_ready, it * 2 + s + 1)
                    part = X[:, bass.ds(at, CHUNK), :]
                    nc.vector.tensor_tensor(part, part, hn[:, bass.ds(at, CHUNK), :], ALU.add).then_inc(added, 1)
                    alone(dve, consts["identity_in"])
                    dve.wait_ge(added, it * 2 + s + 1)
                    for b in range(CHUNK):
                        one = nc.vector.bn_stats(stats[:, s, b, :], X[:, bass.ds(at + b, 1), :])
                    one.then_inc(stats_ready, 1)
                    alone(dve, consts["identity_in"])
                    dve.wait_ge(stats_ready, it * 2 + s + 1)
                    for b in range(CHUNK):
                        one = nc.vector.bn_aggr(mv[:, s, b, :], stats[:, s, b, :])
                    one.then_inc(moments_ready, 1)
                for s in range(2):
                    dve.wait_ge(rstd_ready, it * 2 + s + 1)
                    for b in range(CHUNK):
                        part = X[:, bass.ds((it * 2 + s) * CHUNK + b, 1), :]
                        one = nc.vector.tensor_scalar(part, part, mv[:, s, b, 0:1], rstd[:, s, b:b + 1],
                                                      ALU.subtract, ALU.mult)
                    one.then_inc(normed, 1)

        @block.tensor
        def _(pe):
            pe.sem_inc(turned, 2)
            with pe.Fori(0, ROUNDS) as it:
                for s in range(2):
                    pe.wait_ge(staged_in[s], it * 16 + 16)
                    pe.wait_ge(laid, it * 4 + 2 * s + 1)
                    for b in range(CHUNK):
                        one = nc.tensor.transpose(ps[:, 2 * s + b // 4, (b % 4) * P:(b % 4 + 1) * P],
                                                  staged[:, s, b, :], consts["identity"][:])
                    one.then_inc(turned, 1)


def gated_scan(nc, dram, X, adj, x_fm, consts, inverse_t, inverse):
    with ExitStack() as ctx:
        def sb(name, shape, dt=F32):
            return ctx.enter_context(nc.sbuf_tensor(name, shape, dt))

        def sem(name):
            return ctx.enter_context(nc.semaphore(name))

        BLOCKS = SPAN // S
        GB = P // S
        NG = B // GB
        wx = sb("wx", [P, 3, P])
        wh = sb("wh3", [P, 3, P])
        bias_x = sb("bias_x", [P, 3])
        bias_h = sb("bias_h", [P, 3])
        bias = sb("bias3", [P, 3])
        parts = sb("parts", [PARTS[-1] + S, P // S, S, B], BF16)
        select_f = sb("select_f", [PARTS[-1] + S, S, P])
        select = sb("select", [PARTS[-1] + S, S, P], BF16)
        same_graph = sb("same_graph", [P, GB, S])
        between = sb("between", [P, P // SPAN, len(BLOCK_PAIRS), NG, S])
        step_mat = sb("step_mat", [P, 2, NG, GB, S])
        with ExitStack() as preparing:
            spread_coefficients(nc, dram, consts, preparing, inverse_t, inverse, parts, between)

        sums = sb("sums", [P, SPAN, B])
        delta = sb("delta", [P, S, B])
        h_new = sb("h_new", [P, S, B])
        delta_nm = sb("delta_nm", [P, BLOCKS - 1, NG, P])
        h_nm = sb("h_nm", [P, NG, P])
        r = sb("r3", [P, B])
        z = sb("z3", [P, 2, B])
        hc = sb("hc", [P, 2, B])
        x_par = sb("x_par", [P, 2, B])
        xr = sb("xr", [P, B])
        near_x = sb("near_x", [P, B])
        near_z = sb("near_z", [P, B])
        z_near_x = sb("z_near_x", [P, B])
        early = sb("early", [P, B])
        late = sb("late", [P, B])
        zx = sb("zx", [P, 2, B])
        kept = sb("kept3", [P, 2, B])
        fresh = sb("fresh", [P, B])
        far = sb("far", [P, S, B])
        ps = ctx.enter_context(nc.psum_tensor("ps4", [P, 8, 512], F32))
        R, Z, C, CORR, COEF = (0, 1), (2, 3), 4, 5, (6, 7)
        TURN_H, TURN_DELTA = COEF
        BASE = (C, CORR, *COEF)
        identity = consts["identity"]

        w_in, small_in, select_in = sem("w3_in"), sem("small3_in"), sem("select_in")
        bias_ready, select_ready = sem("bias_ready"), sem("select_ready")
        step_ready, pair_done = sem("step_mat_ready"), sem("pair_done")
        base_done, sums_ready = sem("base_done"), sem("sums_ready")
        r_done, z_done, c_done, coef_done = sem("r3_done"), sem("z3_done"), sem("c3_done"), sem("coef_done")
        r_ready, z_ready, hc_ready = sem("r3_ready"), sem("z3_ready"), sem("hc_ready")
        x_ready, xr_ready = sem("x_par_ready"), sem("xr_ready")
        near_x_ready, near_z_ready, z_near_x_ready = sem("near_x_ready"), sem("near_z_ready"), sem("z_near_x_ready")
        early_ready, late_ready = sem("early_ready"), sem("late_ready")
        fresh_ready, delta_ready = sem("fresh_ready"), sem("delta_ready")
        far_ready, near_added, far_added = sem("far_ready"), sem("near_added"), sem("far_added")
        zx_ready, kept_ready, h_ready = sem("zx_ready"), sem("kept_ready"), sem("h3_ready")
        delta_turned, delta_nm_ready = sem("delta_turned"), sem("delta_nm_ready")
        h_turned, h_nm_ready, rows_in = sem("h_turned"), sem("h_nm_ready"), sem("rows_in")

        def old(block, s, nodes=1):
            part = x_fm[:, bass.ds(block * S + s, nodes), :]
            return part.squeeze(1) if nodes == 1 else part

        block_of_engines = ctx.enter_context(nc.Block())

        @block_of_engines.sync
        def _(sp):
            sp.sem_inc(rows_in, 16)
            sp.dma_start(wx[:], dram["L3_wx"]).then_inc(w_in, 16)
            sp.dma_start(wh[:], dram["L3_wh"]).then_inc(w_in, 16)
            sp.dma_start(select_f[:], dram["select"]).then_inc(select_in, 16)
            for block in range(P // S):
                sp.wait_ge(h_nm_ready, block + 1)
                sp.wait_ge(base_done, (block // BLOCKS + 1) * NG)
                sp.dma_start(X[block * S:(block + 1) * S].rearrange("n (b g) d -> n b (g d)", g=NG),
                             h_nm[:].rearrange("p g d -> p (g d)")).then_inc(rows_in, 16)
            sp.wait_ge(rows_in, 16 * (P // S) + 16)

        @block_of_engines.scalar
        def _(act):
            act.dma_start(bias_x[:], dram["L3_bx"]).then_inc(small_in, 16)
            act.dma_start(bias_h[:], dram["L3_bh"]).then_inc(small_in, 16)
            act.dma_start(same_graph[:], dram["same_graph"]).then_inc(small_in, 16)
            act.wait_ge(select_in, 16)
            nc.scalar.copy(select[:], select_f[:]).then_inc(select_ready, 1)
            act.wait_ge(bias_ready, 1)
            with act.Fori(0, P // SPAN) as span:
                for p in range(BLOCKS):
                    block = span * BLOCKS + p
                    for s in range(S):
                        turn = block * S + s + 1
                        at = slice(s * B, (s + 1) * B)
                        act.wait_ge(r_done, turn)
                        nc.scalar.activation(r[:], ps[:, R[p % 2], at], ACT.Sigmoid, bias=bias[:, 0:1]).then_inc(r_ready, 1)
                        act.wait_ge(z_done, turn)
                        nc.scalar.activation(z[:, s % 2], ps[:, Z[p % 2], at], ACT.Sigmoid,
                                             bias=bias[:, 1:2]).then_inc(z_ready, 1)
                        act.wait_ge(c_done, turn)
                        nc.scalar.activation(hc[:, s % 2], ps[:, C, 0:B], ACT.Tanh, bias=bias[:, 2:3]).then_inc(hc_ready, 1)
                    act.wait_ge(h_turned, block + 1)
                    act.wait_ge(rows_in, block * 16 + 16)
                    nc.scalar.copy(h_nm[:].rearrange("p g d -> p (g d)"), ps[:, TURN_H, :]).then_inc(h_nm_ready, 1)

        @block_of_engines.gpsimd
        def _(pool):
            pool.wait_ge(small_in, 48)

            def build(span, pair):
                alone(pool, consts["identity_in"])
                pool.wait_ge(pair_done, span * len(BLOCK_PAIRS) + pair + 1)
                nc.gpsimd.tensor_tensor(
                    step_mat[:, pair % 2],
                    between[:, bass.ds(span, 1), pair].squeeze(1).unsqueeze(2).broadcast_to([P, NG, GB, S]),
                    same_graph[:].unsqueeze(1).broadcast_to([P, NG, GB, S]), ALU.mult).then_inc(step_ready, 1)

            when = {(0, 2): 0, (0, 5): 1, (1, 2): 2, (1, 6): 3, (2, 1): 4, (2, 5): 5}
            with pool.Fori(0, P // SPAN) as span:
                for p in range(BLOCKS):
                    block = span * BLOCKS + p
                    for s in range(S):
                        turn = block * S + s + 1
                        if (p, s) in when:
                            build(span, when[p, s])
                        if s and s + 1 < S:
                            row = p * S + s + 1
                            pool.wait_ge(far_ready, block * (S - 2) + s)
                            pool.wait_ge(sums_ready, block + 1)
                            nc.gpsimd.tensor_tensor(sums[:, row], sums[:, row], far[:, s + 1], ALU.add).then_inc(near_added, 1)
                        pool.wait_ge(x_ready, turn)
                        pool.wait_ge(z_ready, turn)
                        nc.gpsimd.tensor_tensor(zx[:, s % 2], z[:, s % 2], x_par[:, s % 2], ALU.mult).then_inc(zx_ready, 1)
                        alone(pool, consts["identity_in"])
                        pool.wait_ge(zx_ready, turn)
                        nc.gpsimd.tensor_tensor(kept[:, s % 2], zx[:, s % 2], old(block, s), ALU.subtract).then_inc(kept_ready, 1)
                        if s and s + 2 < S:
                            rows = slice(p * S + s + 2, (p + 1) * S)
                            nc.gpsimd.tensor_tensor(sums[:, rows], sums[:, rows], far[:, s + 2:S], ALU.add).then_inc(far_added, 1)
                        if s == S - 1:
                            alone(pool, consts["identity_in"])
                            pool.wait_ge(delta_ready, turn - 1)
                            nc.gpsimd.tensor_tensor(h_new[:, 0:s], delta[:, 0:s], old(block, 0, s), ALU.add).then_inc(h_ready, 1)
                            alone(pool, consts["identity_in"])
                            pool.wait_ge(delta_ready, turn)
                            nc.gpsimd.tensor_tensor(h_new[:, s], delta[:, s], old(block, s), ALU.add).then_inc(h_ready, 1)

        @block_of_engines.vector
        def _(dve):
            dve.wait_ge(small_in, 48)
            nc.vector.tensor_tensor(bias[:], bias_x[:], bias_h[:], ALU.add).then_inc(bias_ready, 1)

            def coefficients(s):
                return ps[:, COEF[s % 2], :].rearrange("p (i b) -> p i b", b=B)

            def after_tanh(block, s):
                turn = block * S + s + 1
                dve.wait_ge(hc_ready, turn)
                if s + 1 < S:
                    step = block * (S - 1) + s + 1
                    dve.wait_ge(near_z_ready, step)
                    nc.vector.tensor_tensor(late[:], near_z[:], hc[:, s % 2], ALU.mult).then_inc(late_ready, 1)
                nc.vector.scalar_tensor_tensor(out=fresh[:], in0=z[:, s % 2], scalar=1.0, in1=hc[:, s % 2],
                                               op0=ALU.subtract, op1=ALU.mult, reverse0=True).then_inc(fresh_ready, 1)
                if s + 1 < S:
                    dve.wait_ge(early_ready, step)
                    dve.wait_ge(late_ready, step)
                    nc.vector.tensor_tensor(x_par[:, (s + 1) % 2], early[:], late[:], ALU.add).then_inc(x_ready, 1)
                dve.wait_ge(fresh_ready, turn)
                dve.wait_ge(kept_ready, turn)
                nc.vector.tensor_tensor(delta[:, s], fresh[:], kept[:, s % 2], ALU.add).then_inc(delta_ready, 1)
                if s + 2 < S:
                    if s:
                        dve.wait_ge(far_added, block * (S - 3) + s)
                    dve.wait_ge(delta_ready, turn)
                    nc.vector.tensor_tensor(far[:, s + 2:S], coefficients(s)[:, s + 2:S],
                                            delta[:, s].unsqueeze(1).broadcast_to([P, S - s - 2, B]),
                                            ALU.mult).then_inc(far_ready, 1)

            with dve.Fori(0, P // SPAN) as span:
                for g, bank in enumerate(BASE):
                    dve.wait_ge(base_done, span * NG + g + 1)
                    copied = nc.vector.tensor_copy(sums[:, :, g * GB:(g + 1) * GB],
                                                   ps[:, bank, :].rearrange("p (b i) -> p i b", i=SPAN))
                copied.then_inc(sums_ready, 1)
                for p in range(BLOCKS):
                    block = span * BLOCKS + p
                    rows = slice(p * S + 1, (p + 1) * S)
                    if p == 0:
                        dve.wait_ge(sums_ready, block + 1)
                        nc.vector.tensor_copy(x_par[:, 0], sums[:, 0]).then_inc(x_ready, 1)
                    else:
                        corr = ps[:, CORR, :].rearrange("p (b i) -> p i b", i=S)
                        dve.wait_ge(pair_done, span * len(BLOCK_PAIRS) + PAIRS_UP_TO[p] + 2)
                        nc.vector.tensor_tensor(x_par[:, 0], sums[:, p * S], corr[:, 0], ALU.add).then_inc(x_ready, 1)
                        nc.vector.tensor_tensor(sums[:, rows], sums[:, rows], corr[:, 1:S], ALU.add).then_inc(sums_ready, 1)
                    for s in range(S):
                        turn, step = block * S + s + 1, block * (S - 1) + s + 1
                        if s:
                            after_tanh(block, s - 1)
                        if s + 1 < S:
                            near = coefficients(s)[:, s + 1]
                            dve.wait_ge(coef_done, step)
                            dve.wait_ge(x_ready, turn)
                            nc.vector.tensor_tensor(near_x[:], x_par[:, s % 2], near, ALU.mult).then_inc(near_x_ready, 1)
                        dve.wait_ge(r_ready, turn)
                        dve.wait_ge(x_ready, turn)
                        nc.vector.tensor_tensor(xr[:], x_par[:, s % 2], r[:], ALU.mult).then_inc(xr_ready, 1)
                        if s + 1 < S:
                            dve.wait_ge(z_ready, turn)
                            dve.wait_ge(near_x_ready, step)
                            nc.vector.tensor_tensor(z_near_x[:], z[:, s % 2], near_x[:], ALU.mult).then_inc(z_near_x_ready, 1)
                            nc.vector.scalar_tensor_tensor(out=near_z[:], in0=z[:, s % 2], scalar=1.0, in1=near,
                                                           op0=ALU.subtract, op1=ALU.mult, reverse0=True).then_inc(near_z_ready, 1)
                            dve.wait_ge(sums_ready, block + 1)
                            if s:
                                dve.wait_ge(near_added, block * (S - 2) + s)
                            dve.wait_ge(z_near_x_ready, step)
                            nc.vector.tensor_tensor(early[:], sums[:, p * S + s + 1], z_near_x[:], ALU.add).then_inc(early_ready, 1)
                    after_tanh(block, S - 1)
                    if p + 1 < BLOCKS:
                        dve.wait_ge(delta_turned, span * (BLOCKS - 1) + p + 1)
                        nc.vector.tensor_copy(delta_nm[:, p].rearrange("p g d -> p (g d)"),
                                              ps[:, TURN_DELTA, :]).then_inc(delta_nm_ready, 1)

        @block_of_engines.tensor
        def _(pe):
            pe.sem_inc(pair_done, 2)
            pe.wait_ge(w_in, 32)
            pe.wait_ge(select_ready, 1)

            def gates_of_x(block, chunk, banks):
                gate, at = chunk // 4, chunk % 4
                nc.tensor.matmul(ps[:, banks[gate], at * 2 * B:(at + 1) * 2 * B], wx[:, gate, :], old(block, 2 * at, 2),
                                 start=at == 0, stop=False, skip_group_check=True)

            def spread(block, pair, g):
                k, target = BLOCK_PAIRS[pair]
                return nc.tensor.matmul(ps[:, CORR, :].rearrange("p (b g i) -> p g b i", g=NG, i=S)[:, g],
                                        delta_nm[:, k, g, :], step_mat[:, pair % 2, g], start=k == 0 and g == 0,
                                        stop=True, skip_group_check=True)

            def turn_block(slab, bank):
                for g in range(NG):
                    one = nc.tensor.transpose(ps[:, bank, g * P:(g + 1) * P],
                                              slab[:].rearrange("p n (b g) -> p g n b", g=NG)[:, g], identity[:])
                return one

            with pe.Fori(0, P // SPAN) as span:
                for chunk in range(8):
                    gates_of_x(span * BLOCKS, chunk, (R[0], Z[0]))
                pe.wait_ge(rows_in, span * BLOCKS * 16 + 16)
                for b in range(B):
                    at = b % GB
                    one = nc.tensor.matmul(ps[:, BASE[b // GB], at * SPAN:(at + 1) * SPAN], X[:, b, :],
                                           adj[:, b, bass.ds(span * SPAN, SPAN)], start=at == 0, stop=True,
                                           skip_group_check=True)
                    if at == GB - 1:
                        one.then_inc(base_done, 1)
                for p in range(BLOCKS):
                    block = span * BLOCKS + p
                    early_steps = [(pair, g) for pair, (k, target) in enumerate(BLOCK_PAIRS) if target == p + 1 and k < p
                                   for g in range(NG)]
                    for s in range(S):
                        turn, step = block * S + s + 1, block * (S - 1) + s + 1
                        pe.wait_ge(x_ready, turn)
                        nc.tensor.matmul(ps[:, R[p % 2], s * B:(s + 1) * B], wh[:, 0, :], x_par[:, s % 2], start=False,
                                         stop=True, skip_group_check=True).then_inc(r_done, 1)
                        nc.tensor.matmul(ps[:, Z[p % 2], s * B:(s + 1) * B], wh[:, 1, :], x_par[:, s % 2], start=False,
                                         stop=True, skip_group_check=True).then_inc(z_done, 1)
                        if s + 1 < S:
                            if s > 1:
                                pe.wait_ge(far_ready, block * (S - 2) + s - 1)
                            if s == 0 and p:
                                pe.wait_ge(h_nm_ready, block)
                            nc.tensor.matmul(ps[:, COEF[s % 2], (s + 1) * B:S * B], select[:, s, :],
                                             parts[:, bass.ds(block, 1), s + 1:S, :].squeeze(1), start=True,
                                             stop=True).then_inc(coef_done, 1)
                        if s == 0:
                            nc.tensor.matmul(ps[:, C, 0:B], wx[:, 2, :], old(block, 0), start=True, stop=False)
                        pe.wait_ge(xr_ready, turn)
                        nc.tensor.matmul(ps[:, C, 0:B], wh[:, 2, :], xr[:], start=False, stop=True).then_inc(c_done, 1)
                        if p + 1 < BLOCKS:
                            gates_of_x(block + 1, s, (R[(p + 1) % 2], Z[(p + 1) % 2]))
                        if s < len(early_steps):
                            pair, g = early_steps[s]
                            if s == 0:
                                pe.wait_ge(sums_ready, block + 1)
                            if g == 0:
                                pe.wait_ge(step_ready, span * len(BLOCK_PAIRS) + pair + 1)
                            one = spread(block, pair, g)
                            if g == NG - 1:
                                one.then_inc(pair_done, 1)
                        if s + 1 < S:
                            pe.wait_ge(hc_ready, turn)
                            nc.tensor.matmul(ps[:, C, 0:B], wx[:, 2, :], old(block, s + 1), start=True, stop=False)
                    if p + 1 < BLOCKS:
                        pe.wait_ge(delta_ready, (block + 1) * S)
                        turn_block(delta, TURN_DELTA).then_inc(delta_turned, 1)
                    pe.wait_ge(h_ready, (block + 1) * 2)
                    turn_block(h_new, TURN_H).then_inc(h_turned, 1)
                    if p + 1 < BLOCKS:
                        pair = BLOCK_PAIRS.index((p, p + 1))
                        pe.wait_ge(step_ready, span * len(BLOCK_PAIRS) + pair + 1)
                        pe.wait_ge(delta_nm_ready, span * (BLOCKS - 1) + p + 1)
                        for g in range(NG):
                            one = spread(block, pair, g)
                        one.then_inc(pair_done, 1)


def spread_coefficients(nc, dram, consts, ctx, inverse_t, inverse, parts, between):
    def sb(name, shape, dt=F32):
        return ctx.enter_context(nc.sbuf_tensor(name, shape, dt))

    def sem(name):
        return ctx.enter_context(nc.semaphore(name))

    NG = B * S // P
    diag = sb("diag", [P, B, S])
    low = sb("low", [P, B, S])
    parts_bf = sb("parts_bf", [P, 3, S, B], BF16)
    inverse_8 = sb("inverse_8", [P, B, S])
    eye_8 = sb("eye_8", [P, S])
    same_block = sb("same_block", [P, P])
    inverse_n = sb("inverse_n", [P, NG, P])
    ps = ctx.enter_context(nc.psum_tensor("ps5", [P, 512], F32))
    between_in, diag_in, cleared = sem("between_in"), sem("diag_in"), sem("cleared")
    diagonal_ready, inverse_done, split, between_ready = sem("diagonal_ready"), sem("inverse_done"), sem("split"), sem("between_ready")
    parts_out, parts_in = sem("parts_out"), sem("parts_in")

    block = ctx.enter_context(nc.Block())

    @block.sync
    def _(sp):
        sp.dma_start(diag[:], dram["adj_diag"]).then_inc(diag_in, 16)
        sp.dma_start(eye_8[:], dram["eye_8"]).then_inc(diag_in, 16)
        sp.dma_start(same_block[:], dram["same_block"]).then_inc(diag_in, 16)
        for n in range(S):
            sp.dma_start(inverse_n[n * P // S:(n + 1) * P // S],
                         inverse_t.rearrange("(b g) i -> b g i", g=NG)).then_inc(between_in, 16)
        sp.dma_start(between[:], dram["adj_between"]).then_inc(between_in, 16)
        sp.wait_ge(split, 6)
        sp.dma_start(dram["parts"], parts_bf[:].rearrange("p k i b -> p k (i b)")).then_inc(parts_out, 16)
        sp.wait_ge(parts_out, 16)
        sp.wait_ge(cleared, 1)
        for k, at in enumerate(PARTS):
            sp.dma_start(parts[at:at + S].rearrange("n m i b -> n m (i b)"),
                         dram["parts"][:, k, :].rearrange("(m n) f -> n m f", n=S)).then_inc(parts_in, 16)
        sp.wait_ge(parts_in, 16 * len(PARTS))

    @block.gpsimd
    def _(pool):
        nc.gpsimd.memset(parts[:], 0.0).then_inc(cleared, 1)

    @block.vector
    def _(dve):
        dve.wait_ge(diag_in, 48)
        nc.vector.tensor_tensor(inverse_8[:], inverse[:].unsqueeze(2).broadcast_to([P, B, S]),
                                eye_8[:].unsqueeze(1).broadcast_to([P, B, S]), ALU.mult).then_inc(diagonal_ready, 1)
        dve.wait_ge(inverse_done, 1)
        nc.vector.tensor_tensor(diag[:], diag[:], ps[:].rearrange("p (b i) -> p b i", i=S), ALU.mult).then_inc(split, 1)

        def part(k):
            return parts_bf[:, k].rearrange("p i b -> p b i")

        for k in range(3):
            rest = diag if k == 0 else low
            dve.wait_ge(split, 2 * k + 1)
            nc.vector.tensor_copy(part(k), rest[:]).then_inc(split, 1)
            if k < 2:
                dve.wait_ge(split, 2 * k + 2)
                nc.vector.tensor_tensor(low[:], rest[:], part(k), ALU.subtract).then_inc(split, 1)
        dve.wait_ge(between_in, 16 * (S + 1))
        for pair, (_, target) in enumerate(BLOCK_PAIRS):
            columns = inverse_n[:].rearrange("p g (m i) -> p m g i", i=SPAN)[:, :, :, target * S:(target + 1) * S]
            nc.vector.tensor_tensor(between[:, :, pair], between[:, :, pair], columns, ALU.mult).then_inc(between_ready, 1)

    @block.tensor
    def _(pe):
        pe.wait_ge(diagonal_ready, 1)
        nc.tensor.matmul(ps[:], same_block[:], inverse_8[:].rearrange("p b i -> p (b i)"), start=True,
                         stop=True).then_inc(inverse_done, 1)


def final_norm(nc, X, x_kept, consts, out):
    with ExitStack() as ctx:
        def sb(name, shape):
            return ctx.enter_context(nc.sbuf_tensor(name, shape, F32))

        def sem(name):
            return ctx.enter_context(nc.semaphore(name))

        CHUNK = 8
        stats = sb("stats6", [P, 2, CHUNK, 6])
        mv = sb("mv6", [P, 2, CHUNK, 2])
        rstd = sb("rstd6", [P, 2, CHUNK])
        spare = sb("spare6", [P, 1])
        summed, stats_ready, moments_ready = sem("summed6"), sem("stats6_ready"), sem("moments6_ready")
        var_eps, rstd_ready, normed, stored = sem("var_eps6"), sem("rstd6_ready"), sem("normed6"), sem("stored")
        ROUNDS = B // CHUNK // 2
        block = ctx.enter_context(nc.Block())

        @block.sync
        def _(sp):
            with sp.Fori(0, ROUNDS) as it:
                for s in range(2):
                    part = bass.ds((it * 2 + s) * CHUNK, CHUNK)
                    sp.wait_ge(normed, it * 2 + s + 1)
                    sp.dma_start(out[:, part, :], X[:, part, :]).then_inc(stored, 16)
            sp.wait_ge(stored, 16 * 2 * ROUNDS)

        @block.gpsimd
        def _(pool):
            with pool.Fori(0, ROUNDS) as it:
                for s in range(2):
                    pool.wait_ge(moments_ready, it * 2 + s + 1)
                    nc.gpsimd.tensor_tensor(mv[:, s, :, 1], mv[:, s, :, 1], consts["eps"][:, 0:CHUNK],
                                            ALU.add).then_inc(var_eps, 1)
                    pool.wait_ge(var_eps, it * 2 + s + 1)
                    nc.gpsimd.tensor_tensor(rstd[:, s, :], mv[:, s, :, 1], consts["minus_half"][:, 0:CHUNK],
                                            ALU.pow).then_inc(rstd_ready, 1)

        @block.vector
        def _(dve):
            with dve.Fori(0, ROUNDS) as it:
                for s in range(2):
                    at = (it * 2 + s) * CHUNK
                    part = X[:, bass.ds(at, CHUNK), :]
                    nc.vector.tensor_tensor(part, part, x_kept[:, bass.ds(at, CHUNK), :], ALU.add).then_inc(summed, 1)
                    dve.wait_ge(summed, it * 2 + s + 1)
                    nc.vector.memset(spare[:], 0.0)
                    for b in range(CHUNK):
                        one = nc.vector.bn_stats(stats[:, s, b, :], X[:, bass.ds(at + b, 1), :])
                    one.then_inc(stats_ready, 1)
                    alone(dve, consts["identity_in"])
                    dve.wait_ge(stats_ready, it * 2 + s + 1)
                    for b in range(CHUNK):
                        one = nc.vector.bn_aggr(mv[:, s, b, :], stats[:, s, b, :])
                    one.then_inc(moments_ready, 1)
                for s in range(2):
                    dve.wait_ge(rstd_ready, it * 2 + s + 1)
                    for b in range(CHUNK):
                        part = X[:, bass.ds((it * 2 + s) * CHUNK + b, 1), :]
                        one = nc.vector.tensor_scalar(part, part, mv[:, s, b, 0:1], rstd[:, s, b:b + 1],
                                                      ALU.subtract, ALU.mult)
                    one.then_inc(normed, 1)


def graph_layers(nc, dram, out):
    with ExitStack() as ctx:
        def sb(name, shape):
            return ctx.enter_context(nc.sbuf_tensor(name, shape, F32))

        def sem(name):
            return ctx.enter_context(nc.semaphore(name))

        X = sb("X", [P, B, P])
        adj = sb("adj", [P, B, P])
        node_degree = sb("node_degree", [P, B])
        degrees_ready = sem("degrees_ready")
        inverse_stored = sem("inverse_stored")
        consts = {"identity": sb("identity", [P, P]), "minus_half": sb("minus_half", [P, B]), "eps": sb("eps", [P, B]),
                  "identity_in": sem("identity_in")}
        with ExitStack() as groups:
            norm_t = groups.enter_context(nc.sbuf_tensor("norm_t", [Q, B, Q], F32))
            root_diag = groups.enter_context(nc.sbuf_tensor("root_diag", [Q, B, Q], F32))
            groups_ready = groups.enter_context(nc.semaphore("groups_ready"))
            gated_convolution(nc, dram, X, adj, consts, norm_t, root_diag, groups_ready, node_degree,
                              degrees_ready)
            group_convolution(nc, dram, X, consts, norm_t, root_diag, groups_ready, node_degree,
                              dram["inverse_t"], inverse_stored)
        hn = ctx.enter_context(nc.sbuf_tensor("hn", [P, B, P], F32))
        graph_attention(nc, dram, X, adj, hn, consts)
        x_fm = ctx.enter_context(nc.sbuf_tensor("x_fm", [P, P, B], F32))
        finish_attention(nc, dram, X, adj, hn, x_fm, consts, dram["inverse_t"])
        gated_scan(nc, dram, X, adj, x_fm, consts, dram["inverse_t"], node_degree)
        final_norm(nc, X, hn, consts, out)


def kernel(**inputs):
    import numpy as np
    import concourse.bacc as bacc
    from concourse.bass_utils import run_bass_kernel_spmd

    def lay(a):
        return np.ascontiguousarray(a)

    a = {k: np.asarray(v) for k, v in inputs.items()}
    x, adj = a["x"], a["adj"]
    group_of = [g for g, nodes in enumerate(GROUPS) for _ in nodes]
    blocks = np.zeros((Q, B, Q), adj.dtype)
    blocks_t = np.zeros((Q, B, Q), adj.dtype)
    to_joint = np.zeros((Q, JOINTS), np.float32)
    for q, n in enumerate(ROWS):
        to_joint[q, n] = 1.0
        for p, m in enumerate(ROWS):
            if group_of[p] == group_of[q]:
                blocks[q, :, p] = adj[:, n, m]
                blocks_t[q, :, p] = adj[:, m, n]
    G = len(GROUPS)
    blocks_of = P // S
    by_block = adj.reshape(B, blocks_of, S, blocks_of, S)
    own = np.stack([by_block[:, m, :, m] for m in range(blocks_of)])
    spans, in_span = P // SPAN, SPAN // S
    between = np.stack([np.stack([by_block[:, m * in_span + k, :, m * in_span + target] for k, target in BLOCK_PAIRS])
                        for m in range(spans)])
    select = np.zeros((PARTS[-1] + S, S, P), np.float32)
    for s in range(S):
        for at in PARTS:
            select[at + s, s] = 1.0
    node = np.arange(P)
    gate = a["L3_gnn_W_ioux"].reshape(2, P, P).transpose(2, 0, 1), a["L3_gnn_W_iouh"].reshape(2, P, P).transpose(2, 0, 1)
    wide = (P, P)
    arrays = {
        "adj_diag": lay(own.transpose(0, 2, 1, 3).reshape(P, B, S)),
        "adj_between": lay(between.reshape(spans, len(BLOCK_PAIRS), P // S, B * S // P, S, S).transpose(
            4, 2, 0, 1, 3, 5).reshape(P, spans, len(BLOCK_PAIRS), B * S // P, S)),
        "not_next": (1 - ((node[:, None] + 1 == node) & (node % S != 0))).astype(np.float32),
        "eye_8": (node[:, None] % S == np.arange(S)).astype(np.float32),
        "same_block": (node[:, None] // S == node // S).astype(np.float32),
        "same_graph": lay(np.broadcast_to((node[:, None] % (P // S) == np.arange(P // S))[:, :, None],
                                          (P, P // S, S)).astype(np.float32)),
        "select": select,
        "L3_wx": lay(np.concatenate([gate[0], a["L3_gnn_W_coux"].T[:, None]], axis=1)),
        "L3_wh": lay(np.concatenate([gate[1], a["L3_gnn_W_couh"].T[:, None]], axis=1)),
        "L3_bx": lay(np.stack([*a["L3_gnn_b_ioux"].reshape(2, P), a["L3_gnn_b_coux"]], axis=1)),
        "L3_bh": lay(np.stack([*a["L3_gnn_b_iouh"].reshape(2, P), a["L3_gnn_b_couh"]], axis=1)),
        "L2_W": a["L2_gnn_W"],
        "L2_W_t": lay(a["L2_gnn_W"].T),
        "L2_a1": lay(np.broadcast_to(a["L2_gnn_a"][:P], wide)),
        "L2_a2": lay(np.broadcast_to(a["L2_gnn_a"][P:], wide)),
        "L2_gamma": lay(np.broadcast_to(a["L2_gnn_gamma"], wide)),
        "L2_beta": lay(np.broadcast_to(a["L2_gnn_beta"], wide)),
        "adj_groups": blocks,
        "adj_groups_t": blocks_t,
        "to_joint": to_joint,
        "L1_W1": lay(a["L1_gnn_W1"].reshape(G, P, HALVES, P).transpose(1, 0, 2, 3)),
        "L1_W2": lay(a["L1_gnn_W2"].reshape(G, HALVES, P, P).transpose(2, 0, 1, 3)),
        "L1_b1": lay(a["L1_gnn_b1"].reshape(G, HALVES, P).transpose(2, 0, 1)),
        "L1_b2": lay(a["L1_gnn_b2"].T),
        "L1_fusion_w": lay(np.broadcast_to(a["L1_gnn_fusion_w"], (P, G))),
        "x_nm": lay(x.transpose(1, 0, 2)),
        "x_fm": lay(x.transpose(2, 0, 1).reshape(P, B * P)),
        "adj_nm": lay(adj.transpose(1, 0, 2)),
        "mask": lay(a["nodemask"].T),
        "identity": np.eye(P, dtype=np.float32),
        "L0_weight": lay(a["L0_gnn_weight"].transpose(1, 0, 2)),
        "L0_w_ih": lay(a["L0_gnn_w_ih"].reshape(3, P, P).transpose(2, 0, 1)),
        "L0_w_hh": lay(a["L0_gnn_w_hh"].reshape(3, P, P).transpose(2, 0, 1)),
        "L0_b_ih": lay(a["L0_gnn_b_ih"].reshape(3, P).T),
        "L0_b_hh": lay(a["L0_gnn_b_hh"].reshape(3, P).T),
    }
    nc = bacc.Bacc("TRN2", target_bir_lowering=False, num_devices=1)
    dram = {name: nc.dram_tensor(f"in_{name}", v.shape, F32, kind="ExternalInput").ap() for name, v in arrays.items()}
    dram["inverse_t"] = nc.dram_tensor("inverse_t", (B, P), F32, kind="Internal").ap()
    dram["parts"] = nc.dram_tensor("parts_scratch", (P, 3, S * B), BF16, kind="Internal").ap()
    out = nc.dram_tensor("out_nm", (P, B, P), F32, kind="ExternalOutput").ap()
    graph_layers(nc, dram, out)
    result = run_bass_kernel_spmd(nc, [{f"in_{name}": v for name, v in arrays.items()}], core_ids=[0])
    return lay(result.results[0]["out_nm"].transpose(1, 0, 2))
```

```python
from contextlib import ExitStack

import concourse.bass as bass
from concourse import mybir

F32 = mybir.dt.float32
BF16 = mybir.dt.bfloat16
ALU = mybir.AluOpType
ACT = mybir.ActivationFunctionType
AX_X = mybir.AxisListType.X

P = 128
B = 64
LAYERS = 5
TILE = 4
COLS = TILE * P
PAIRS = B // (2 * TILE)
S = 8
SPAN = 32
BLOCK_PAIRS = [(k, target) for target in range(1, SPAN // S) for k in range(target)]
PAIRS_UP_TO = [sum(target <= p for _, target in BLOCK_PAIRS) for p in range(SPAN // S)]
PARTS = (0, 64, 96)
EPS = 1e-5
ALPHA = 0.2
NEG = -9e15


GROUPS = (list(range(25)), list(range(9)), [0, *range(9, 15)], [6, 7, 8, 12, 13, 14], [3, 4, 5, 9, 10, 11])
JOINTS = 25
ROWS = [n for nodes in GROUPS for n in nodes]
Q = len(ROWS)
FIRST = [sum(len(nodes) for nodes in GROUPS[:g]) for g in range(len(GROUPS))]
HALVES = 2
T1 = 8


def runs(nodes):
    found, at = [], 0
    while at < len(nodes):
        k = 1
        while at + k < len(nodes) and nodes[at + k] == nodes[at] + k:
            k += 1
        found.append((at, nodes[at], k))
        at += k
    return found


def alone(eng, met):
    eng.wait_ge(met, 1)


def is_first(it):
    return isinstance(it, int) and it == 0


def gated_convolution(nc, dram, X, adj, consts, norm_t, root_diag, groups_ready, node_degree, degrees_ready):
    with nc.cleanup_on_exit(), ExitStack() as ctx:
        def sb(name, shape):
            return ctx.enter_context(nc.sbuf_tensor(name, shape, F32))

        def sem(name):
            return nc.alloc_semaphore(name)

        w_msg = sb("w_msg", [P, LAYERS, P])
        w_ih = sb("w_ih", [P, 3, P])
        w_hh = sb("w_hh", [P, 3, P])
        b_ih = sb("b_ih", [P, 3])
        b_hh = sb("b_hh", [P, 3])
        b_rz = sb("b_rz", [P, 2])
        mask = sb("mask", [P, B])
        h_in = sb("h_in", [P, 2, COLS])
        h = sb("h", [P, 2, COLS])
        h_last = sb("h_last", [P, 2, COLS])
        edges = sb("edges", [P, 2, COLS])
        m_sb = sb("m_sb", [P, 2, COLS])
        agg_sb = sb("agg_sb", [P, 2, COLS])
        r = sb("r", [P, 2, COLS])
        z = sb("z", [P, 2, COLS])
        n_pre = sb("n_pre", [P, 2, COLS])
        n = sb("n", [P, 2, COLS])
        zh = sb("zh", [P, 2, COLS])
        stats = sb("stats", [P, TILE, 6])
        mv = sb("mv", [P, 2, TILE, 2])
        rstd = sb("rstd", [P, 2, TILE])
        adj_groups = sb("adj_groups", [Q, B, Q])
        eye_q = sb("eye_q", [Q, Q])
        degree = sb("degree", [Q, 2 * TILE])
        root = sb("root", [Q, 2 * TILE])
        ps = ctx.enter_context(nc.psum_tensor("ps0", [P, 8, COLS], F32))
        R, Z, HN, SHARED = (0, 1), (2, 3), (4, 5), (6, 7)

        w_first_in, w_hh_in, w_ih_in, w_msg_in = sem("w_first_in"), sem("w_hh_in"), sem("w_ih_in"), sem("w_msg_in")
        small_in = sem("small_in")
        h_loaded = [sem(f"h_loaded{s}") for s in range(2)]
        nodes_loaded = sem("nodes_loaded")
        adj_loaded = sem("adj_loaded")
        edges_ready = sem("edges_ready")
        m_done = sem("m_done")
        m_copied = sem("m_copied")
        agg_done = sem("agg_done")
        agg_copied = sem("agg_copied")
        r_done = sem("r_done")
        z_done = sem("z_done")
        n_done = sem("n_done")
        r_ready = sem("r_ready")
        z_ready = sem("z_ready")
        n_pre_ready = sem("n_pre_ready")
        n_ready = sem("n_ready")
        chain = sem("gru_chain")
        zh_ready = sem("zh_ready")
        h_ready = sem("h_ready")
        turned = sem("turned")
        summed = sem("summed")
        moments_ready = sem("moments_ready")
        var_eps = sem("var_eps")
        rstd_ready = sem("rstd_ready")
        normed = sem("normed")
        const_ready = sem("const_ready")

        groups_in = sem("groups_in")
        eye_added = sem("eye_added")
        degree_step = sem("degree_step")
        guarded = sem("guarded")
        powered = sem("powered")
        root_ready = sem("root_ready")
        rows_scaled = sem("rows_scaled")

        def graphs(it):
            return bass.ds(it * 2 * TILE, 2 * TILE)

        STEPS = 2 * LAYERS

        def pairs(eng, body):
            body(0)
            with eng.Fori(1, PAIRS) as it:
                body(it)

        block = ctx.enter_context(nc.Block())

        @block.sync
        def _(sp):
            def pair_in(it):
                for s in range(2):
                    if not is_first(it):
                        sp.wait_ge(h_ready, (it - 1) * STEPS + s + 1)
                    sp.dma_start(h_in[:, s, :], dram["x_fm"][:, bass.ds((it * 2 + s) * COLS, COLS)]).then_inc(h_loaded[s], 16)
                    if s == 0:
                        sp.dma_start(adj[:, bass.ds(it * 2 * TILE, 2 * TILE), :],
                                     dram["adj_nm"][:, bass.ds(it * 2 * TILE, 2 * TILE), :]).then_inc(adj_loaded, 16)
                if is_first(it):
                    sp.dma_start(w_msg[:, 1:LAYERS, :], dram["L0_weight"][:, 1:LAYERS, :]).then_inc(w_msg_in, 16)
                    sp.dma_start(norm_t[:], dram["adj_groups_t"]).then_inc(groups_in, 16)
                    sp.dma_start(adj_groups[:], dram["adj_groups"]).then_inc(groups_in, 16)
                    sp.dma_start(eye_q[:], dram["identity"][0:Q, 0:Q]).then_inc(groups_in, 16)
                sp.dma_start(X[:, bass.ds(it * 2 * TILE, 2 * TILE), :],
                             dram["x_nm"][:, bass.ds(it * 2 * TILE, 2 * TILE), :]).then_inc(nodes_loaded, 16)

            sp.dma_start(w_msg[:, 0:1, :], dram["L0_weight"][:, 0:1, :]).then_inc(w_first_in, 16)
            pairs(sp, pair_in)

        @block.scalar
        def _(act):
            act.dma_start(w_hh[:], dram["L0_w_hh"]).then_inc(w_hh_in, 16)
            act.dma_start(w_ih[:], dram["L0_w_ih"]).then_inc(w_ih_in, 16)
            act.dma_start(b_ih[:], dram["L0_b_ih"]).then_inc(small_in, 16)
            act.dma_start(b_hh[:], dram["L0_b_hh"]).then_inc(small_in, 16)
            act.dma_start(mask[:], dram["mask"]).then_inc(small_in, 16)
            act.dma_start(consts["identity"][:], dram["identity"]).then_inc(consts["identity_in"], 16)
            act.wait_ge(const_ready, 2)

            def pair(it):
                for u in range(STEPS):
                    s, turn = u % 2, it * STEPS + u
                    act.wait_ge(m_done, turn + 1)
                    nc.scalar.copy(m_sb[:, s, :], ps[:, SHARED[s], :]).then_inc(m_copied, 1)
                    act.wait_ge(agg_done, turn + 1)
                    nc.scalar.copy(agg_sb[:, s, :], ps[:, SHARED[1 - s], :]).then_inc(agg_copied, 1)
                    act.wait_ge(r_done, turn + 1)
                    nc.scalar.activation(r[:, s, :], ps[:, R[s], :], ACT.Sigmoid, bias=b_rz[:, 0:1]).then_inc(r_ready, 1)
                    act.wait_ge(z_done, turn + 1)
                    nc.scalar.activation(z[:, s, :], ps[:, Z[s], :], ACT.Sigmoid, bias=b_rz[:, 1:2]).then_inc(z_ready, 1)
                    act.wait_ge(n_pre_ready, turn + 1)
                    nc.scalar.activation(n[:, s, :], n_pre[:, s, :], ACT.Tanh, bias=b_ih[:, 2:3]).then_inc(n_ready, 1)

            pairs(act, pair)

        @block.gpsimd
        def _(pool):
            nc.gpsimd.memset(consts["minus_half"][:], -0.5)
            nc.gpsimd.memset(consts["eps"][:], EPS).then_inc(const_ready, 1)

            def reciprocal_root(it, s):
                pool.wait_ge(moments_ready, it * 2 + s + 1)
                nc.gpsimd.tensor_tensor(mv[:, s, :, 1], mv[:, s, :, 1], consts["eps"][:, 0:TILE],
                                        ALU.add).then_inc(var_eps, 1)
                pool.wait_ge(var_eps, it * 2 + s + 1)
                nc.gpsimd.tensor_tensor(rstd[:, s, :], mv[:, s, :, 1], consts["minus_half"][:, 0:TILE],
                                        ALU.pow).then_inc(rstd_ready, 1)

            pool.wait_ge(const_ready, 1)

            def pair(it):
                for u in range(STEPS):
                    s, turn = u % 2, it * STEPS + u
                    if u < 2:
                        pool.wait_ge(h_loaded[s], (it + 1) * 16)
                    pool.wait_ge(z_ready, turn + 1)
                    src = h_in if u < 2 else h
                    nc.gpsimd.tensor_tensor(zh[:, s, :], z[:, s, :], src[:, s, :], ALU.mult).then_inc(zh_ready, 1)
                    if u == 3:
                        pool.wait_ge(groups_in, 48)
                        nc.gpsimd.tensor_tensor(norm_t[:, graphs(it), :], norm_t[:, graphs(it), :],
                                                eye_q[:].unsqueeze(1).broadcast_to([Q, 2 * TILE, Q]),
                                                ALU.add).then_inc(eye_added, 1)
                    if u == 5:
                        pool.wait_ge(guarded, it + 1)
                        nc.gpsimd.tensor_tensor(root[:], root[:], consts["minus_half"][0:Q, 0:2 * TILE],
                                                ALU.pow).then_inc(powered, 1)
                    if u == 7:
                        alone(pool, consts["identity_in"])
                        pool.wait_ge(eye_added, it + 1)
                        pool.wait_ge(root_ready, it + 1)
                        nc.gpsimd.tensor_tensor(norm_t[:, graphs(it), :], norm_t[:, graphs(it), :],
                                                root[:].unsqueeze(2).broadcast_to([Q, 2 * TILE, Q]),
                                                ALU.mult).then_inc(rows_scaled, 1)
                    if u == 8:
                        nc.gpsimd.tensor_tensor(root_diag[:, graphs(it), :],
                                                eye_q[:].unsqueeze(1).broadcast_to([Q, 2 * TILE, Q]),
                                                root[:].unsqueeze(2).broadcast_to([Q, 2 * TILE, Q]),
                                                ALU.mult).then_inc(groups_ready, 1)
                    if u == 1 and not is_first(it):
                        reciprocal_root(it - 1, 0)
                    if u == 2 and not is_first(it):
                        reciprocal_root(it - 1, 1)

            pairs(pool, pair)
            reciprocal_root(PAIRS - 1, 0)
            reciprocal_root(PAIRS - 1, 1)

        @block.vector
        def _(dve):
            dve.wait_ge(small_in, 48)
            nc.vector.tensor_tensor(b_rz[:], b_ih[:, 0:2], b_hh[:, 0:2], ALU.add).then_inc(const_ready, 1)

            def residual(it, s):
                dve.wait_ge(nodes_loaded, (it + 1) * 16)
                dve.wait_ge(turned, it * 2 + s + 1)
                for g in range(TILE):
                    b = it * 2 * TILE + s * TILE + g
                    one = nc.vector.scalar_tensor_tensor(
                        out=X[:, bass.ds(b, 1), :], in0=ps[:, HN[s], g * P:(g + 1) * P].unsqueeze(1), scalar=mask[:, bass.ds(b, 1)],
                        in1=X[:, bass.ds(b, 1), :], op0=ALU.mult, op1=ALU.add)
                one.then_inc(summed, 1)
                alone(dve, consts["identity_in"])
                dve.wait_ge(summed, it * 2 + s + 1)
                for g in range(TILE):
                    b = it * 2 * TILE + s * TILE + g
                    one = nc.vector.bn_stats(stats[:, g, :], X[:, bass.ds(b, 1), :])
                one.then_inc(chain, 1)
                alone(dve, consts["identity_in"])
                dve.wait_ge(chain, it * 2 + s + 1)
                for g in range(TILE):
                    one = nc.vector.bn_aggr(mv[:, s, g, :], stats[:, g, :])
                one.then_inc(moments_ready, 1)

            def normalise(it, s):
                dve.wait_ge(rstd_ready, it * 2 + s + 1)
                for g in range(TILE):
                    b = it * 2 * TILE + s * TILE + g
                    one = nc.vector.tensor_scalar(X[:, bass.ds(b, 1), :], X[:, bass.ds(b, 1), :], mv[:, s, g, 0:1],
                                                  rstd[:, s, g:g + 1], ALU.subtract, ALU.mult)
                one.then_inc(normed, 1)

            def pair(it):
                dve.wait_ge(adj_loaded, (it + 1) * 16)
                for u in range(STEPS):
                    s, turn = u % 2, it * STEPS + u
                    if u < 2:
                        if not is_first(it):
                            dve.wait_ge(agg_done, it * STEPS - 1 + s)
                        nc.vector.tensor_scalar(edges[:, s, :].rearrange("p (b n) -> p b n", b=TILE),
                                                adj[:, bass.ds(it * 2 * TILE + s * TILE, TILE), :],
                                                0.0, None, ALU.not_equal).then_inc(edges_ready, 1)
                    if u < 2 and not is_first(it):
                        residual(it - 1, s)
                    dve.wait_ge(r_ready, turn + 1)
                    nc.vector.scalar_tensor_tensor(out=n_pre[:, s, :], in0=ps[:, HN[s], :], scalar=b_hh[:, 2:3],
                                                   in1=r[:, s, :], op0=ALU.add, op1=ALU.mult).then_inc(r_used, 1)
                    dve.wait_ge(r_used, turn + 1)
                    dve.wait_ge(n_done, turn + 1)
                    nc.vector.tensor_tensor(n_pre[:, s, :], n_pre[:, s, :], ps[:, SHARED[s], :],
                                            ALU.add).then_inc(n_pre_ready, 1)
                    dve.wait_ge(z_ready, turn + 1)
                    nc.vector.tensor_scalar(z1[:, s, :], z[:, s, :], -1.0, 1.0, ALU.mult, ALU.add).then_inc(z1_ready, 1)
                    dve.wait_ge(z1_ready, turn + 1)
                    dve.wait_ge(n_ready, turn + 1)
                    nc.vector.tensor_tensor(n[:, s, :], n[:, s, :], z1[:, s, :], ALU.mult).then_inc(n_scaled, 1)
                    dve.wait_ge(n_scaled, turn + 1)
                    dve.wait_ge(zh_ready, turn + 1)
                    dst = h_last if u >= STEPS - 2 else h
                    nc.vector.tensor_tensor(dst[:, s, :], n[:, s, :], zh[:, s, :], ALU.add).then_inc(h_ready, 1)
                    if u in (2, 3) and not is_first(it):
                        normalise(it - 1, u % 2)
                    if u == 3:
                        dve.wait_ge(groups_in, 48)
                        if not is_first(it):
                            dve.wait_ge(groups_ready, it)
                        nc.vector.tensor_reduce(degree[:], adj_groups[:, graphs(it), :], AX_X,
                                                ALU.add).then_inc(degree_step, 1)
                        dve.wait_ge(degree_step, 2 * it + 1)
                        nc.vector.tensor_scalar(degree[:], degree[:], 1.0, None, ALU.add).then_inc(degree_step, 1)
                        dve.wait_ge(degree_step, 2 * it + 2)
                        nc.vector.scalar_tensor_tensor(out=root[:], in0=degree[:], scalar=0.0, in1=degree[:],
                                                       op0=ALU.is_equal, op1=ALU.add).then_inc(guarded, 1)
                    if u == 4:
                        nc.vector.tensor_reduce(node_degree[:, graphs(it)], adj[:, graphs(it), :], AX_X,
                                                ALU.add).then_inc(degrees_ready, 1)
                    if u == 6:
                        dve.wait_ge(powered, it + 1)
                        nc.vector.scalar_tensor_tensor(out=root[:], in0=degree[:], scalar=0.0, in1=root[:],
                                                       op0=ALU.is_equal, op1=ALU.subtract).then_inc(root_ready, 1)

            z1 = sb("z1", [P, 2, COLS])
            r_used, z1_ready, n_scaled = sem("r_used"), sem("z1_ready"), sem("n_scaled")
            pairs(dve, pair)
            for s in range(2):
                residual(PAIRS - 1, s)
            for s in range(2):
                normalise(PAIRS - 1, s)

        @block.tensor
        def _(pe):
            pe.wait_ge(w_first_in, 16)

            def turn_back(it, s):
                pe.wait_ge(h_ready, it * STEPS + STEPS - 1 + s)
                for g in range(TILE):
                    one = nc.tensor.transpose(ps[:, HN[s], g * P:(g + 1) * P], h_last[:, s, g * P:(g + 1) * P],
                                              consts["identity"][:])
                one.then_inc(turned, 1)

            def hidden_n(state, s, half):
                cols = slice(half * COLS // 2, (half + 1) * COLS // 2)
                nc.tensor.matmul(ps[:, HN[s], cols], w_hh[:, 2, :], state[:, s, cols], start=True, stop=True)

            def pair(it):
                for u in range(STEPS):
                    s, layer, turn = u % 2, u // 2, it * STEPS + u
                    state = h_in if u < 2 else h
                    if u < 2:
                        pe.wait_ge(h_loaded[s], (it + 1) * 16)
                        if not is_first(it):
                            pe.wait_ge(h_ready, turn - 1)
                    else:
                        pe.wait_ge(h_ready, turn - 1)
                    for g in range(TILE):
                        one = nc.tensor.matmul(ps[:, SHARED[s], g * P:(g + 1) * P], state[:, s, g * P:(g + 1) * P],
                                               w_msg[:, layer, :], start=True, stop=True)
                    one.then_inc(m_done, 1)
                    if is_first(it) and u == 0:
                        pe.wait_ge(w_hh_in, 16)
                    nc.tensor.matmul(ps[:, R[s], :], w_hh[:, 0, :], state[:, s, :], start=True, stop=False)
                    if u < 2:
                        nc.tensor.matmul(ps[:, Z[s], :], w_hh[:, 1, :], state[:, s, :], start=True, stop=False)
                    else:
                        hidden_n(state, s, 0)
                    pe.wait_ge(m_copied, turn + 1)
                    if u < 2:
                        pe.wait_ge(edges_ready, it * 2 + s + 1)
                    for g in range(TILE):
                        one = nc.tensor.matmul(ps[:, SHARED[1 - s], g * P:(g + 1) * P], m_sb[:, s, g * P:(g + 1) * P],
                                               edges[:, s, g * P:(g + 1) * P], start=True, stop=True)
                    one.then_inc(agg_done, 1)
                    if u < 2:
                        if not is_first(it):
                            pe.wait_ge(summed, (it - 1) * 2 + s + 1)
                        hidden_n(state, s, 0)
                    else:
                        nc.tensor.matmul(ps[:, Z[s], :], w_hh[:, 1, :], state[:, s, :], start=True, stop=False)
                    hidden_n(state, s, 1)
                    pe.wait_ge(agg_copied, turn + 1)
                    if is_first(it) and u == 0:
                        pe.wait_ge(w_ih_in, 16)
                        pe.wait_ge(w_msg_in, 16)
                        pe.wait_ge(consts["identity_in"], 16)
                    nc.tensor.matmul(ps[:, R[s], :], w_ih[:, 0, :], agg_sb[:, s, :], start=False, stop=True).then_inc(r_done, 1)
                    nc.tensor.matmul(ps[:, SHARED[s], :], w_ih[:, 2, :], agg_sb[:, s, :], start=True,
                                     stop=True).then_inc(n_done, 1)
                    nc.tensor.matmul(ps[:, Z[s], :], w_ih[:, 1, :], agg_sb[:, s, :], start=False, stop=True).then_inc(z_done, 1)
                    if u == 0 and not is_first(it):
                        turn_back(it - 1, 1)
                turn_back(it, 0)

            pairs(pe, pair)
            turn_back(PAIRS - 1, 1)


def group_convolution(nc, dram, X, consts, norm_t, root_diag, groups_ready, node_degree, inverse_t, inverse_stored):
    with ExitStack() as ctx:
        def sb(name, shape):
            return ctx.enter_context(nc.sbuf_tensor(name, shape, F32))

        def sem(name):
            return ctx.enter_context(nc.semaphore(name))

        G, SLOTS = len(GROUPS), 4
        ROUNDS = B // T1 // SLOTS
        ones_q = sb("ones_q", [Q, Q])
        w1 = sb("w1", [P, G, HALVES, P])
        w2 = sb("w2", [P, G, HALVES, P])
        b1 = sb("b1", [P, G, HALVES])
        b2 = sb("b2", [P, G])
        fusion = sb("fusion", [P, G])
        weight = sb("weight", [P, G])
        b2w = sb("b2w", [P, G])
        top = sb("top", [P, 1])
        total = sb("total", [P, 1])
        spare = sb("spare", [P, 1])
        x_in = sb("x_in", [Q, SLOTS, T1, P])
        u_sb = sb("u_sb", [P, SLOTS, T1, Q])
        hid = sb("hid", [P, SLOTS, HALVES, T1, Q])
        sup = sb("sup", [P, SLOTS, T1, Q])
        sup_nm = sb("sup_nm", [Q, SLOTS, T1 * P])
        out_w = sb("out_w", [P, SLOTS, T1, Q])
        stats = sb("stats1", [P, SLOTS, T1, 6])
        mv = sb("mv1", [P, SLOTS, T1, 2])
        rstd = sb("rstd1", [P, SLOTS, T1])
        ps = ctx.enter_context(nc.psum_tensor("ps1", [P, 8, 512], F32))
        identity = consts["identity"]

        small_in = sem("small1_in")
        w_in = sem("w12_in")
        ones_set = sem("ones_set")
        root_done = sem("root_done")
        norm_ready = sem("norm_ready")
        fuse_step = sem("fuse_step")
        fuse_exp = sem("fuse_exp")
        fuse_ready = sem("fuse_ready")
        x_ready = [sem(f"x_ready{s}") for s in range(SLOTS)]
        u_done = sem("u_done")
        u_ready = sem("u_ready")
        hid_done = sem("hid_done")
        hid0_ready = sem("hid0_ready")
        hid1_ready = sem("hid1_ready")
        sup_done = sem("sup_done")
        sup_ready = sem("sup_ready")
        sup_turned = sem("sup_turned")
        sup_nm0_ready = sem("sup_nm0_ready")
        sup_nm1_ready = sem("sup_nm1_ready")
        out_done = sem("out_done")
        out_ready = sem("out_ready")
        fused_step = sem("fused_step")
        fused_ready = sem("fused_ready")
        fused_turned = sem("fused_turned")
        summed = sem("summed1")
        stats_ready = sem("stats1_ready")
        moments_ready = sem("moments1_ready")
        var_eps = sem("var_eps1")
        rstd_ready = sem("rstd1_ready")
        normed = sem("normed1")

        inverse_step = sem("inverse_step")
        inverse_turned = sem("inverse_turned")
        guard = sb("guard", [P, B])
        turned = sb("inverse_turned_sb", [B, P])

        def bank(k):
            return ps[:, k, 0:T1 * Q].rearrange("p (b q) -> p b q", b=T1)

        def group(ap, g):
            return ap[:, :, FIRST[g]:FIRST[g] + len(GROUPS[g])]

        RUNS = [(FIRST[g] + at, node, k) for g, nodes in enumerate(GROUPS) for at, node, k in runs(nodes)]

        PLACES = [[], []]
        for g in range(1, G):
            for at, node, k in runs(GROUPS[g]):
                free = all(node + k <= other or other + length <= node for _, other, length in PLACES[0])
                PLACES[0 if free else 1].append((FIRST[g] + at, node, k))

        def first(it, s):
            return it * SLOTS * T1 + s * T1

        block = ctx.enter_context(nc.Block())

        @block.sync
        def _(sp):
            sp.dma_start(w1[:], dram["L1_W1"]).then_inc(w_in, 16)
            sp.dma_start(w2[:], dram["L1_W2"]).then_inc(w_in, 16)
            sp.wait_ge(inverse_step, 5)
            sp.dma_start(inverse_t, turned[:]).then_inc(inverse_stored, 16)
            sp.dma_start(dram["inverse_n"], node_degree[:]).then_inc(inverse_stored, 16)
            with sp.Fori(0, ROUNDS) as it:
                for s in range(SLOTS):
                    sp.wait_ge(u_done, it * SLOTS + s + 1)
                    for q, node, k in RUNS:
                        sp.dma_start(x_in[q:q + k, s], X[node:node + k, bass.ds(first(it, s), T1), :]).then_inc(x_ready[s], 16)
            sp.wait_ge(inverse_stored, 32)

        @block.scalar
        def _(act):
            act.dma_start(b1[:], dram["L1_b1"]).then_inc(small_in, 16)
            act.dma_start(b2[:], dram["L1_b2"]).then_inc(small_in, 16)
            act.dma_start(fusion[:], dram["L1_fusion_w"]).then_inc(small_in, 16)
            act.wait_ge(fuse_step, 2)
            nc.scalar.activation(weight[:], fusion[:], ACT.Exp, accum_out=total[:]).then_inc(fuse_exp, 1)
            act.wait_ge(fuse_ready, 1)
            with act.Fori(0, ROUNDS) as it:
                for s in range(SLOTS):
                    act.wait_ge(u_done, it * SLOTS + s + 1 + SLOTS)
                    nc.scalar.copy(u_sb[:, s], bank(2 * s)).then_inc(u_ready, 1)
                for s in range(SLOTS):
                    act.wait_ge(hid_done, it * SLOTS + s + 1)
                    for g in range(G):
                        one = nc.scalar.activation(group(hid[:, s, 0], g), group(bank(2 * s), g), ACT.Relu,
                                                   bias=b1[:, g, 0:1])
                    one.then_inc(hid0_ready, 1)
                for s in range(SLOTS):
                    act.wait_ge(sup_done, it * SLOTS + s + 1)
                    nc.scalar.copy(sup[:, s], bank(2 * s)).then_inc(sup_ready, 1)
                for s in range(SLOTS):
                    act.wait_ge(sup_turned, it * SLOTS + s + 1)
                    nc.scalar.copy(sup_nm[:, s, 0:512], ps[0:Q, 2 * s, :]).then_inc(sup_nm0_ready, 1)
                for s in range(SLOTS):
                    act.wait_ge(out_done, it * SLOTS + s + 1)
                    for g in range(G):
                        one = nc.scalar.activation(group(out_w[:, s], g), group(bank(2 * s), g), ACT.Relu,
                                                   bias=b2w[:, g:g + 1], scale=weight[:, g:g + 1])
                    one.then_inc(out_ready, 1)

        @block.gpsimd
        def _(pool):
            nc.gpsimd.memset(ones_q[:], 1.0).then_inc(ones_set, 1)
            with pool.Fori(0, ROUNDS) as it:
                for s in range(SLOTS):
                    pool.wait_ge(moments_ready, it * SLOTS + s + 1)
                    nc.gpsimd.tensor_tensor(mv[:, s, :, 1], mv[:, s, :, 1], consts["eps"][:, 0:T1],
                                            ALU.add).then_inc(var_eps, 1)
                    pool.wait_ge(var_eps, it * SLOTS + s + 1)
                    nc.gpsimd.tensor_tensor(rstd[:, s, :], mv[:, s, :, 1], consts["minus_half"][:, 0:T1],
                                            ALU.pow).then_inc(rstd_ready, 1)

        @block.vector
        def _(dve):
            dve.sem_inc(summed, SLOTS)
            nc.vector.tensor_scalar(guard[:], node_degree[:], 0.0, None, ALU.not_equal).then_inc(inverse_step, 1)
            nc.vector.scalar_tensor_tensor(out=node_degree[:], in0=node_degree[:], scalar=0.0, in1=node_degree[:],
                                           op0=ALU.is_equal, op1=ALU.add).then_inc(inverse_step, 1)
            dve.wait_ge(inverse_step, 2)
            nc.vector.reciprocal(node_degree[:], node_degree[:]).then_inc(inverse_step, 1)
            dve.wait_ge(inverse_step, 3)
            nc.vector.tensor_tensor(node_degree[:], node_degree[:], guard[:], ALU.mult).then_inc(inverse_step, 1)
            dve.wait_ge(inverse_turned, 1)
            nc.vector.tensor_copy(turned[:], ps[0:B, 7, 0:P]).then_inc(inverse_step, 1)
            dve.wait_ge(small_in, 48)
            nc.vector.tensor_reduce(top[:], fusion[:], AX_X, ALU.max).then_inc(fuse_step, 1)
            dve.wait_ge(fuse_step, 1)
            nc.vector.tensor_scalar(fusion[:], fusion[:], top[:, 0:1], None, ALU.subtract).then_inc(fuse_step, 1)
            for k in range(8):
                dve.wait_ge(root_done, k + 1)
                part = norm_t[:, k * T1:(k + 1) * T1, :]
                nc.vector.tensor_tensor(part, part, bank(k)[0:Q], ALU.mult).then_inc(norm_ready, 1)
            dve.wait_ge(fuse_exp, 1)
            nc.vector.reciprocal(total[:], total[:]).then_inc(fuse_step, 1)
            dve.wait_ge(fuse_step, 3)
            nc.vector.tensor_scalar(weight[:], weight[:], total[:, 0:1], None, ALU.mult).then_inc(fuse_step, 1)
            dve.wait_ge(fuse_step, 4)
            nc.vector.tensor_tensor(b2w[:], b2[:], weight[:], ALU.mult).then_inc(fuse_ready, 1)

            with dve.Fori(0, ROUNDS) as it:
                for s in range(SLOTS):
                    dve.wait_ge(hid_done, it * SLOTS + s + 1)
                    for g in range(G):
                        one = nc.vector.tensor_scalar(group(hid[:, s, 1], g), group(bank(2 * s + 1), g),
                                                      b1[:, g, 1:2], 0.0, ALU.add, ALU.max)
                    one.then_inc(hid1_ready, 1)
                for s in range(SLOTS):
                    dve.wait_ge(sup_turned, it * SLOTS + s + 1)
                    nc.vector.tensor_copy(sup_nm[:, s, 512:1024], ps[0:Q, 2 * s + 1, :]).then_inc(sup_nm1_ready, 1)
                for s in range(SLOTS):
                    dve.wait_ge(out_ready, it * SLOTS + s + 1)
                    for level, (places, done) in enumerate(zip(PLACES, (fused_step, fused_ready))):
                        if level:
                            dve.wait_ge(fused_step, it * SLOTS + s + 1)
                        for q, node, k in places:
                            part = out_w[:, s, :, node:node + k]
                            one = nc.vector.tensor_tensor(part, part, out_w[:, s, :, q:q + k], ALU.add)
                        one.then_inc(done, 1)
                for s in range(SLOTS):
                    dve.wait_ge(fused_turned, it * SLOTS + s + 1)
                    for k in range(2):
                        part = X[0:JOINTS, bass.ds(first(it, s) + 4 * k, 4), :]
                        one = nc.vector.tensor_tensor(part, part, ps[0:JOINTS, 2 * s + k, :].rearrange(
                            "p (b d) -> p b d", b=4), ALU.add)
                    one.then_inc(summed, 1)
                    dve.wait_ge(summed, it * SLOTS + s + 1 + SLOTS)
                    nc.vector.memset(spare[:], 0.0)
                    for b in range(T1):
                        one = nc.vector.bn_stats(stats[:, s, b, :], X[:, bass.ds(first(it, s) + b, 1), :])
                    one.then_inc(stats_ready, 1)
                    alone(dve, consts["identity_in"])
                    dve.wait_ge(stats_ready, it * SLOTS + s + 1)
                    for b in range(T1):
                        one = nc.vector.bn_aggr(mv[:, s, b, :], stats[:, s, b, :])
                    one.then_inc(moments_ready, 1)
                for s in range(SLOTS):
                    dve.wait_ge(rstd_ready, it * SLOTS + s + 1)
                    for b in range(T1):
                        part = X[:, bass.ds(first(it, s) + b, 1), :]
                        one = nc.vector.tensor_scalar(part, part, mv[:, s, b, 0:1], rstd[:, s, b:b + 1],
                                                      ALU.subtract, ALU.mult)
                    one.then_inc(normed, 1)

        @block.tensor
        def _(pe):
            pe.sem_inc(u_done, SLOTS)
            pe.wait_ge(inverse_step, 4)
            nc.tensor.transpose(ps[0:B, 7, 0:P], node_degree[:], identity[:]).then_inc(inverse_turned, 1)
            pe.wait_ge(ones_set, 1)
            pe.wait_ge(groups_ready, B // T1)
            for k in range(8):
                if k == 7:
                    pe.wait_ge(inverse_step, 5)
                nc.tensor.matmul(bank(k)[0:Q], ones_q[:], root_diag[:, k * T1:(k + 1) * T1, :], start=True,
                                 stop=True).then_inc(root_done, 1)
            pe.wait_ge(norm_ready, 8)
            pe.wait_ge(w_in, 32)
            with pe.Fori(0, ROUNDS) as it:
                for s in range(SLOTS):
                    pe.wait_ge(x_ready[s], (it + 1) * 16 * len(RUNS))
                    pe.wait_ge(summed, it * SLOTS + s + 1)
                    for b in range(T1):
                        one = nc.tensor.matmul(bank(2 * s)[:, b, :], x_in[:, s, b, :],
                                               norm_t[:, bass.ds(first(it, s) + b, 1), :].squeeze(1), start=True,
                                               stop=True)
                    one.then_inc(u_done, 1)
                for s in range(SLOTS):
                    pe.wait_ge(u_ready, it * SLOTS + s + 1)
                    for half in range(HALVES):
                        for g in range(G):
                            one = nc.tensor.matmul(group(bank(2 * s + half), g), w1[:, g, half, :],
                                                   group(u_sb[:, s], g), start=True, stop=True)
                    one.then_inc(hid_done, 1)
                for s in range(SLOTS):
                    pe.wait_ge(hid0_ready, it * SLOTS + s + 1)
                    pe.wait_ge(hid1_ready, it * SLOTS + s + 1)
                    for g in range(G):
                        for half in range(HALVES):
                            one = nc.tensor.matmul(group(bank(2 * s), g), w2[:, g, half, :],
                                                   group(hid[:, s, half], g), start=half == 0, stop=half == 1)
                    one.then_inc(sup_done, 1)
                for s in range(SLOTS):
                    alone(pe, consts["identity_in"])
                    pe.wait_ge(sup_ready, it * SLOTS + s + 1)
                    for b in range(T1):
                        one = nc.tensor.transpose(ps[0:Q, 2 * s + b // 4, (b % 4) * P:(b % 4 + 1) * P],
                                                  sup[:, s, b, :], identity[:])
                    one.then_inc(sup_turned, 1)
                for s in range(SLOTS):
                    alone(pe, consts["identity_in"])
                    pe.wait_ge(sup_nm0_ready, it * SLOTS + s + 1)
                    pe.wait_ge(sup_nm1_ready, it * SLOTS + s + 1)
                    for b in range(T1):
                        one = nc.tensor.matmul(bank(2 * s)[:, b, :], sup_nm[:, s, b * P:(b + 1) * P],
                                               norm_t[:, bass.ds(first(it, s) + b, 1), :].squeeze(1), start=True, stop=True)
                    one.then_inc(out_done, 1)
                for s in range(SLOTS):
                    alone(pe, consts["identity_in"])
                    pe.wait_ge(fused_ready, it * SLOTS + s + 1)
                    for b in range(T1):
                        one = nc.tensor.transpose(ps[0:JOINTS, 2 * s + b // 4, (b % 4) * P:(b % 4 + 1) * P],
                                                  out_w[:, s, b, 0:JOINTS], identity[:])
                    one.then_inc(fused_turned, 1)


def graph_attention(nc, dram, X, adj, hn, consts):
    with ExitStack() as ctx:
        def sb(name, shape):
            return ctx.enter_context(nc.sbuf_tensor(name, shape, F32))

        def sem(name):
            return ctx.enter_context(nc.semaphore(name))

        SLOTS = 4
        ROUNDS = B // TILE // SLOTS
        w = sb("w_att", [P, P])
        w_t = sb("w_att_t", [P, P])
        a1 = sb("a1", [P, P])
        a2 = sb("a2", [P, P])
        wa1 = sb("wa1", [P, P])
        wa2 = sb("wa2", [P, P])
        gamma = sb("gamma", [P, P])
        beta = sb("beta", [P, P])
        not_next = sb("not_next", [P, P])
        x_in = sb("x2_in", [P, SLOTS, COLS])
        bars = sb("bars", [P, SLOTS, COLS])
        xt = sb("xt", [P, SLOTS, COLS])
        wh = sb("wh", [P, SLOTS, COLS])
        score = sb("score", [P, SLOTS, COLS])
        att = sb("att", [P, SLOTS, COLS])
        att_t = xt
        top = sb("top2", [P, SLOTS, TILE])
        total = sb("total2", [P, SLOTS, TILE])
        scale = sb("scale2", [P, SLOTS, TILE])
        stats = sb("stats2", [P, SLOTS, TILE, 6])
        mv = sb("mv2", [P, SLOTS, TILE, 2])
        ps = ctx.enter_context(nc.psum_tensor("ps2", [P, 8, COLS], F32))
        identity = consts["identity"]

        w_in = sem("w_att_in")
        wa_done = sem("wa_done")
        wa_ready = sem("wa_ready")
        x_loaded = [sem(f"x2_loaded{s}") for s in range(SLOTS)]
        x_turned = sem("x2_turned")
        xt_ready = sem("xt_ready")
        wh_done = sem("wh_done")
        wh_ready = sem("wh_ready")
        score_done = sem("score_done")
        score_copied = sem("score_copied")
        barred = sem("barred")
        not_next_in, cut = sem("not_next_in"), sem("cut")
        leaked = sem("leaked")
        masked = sem("masked")
        top_found = sem("top_found")
        top_ready = sem("top_ready")
        exp_ready = sem("exp_ready")
        att_turned = sem("att_turned")
        att_t_ready = sem("att_t_ready")
        head_done = sem("head_done")
        head_ready = sem("head_ready")
        stats_ready = sem("stats2_ready")
        moments_ready = sem("moments2_ready")
        total_inverted = sem("total_inverted")
        scale_step = sem("scale_step")
        scale_ready = sem("scale_ready")
        head_normed = sem("head_normed")
        gained = sem("gained")
        hn_ready = sem("hn_ready")

        def graph(ap, s, g):
            return ap[:, s, g * P:(g + 1) * P]

        def graphs(ap):
            return ap.rearrange("p (b d) -> p b d", b=TILE)

        block = ctx.enter_context(nc.Block())

        @block.sync
        def _(sp):
            sp.dma_start(not_next[:], dram["not_next"]).then_inc(not_next_in, 16)
            with sp.Fori(0, ROUNDS) as it:
                for s in range(SLOTS):
                    tile = bass.ds((it * SLOTS + s) * TILE, TILE)
                    sp.wait_ge(x_turned, it * SLOTS + s + 1)
                    sp.dma_start(graphs(x_in[:, s]), X[:, tile, :]).then_inc(x_loaded[s], 16)

        @block.scalar
        def _(act):
            for k, dst in enumerate((w, w_t, a1, a2, gamma, beta)):
                act.dma_start(dst[:], dram[("L2_W", "L2_W_t", "L2_a1", "L2_a2", "L2_gamma", "L2_beta")[k]]).then_inc(w_in, 16)
            act.wait_ge(wa_done, 1)
            nc.scalar.copy(wa1[:], ps[:, 0, 0:P])
            nc.scalar.copy(wa2[:], ps[:, 0, P:2 * P]).then_inc(wa_ready, 1)
            with act.Fori(0, ROUNDS) as it:
                def turn(s):
                    return it * SLOTS + s + 1
                for s in range(SLOTS):
                    act.wait_ge(x_turned, it * SLOTS + s + 1 + SLOTS)
                    nc.scalar.copy(xt[:, s], ps[:, 2 * s, :]).then_inc(xt_ready, 1)
                for s in range(SLOTS):
                    act.wait_ge(score_done, turn(s))
                    nc.scalar.copy(score[:, s], ps[:, 2 * s, :]).then_inc(score_copied, 1)
                for s in range(SLOTS):
                    act.wait_ge(top_ready, turn(s))
                    act.wait_ge(hn_ready, turn(s))
                    for g in range(TILE):
                        one = nc.scalar.activation(graph(att, s, g), graph(score, s, g), ACT.Exp,
                                                   bias=top[:, s, g:g + 1], accum_out=total[:, s, g:g + 1])
                    one.then_inc(exp_ready, 1)
                for s in range(SLOTS):
                    act.wait_ge(att_turned, turn(s))
                    nc.scalar.copy(att_t[:, s], ps[:, 2 * s, :]).then_inc(att_t_ready, 1)
                for s in range(SLOTS):
                    act.wait_ge(head_done, turn(s))
                    nc.scalar.copy(att[:, s], ps[:, 2 * s + 1, :]).then_inc(head_ready, 1)

        @block.gpsimd
        def _(pool):
            pool.sem_inc(hn_ready, SLOTS)
            pool.wait_ge(not_next_in, 16)
            with pool.Fori(0, ROUNDS) as it:
                def turn(s):
                    return it * SLOTS + s + 1
                for s in range(SLOTS):
                    part = adj[:, bass.ds((it * SLOTS + s) * TILE, TILE), :]
                    alone(pool, consts["identity_in"])
                    pool.wait_ge(barred, turn(s))
                    nc.gpsimd.tensor_tensor(part, part, not_next[:].unsqueeze(1).broadcast_to([P, TILE, P]),
                                            ALU.mult).then_inc(cut, 1)
                for s in range(SLOTS):
                    pool.wait_ge(total_inverted, turn(s))
                    steps = ((scale, total, total, ALU.mult), (scale, scale, None, ALU.mult),
                             (scale, scale, "eps", ALU.add), (scale, scale, "minus_half", ALU.pow),
                             (scale, scale, total, ALU.mult))
                    pool.wait_ge(moments_ready, turn(s))
                    for k, (dst, one, other, op) in enumerate(steps):
                        if k:
                            pool.wait_ge(scale_step, (it * SLOTS + s) * 4 + k)
                        if other is None:
                            second = mv[:, s, :, 1]
                        elif isinstance(other, str):
                            second = consts[other][:, 0:TILE]
                        else:
                            second = other[:, s]
                        nc.gpsimd.tensor_tensor(dst[:, s], one[:, s], second, op).then_inc(
                            scale_step if k < 4 else scale_ready, 1)
                for s in range(SLOTS):
                    pool.wait_ge(head_normed, turn(s))
                    nc.gpsimd.tensor_tensor(graphs(att[:, s]), graphs(att[:, s]),
                                            gamma[:].unsqueeze(1).broadcast_to([P, TILE, P]), ALU.mult).then_inc(gained, 1)
                    alone(pool, consts["identity_in"])
                    pool.wait_ge(gained, turn(s))
                    nc.gpsimd.tensor_tensor(hn[:, bass.ds((it * SLOTS + s) * TILE, TILE), :], graphs(att[:, s]),
                                            beta[:].unsqueeze(1).broadcast_to([P, TILE, P]), ALU.add).then_inc(hn_ready, 1)

        @block.vector
        def _(dve):
            with dve.Fori(0, ROUNDS) as it:
                def turn(s):
                    return it * SLOTS + s + 1
                for s in range(SLOTS):
                    nc.vector.tensor_scalar(graphs(bars[:, s]), adj[:, bass.ds((it * SLOTS + s) * TILE, TILE), :],
                                            0.0, NEG, ALU.is_le, ALU.mult).then_inc(barred, 1)
                for s in range(SLOTS):
                    dve.wait_ge(wh_done, turn(s))
                    nc.vector.tensor_copy(wh[:, s], ps[:, 2 * s + 1, :]).then_inc(wh_ready, 1)
                for s in range(SLOTS):
                    dve.wait_ge(score_copied, turn(s))
                    nc.vector.scalar_tensor_tensor(out=score[:, s], in0=score[:, s], scalar=ALPHA,
                                                   in1=ps[:, 2 * s, :], op0=ALU.mult, op1=ALU.max).then_inc(leaked, 1)
                    dve.wait_ge(leaked, turn(s))
                    dve.wait_ge(barred, turn(s))
                    nc.vector.tensor_tensor(score[:, s], score[:, s], bars[:, s], ALU.add).then_inc(masked, 1)
                    dve.wait_ge(masked, turn(s))
                    nc.vector.tensor_reduce(top[:, s], graphs(score[:, s]), AX_X, ALU.max).then_inc(top_found, 1)
                    dve.wait_ge(top_found, turn(s))
                    nc.vector.tensor_scalar(top[:, s], top[:, s], -1.0, None, ALU.mult).then_inc(top_ready, 1)
                for s in range(SLOTS):
                    dve.wait_ge(exp_ready, turn(s))
                    nc.vector.reciprocal(total[:, s], total[:, s]).then_inc(total_inverted, 1)
                for s in range(SLOTS):
                    dve.wait_ge(head_ready, turn(s))
                    for g in range(TILE):
                        one = nc.vector.bn_stats(stats[:, s, g, :], graph(att, s, g))
                    one.then_inc(stats_ready, 1)
                    alone(dve, consts["identity_in"])
                    dve.wait_ge(stats_ready, turn(s))
                    for g in range(TILE):
                        one = nc.vector.bn_aggr(mv[:, s, g, :], stats[:, s, g, :])
                    one.then_inc(moments_ready, 1)
                for s in range(SLOTS):
                    dve.wait_ge(scale_ready, turn(s))
                    for g in range(TILE):
                        one = nc.vector.tensor_scalar(graph(att, s, g), graph(att, s, g), mv[:, s, g, 0:1],
                                                      scale[:, s, g:g + 1], ALU.subtract, ALU.mult)
                    one.then_inc(head_normed, 1)

        @block.tensor
        def _(pe):
            pe.sem_inc(x_turned, SLOTS)
            pe.wait_ge(w_in, 96)
            nc.tensor.matmul(ps[:, 0, 0:P], w_t[:], a1[:], start=True, stop=True)
            nc.tensor.matmul(ps[:, 0, P:2 * P], w_t[:], a2[:], start=True, stop=True).then_inc(wa_done, 1)
            pe.wait_ge(wa_ready, 1)
            with pe.Fori(0, ROUNDS) as it:
                def turn(s):
                    return it * SLOTS + s + 1
                for s in range(SLOTS):
                    pe.wait_ge(x_loaded[s], it * 16 + 16)
                    for g in range(TILE):
                        one = nc.tensor.transpose(ps[:, 2 * s, g * P:(g + 1) * P], graph(x_in, s, g), identity[:])
                    one.then_inc(x_turned, 1)
                for s in range(SLOTS):
                    pe.wait_ge(xt_ready, turn(s))
                    for g in range(TILE):
                        one = nc.tensor.matmul(ps[:, 2 * s + 1, g * P:(g + 1) * P], graph(xt, s, g), w[:],
                                               start=True, stop=True)
                    one.then_inc(wh_done, 1)
                    nc.tensor.matmul(ps[:, 2 * s, :], wa2[:], xt[:, s], start=True, stop=False)
                    for g in range(TILE):
                        one = nc.tensor.matmul(ps[:, 2 * s, g * P:(g + 1) * P], graph(xt, s, g), wa1[:],
                                               start=False, stop=g == TILE - 1)
                    one.then_inc(score_done, 1)
                for s in range(SLOTS):
                    pe.wait_ge(exp_ready, turn(s))
                    for g in range(TILE):
                        one = nc.tensor.transpose(ps[:, 2 * s, g * P:(g + 1) * P], graph(att, s, g), identity[:])
                    one.then_inc(att_turned, 1)
                for s in range(SLOTS):
                    pe.wait_ge(att_t_ready, turn(s))
                    pe.wait_ge(wh_ready, turn(s))
                    for g in range(TILE):
                        one = nc.tensor.matmul(ps[:, 2 * s + 1, g * P:(g + 1) * P], graph(att_t, s, g), graph(wh, s, g),
                                               start=True, stop=True)
                    one.then_inc(head_done, 1)


def finish_attention(nc, X, hn, x_fm, consts, x_kept):
    with ExitStack() as ctx:
        def sb(name, shape):
            return ctx.enter_context(nc.sbuf_tensor(name, shape, F32))

        def sem(name):
            return ctx.enter_context(nc.semaphore(name))

        CHUNK = 8
        stats = sb("stats3", [P, 2, CHUNK, 6])
        mv = sb("mv3", [P, 2, CHUNK, 2])
        rstd = sb("rstd3", [P, 2, CHUNK])
        zeros = sb("zeros3", [P, CHUNK])
        shift = sb("shift3", [P, 2, CHUNK])
        staged = sb("staged", [P, 2, CHUNK, P])
        ps = ctx.enter_context(nc.psum_tensor("ps3", [P, 4, 512], F32))

        gelu_ready = sem("gelu_ready")
        added = sem("added2")
        stats_ready = sem("stats3_ready")
        moments_ready = sem("moments3_ready")
        var_eps = sem("var_eps3")
        rstd_ready = sem("rstd3_ready")
        zeros_set, shift_ready = sem("zeros3_set"), sem("shift3_ready")
        normed = sem("normed3")
        staged_in = [sem(f"staged_in{s}") for s in range(2)]
        kept = sem("kept")
        turned = sem("turned3")
        laid = sem("laid3")
        ROUNDS = B // CHUNK // 2

        block = ctx.enter_context(nc.Block())

        @block.sync
        def _(sp):
            with sp.Fori(0, ROUNDS) as it:
                for s in range(2):
                    part = bass.ds((it * 2 + s) * CHUNK, CHUNK)
                    alone(sp, consts["identity_in"])
                    sp.wait_ge(normed, it * 2 + s + 3)
                    alone(sp, consts["identity_in"])
                    sp.wait_ge(turned, it * 2 + s + 3)
                    sp.dma_start(staged[:, s], X[:, part, :]).then_inc(staged_in[s], 16)
                    sp.dma_start(x_kept[:, part, :], X[:, part, :]).then_inc(kept, 16)
            sp.wait_ge(kept, 16 * 2 * ROUNDS)

        @block.scalar
        def _(act):
            act.sem_inc(laid, 4)
            act.sem_inc(normed, 2)
            with act.Fori(0, ROUNDS) as it:
                for s in range(2):
                    part = hn[:, bass.ds((it * 2 + s) * CHUNK, CHUNK), :]
                    nc.scalar.activation(part, part, ACT.Gelu).then_inc(gelu_ready, 1)

            def normalise(it):
                for s in range(2):
                    alone(act, consts["identity_in"])
                    act.wait_ge(shift_ready, it * 2 + s + 1)
                    for b in range(CHUNK):
                        part = X[:, bass.ds((it * 2 + s) * CHUNK + b, 1), :]
                        one = nc.scalar.activation(part, part, ACT.Identity, bias=shift[:, s, b:b + 1],
                                                   scale=rstd[:, s, b:b + 1])
                    one.then_inc(normed, 1)

            def lay(it):
                for s in range(2):
                    for k in range(2):
                        alone(act, consts["identity_in"])
                        act.wait_ge(turned, it * 2 + s + 5)
                        nc.scalar.copy(x_fm[:, :, bass.ds((it * 2 + s) * CHUNK + k * 4, 4)],
                                       ps[:, 2 * s + k, :].rearrange("p (b n) -> p n b", b=4)).then_inc(laid, 1)

            normalise(0)
            with act.Fori(1, ROUNDS) as it:
                normalise(it)
                lay(it - 1)
            lay(ROUNDS - 1)

        @block.gpsimd
        def _(pool):
            nc.gpsimd.memset(zeros[:], 0.0).then_inc(zeros_set, 1)
            pool.wait_ge(zeros_set, 1)
            pool.sem_inc(rstd_ready, 2)
            with pool.Fori(0, ROUNDS) as it:
                for s in range(2):
                    pool.wait_ge(moments_ready, it * 2 + s + 1)
                    pool.wait_ge(normed, it * 2 + s + 1)
                    nc.gpsimd.tensor_tensor(shift[:, s, :], zeros[:], mv[:, s, :, 0], ALU.subtract)
                    nc.gpsimd.tensor_tensor(mv[:, s, :, 1], mv[:, s, :, 1], consts["eps"][:, 0:CHUNK],
                                            ALU.add).then_inc(var_eps, 1)
                    pool.wait_ge(var_eps, it * 2 + s + 1)
                    nc.gpsimd.tensor_tensor(rstd[:, s, :], mv[:, s, :, 1], consts["minus_half"][:, 0:CHUNK],
                                            ALU.pow).then_inc(rstd_ready, 1)
                    pool.wait_ge(rstd_ready, it * 2 + s + 3)
                    nc.gpsimd.tensor_tensor(shift[:, s, :], shift[:, s, :], rstd[:, s, :], ALU.mult).then_inc(shift_ready, 1)

        @block.vector
        def _(dve):
            with dve.Fori(0, ROUNDS) as it:
                for s in range(2):
                    at = (it * 2 + s) * CHUNK
                    dve.wait_ge(rstd_ready, it * 2 + s + 1)
                    dve.wait_ge(gelu_ready, it * 2 + s + 1)
                    part = X[:, bass.ds(at, CHUNK), :]
                    nc.vector.tensor_tensor(part, part, hn[:, bass.ds(at, CHUNK), :], ALU.add).then_inc(added, 1)
                    alone(dve, consts["identity_in"])
                    dve.wait_ge(added, it * 2 + s + 1)
                    for b in range(CHUNK):
                        one = nc.vector.bn_stats(stats[:, s, b, :], X[:, bass.ds(at + b, 1), :])
                    one.then_inc(stats_ready, 1)
                    alone(dve, consts["identity_in"])
                    dve.wait_ge(stats_ready, it * 2 + s + 1)
                    for b in range(CHUNK):
                        one = nc.vector.bn_aggr(mv[:, s, b, :], stats[:, s, b, :])
                    one.then_inc(moments_ready, 1)

        @block.tensor
        def _(pe):
            pe.sem_inc(turned, 4)
            with pe.Fori(0, ROUNDS) as it:
                for s in range(2):
                    pe.wait_ge(staged_in[s], it * 16 + 16)
                    pe.wait_ge(laid, it * 4 + 2 * s + 2)
                    for b in range(CHUNK):
                        one = nc.tensor.transpose(ps[:, 2 * s + b // 4, (b % 4) * P:(b % 4 + 1) * P],
                                                  staged[:, s, b, :], consts["identity"][:])
                    one.then_inc(turned, 1)


def gated_scan(nc, dram, X, adj, x_fm, consts, inverse_t, inverse, x_kept, out):
    with ExitStack() as ctx:
        def sb(name, shape, dt=F32):
            return ctx.enter_context(nc.sbuf_tensor(name, shape, dt))

        def sem(name):
            return ctx.enter_context(nc.semaphore(name))

        BLOCKS = SPAN // S
        GB = P // S
        NG = B // GB
        wx = sb("wx", [P, 3, P])
        wh = sb("wh3", [P, 3, P])
        bias_x = sb("bias_x", [P, 3])
        bias_h = sb("bias_h", [P, 3])
        bias = sb("bias3", [P, 3])
        parts = sb("parts", [PARTS[-1] + S, P // S, S, B], BF16)
        select_f = sb("select_f", [PARTS[-1] + S, S, P])
        select = sb("select", [PARTS[-1] + S, S, P], BF16)
        same_graph = sb("same_graph", [P, GB, S])
        between = sb("between", [P, P // SPAN, len(BLOCK_PAIRS), NG, S])
        step_mat = sb("step_mat", [P, 2, NG, GB, S])
        diag = sb("diag", [P, B, S])
        low = sb("low", [P, B, S])
        parts_nm = sb("parts_nm", [P, 3, S, B], BF16)
        inverse_8 = sb("inverse_8", [P, B, S])
        eye_8 = sb("eye_8", [P, S])
        same_block = sb("same_block", [P, P])
        inverse_group = sb("inverse_group", [P, NG, P])
        sums = sb("sums", [P, SPAN, B])
        delta = sb("delta", [P, S, B])
        h_new = sb("h_new", [P, S, B])
        delta_nm = sb("delta_nm", [P, BLOCKS - 1, NG, P])
        h_nm = sb("h_nm", [P, BLOCKS, NG, P])
        inverse_fm = sb("inverse_fm", [P, SPAN, B])
        result = sb("result", [P, BLOCKS, NG, P])
        stats = sb("stats4", [P, BLOCKS, NG, 6])
        mv = sb("mv4", [P, BLOCKS, NG, 2])
        rstd = sb("rstd4", [P, BLOCKS, NG])
        spare = sb("spare4", [P, 1])
        r = sb("r3", [P, B])
        z = sb("z3", [P, 2, B])
        hc = sb("hc", [P, 2, B])
        x_par = sb("x_par", [P, 2, B])
        xr = sb("xr", [P, B])
        near_x = sb("near_x", [P, B])
        near_z = sb("near_z", [P, B])
        z_near_x = sb("z_near_x", [P, B])
        early = sb("early", [P, B])
        late = sb("late", [P, B])
        zx = sb("zx", [P, 2, B])
        kept = sb("kept3", [P, 2, B])
        fresh = sb("fresh", [P, B])
        far = sb("far", [P, S, B])
        ps = ctx.enter_context(nc.psum_tensor("ps4", [P, 8, 512], F32))
        R, Z, C, CORR, COEF = (0, 1), (2, 3), 4, 5, (6, 7)
        TURN_H = COEF[0]
        TURN_DELTA = (COEF[1], COEF[0])
        BASE = (C, CORR, *COEF)
        SPREAD = Z[1]
        FILL = 3 * P
        identity = consts["identity"]

        w_in, small_in, select_in = sem("w3_in"), sem("small3_in"), sem("select_in")
        diag_in, diagonal_ready, inverse_done, split = sem("diag_in"), sem("diagonal_ready"), sem("inverse_done"), sem("split")
        between_in, between_ready, cleared = sem("between_in"), sem("between_ready"), sem("cleared")
        parts_out, parts_in = sem("parts_out"), sem("parts_in")
        bias_ready, select_ready = sem("bias_ready"), sem("select_ready")
        step_ready, pair_done = sem("step_mat_ready"), sem("pair_done")
        base_done, sums_ready = sem("base_done"), sem("sums_ready")
        r_done, z_done, c_done, coef_done = sem("r3_done"), sem("z3_done"), sem("c3_done"), sem("coef_done")
        r_ready, z_ready, hc_ready = sem("r3_ready"), sem("z3_ready"), sem("hc_ready")
        x_ready, xr_ready = sem("x_par_ready"), sem("xr_ready")
        near_x_ready, near_z_ready, z_near_x_ready = sem("near_x_ready"), sem("near_z_ready"), sem("z_near_x_ready")
        early_ready, late_ready = sem("early_ready"), sem("late_ready")
        fresh_ready, delta_ready = sem("fresh_ready"), sem("delta_ready")
        far_ready, near_added, far_added = sem("far_ready"), sem("near_added"), sem("far_added")
        zx_ready, kept_ready, h_ready = sem("zx_ready"), sem("kept_ready"), sem("h3_ready")
        delta_turned, delta_nm_ready, delta_nm_late = sem("delta_turned"), sem("delta_nm_ready"), sem("delta_nm_late")
        h_turned, h_nm_ready, rows_in = sem("h_turned"), sem("h_nm_ready"), sem("rows_in")
        inverse_in, kept_in, stored = sem("inverse_fm_in"), sem("kept_in"), sem("stored")
        added, stats_ready, moments_ready = sem("added4"), sem("stats4_ready"), sem("moments4_ready")
        var_eps, rstd_ready, normed = sem("var_eps4"), sem("rstd4_ready"), sem("normed4")

        def old(block, s, nodes=1):
            part = x_fm[:, bass.ds(block * S + s, nodes), :]
            return part.squeeze(1) if nodes == 1 else part

        block_of_engines = ctx.enter_context(nc.Block())

        @block_of_engines.sync
        def _(sp):
            sp.sem_inc(rows_in, 16)
            sp.dma_start(diag[:], dram["adj_diag"]).then_inc(diag_in, 16)
            sp.dma_start(eye_8[:], dram["eye_8"]).then_inc(diag_in, 16)
            sp.dma_start(same_block[:], dram["same_block"]).then_inc(diag_in, 16)
            sp.dma_start(wx[:], dram["L3_wx"]).then_inc(w_in, 16)
            sp.dma_start(wh[:], dram["L3_wh"]).then_inc(w_in, 16)
            sp.dma_start(select_f[:], dram["select"]).then_inc(select_in, 16)

            for n in range(S):
                sp.dma_start(inverse_group[n * GB:(n + 1) * GB],
                             inverse_t.rearrange("(b g) i -> b g i", g=NG)).then_inc(between_in, 16)
            sp.dma_start(between[:], dram["adj_between"]).then_inc(between_in, 16)

            def by_node(rows):
                return rows.rearrange("n (b g) d -> n b (g d)", g=NG)

            for span in range(P // SPAN):
                if span:
                    sp.wait_ge(sums_ready, (span - 1) * BLOCKS + 1)
                sp.dma_start(inverse_fm[:].rearrange("p i b -> p (i b)"),
                             dram["inverse_n"][span * SPAN:(span + 1) * SPAN, :].rearrange("i b -> (i b)").unsqueeze(0)
                             .broadcast_to([P, SPAN * B])).then_inc(inverse_in, 16)
                if span:
                    sp.wait_ge(normed, span)
                    for p in range(BLOCKS):
                        block = (span - 1) * BLOCKS + p
                        sp.dma_start(by_node(out[block * S:(block + 1) * S]),
                                     result[:, p].rearrange("p g d -> p (g d)")).then_inc(stored, 16)
                    sp.wait_ge(stored, span * BLOCKS * 16)
                for p in range(BLOCKS):
                    block = span * BLOCKS + p
                    sp.dma_start(result[:, p].rearrange("p g d -> p (g d)"),
                                 by_node(x_kept[block * S:(block + 1) * S])).then_inc(kept_in, 16)
                if span == 0:
                    sp.wait_ge(split, 6)
                    sp.dma_start(dram["parts"], parts_nm[:].rearrange("p k i b -> p k (i b)")).then_inc(parts_out, 16)
                    sp.wait_ge(parts_out, 16)
                    sp.wait_ge(cleared, 1)
                    for k, at in enumerate(PARTS):
                        sp.dma_start(parts[at:at + S].rearrange("n m i b -> n m (i b)"),
                                     dram["parts"][:, k, :].rearrange("(m n) f -> n m f", n=S)).then_inc(parts_in, 16)
                for p in range(BLOCKS):
                    block = span * BLOCKS + p
                    sp.wait_ge(h_nm_ready, block + 1)
                    sp.wait_ge(base_done, (span + 1) * NG)
                    sp.dma_start(by_node(X[block * S:(block + 1) * S]),
                                 h_nm[:, p].rearrange("p g d -> p (g d)")).then_inc(rows_in, 16)
            sp.wait_ge(normed, P // SPAN)
            for p in range(BLOCKS):
                block = P // S - BLOCKS + p
                sp.dma_start(by_node(out[block * S:(block + 1) * S]),
                             result[:, p].rearrange("p g d -> p (g d)")).then_inc(stored, 16)
            sp.wait_ge(stored, 16 * (P // S))
            sp.wait_ge(rows_in, 16 * (P // S) + 16)

        @block_of_engines.scalar
        def _(act):
            act.dma_start(bias_x[:], dram["L3_bx"]).then_inc(small_in, 16)
            act.dma_start(bias_h[:], dram["L3_bh"]).then_inc(small_in, 16)
            act.dma_start(same_graph[:], dram["same_graph"]).then_inc(small_in, 16)
            act.wait_ge(select_in, 16)
            nc.scalar.copy(select[:], select_f[:]).then_inc(select_ready, 1)
            act.wait_ge(bias_ready, 1)
            with act.Fori(0, P // SPAN) as span:
                for p in range(BLOCKS):
                    block = span * BLOCKS + p
                    for s in range(S):
                        turn = block * S + s + 1
                        at = slice(s * B, (s + 1) * B)
                        act.wait_ge(r_done, turn)
                        nc.scalar.activation(r[:], ps[:, R[p % 2], at], ACT.Sigmoid, bias=bias[:, 0:1]).then_inc(r_ready, 1)
                        act.wait_ge(z_done, turn)
                        nc.scalar.activation(z[:, s % 2], ps[:, Z[p % 2], at], ACT.Sigmoid,
                                             bias=bias[:, 1:2]).then_inc(z_ready, 1)
                        act.wait_ge(c_done, turn)
                        nc.scalar.activation(hc[:, s % 2], ps[:, C, s % 2 * B:(s % 2 + 1) * B], ACT.Tanh, bias=bias[:, 2:3]).then_inc(hc_ready, 1)
                    if p + 1 < BLOCKS:
                        act.wait_ge(delta_turned, (span * (BLOCKS - 1) + p) * 2 + 2)
                        nc.scalar.copy(delta_nm[:, p, 2:4].rearrange("p g d -> p (g d)"),
                                       ps[:, TURN_DELTA[1], 0:2 * P]).then_inc(delta_nm_late, 1)
                    act.wait_ge(h_turned, block + 1)
                    if p == 0:
                        act.wait_ge(rows_in, block * 16 + 16)
                        act.wait_ge(added, block + 1)
                    nc.scalar.copy(h_nm[:, p].rearrange("p g d -> p (g d)"), ps[:, TURN_H, :]).then_inc(h_nm_ready, 1)

        @block_of_engines.gpsimd
        def _(pool):
            nc.gpsimd.memset(parts[:], 0.0).then_inc(cleared, 1)
            pool.wait_ge(small_in, 48)
            pool.wait_ge(between_ready, len(BLOCK_PAIRS))

            def build(span, pair):
                alone(pool, consts["identity_in"])
                pool.wait_ge(pair_done, span * len(BLOCK_PAIRS) + pair + 1)
                nc.gpsimd.tensor_tensor(
                    step_mat[:, pair % 2],
                    between[:, bass.ds(span, 1), pair].squeeze(1).unsqueeze(2).broadcast_to([P, NG, GB, S]),
                    same_graph[:].unsqueeze(1).broadcast_to([P, NG, GB, S]), ALU.mult).then_inc(step_ready, 1)

            when = {(0, 2): 0, (0, 5): 1, (1, 2): 2, (1, 6): 3, (2, 1): 4, (2, 5): 5}
            with pool.Fori(0, P // SPAN) as span:
                for p in range(BLOCKS):
                    block = span * BLOCKS + p
                    for s in range(S):
                        turn = block * S + s + 1
                        if (p, s) in when:
                            build(span, when[p, s])
                        if s and s + 1 < S:
                            row = p * S + s + 1
                            pool.wait_ge(far_ready, block * (S - 2) + s)
                            pool.wait_ge(sums_ready, block + 1)
                            nc.gpsimd.tensor_tensor(sums[:, row], sums[:, row], far[:, s + 1], ALU.add).then_inc(near_added, 1)
                        pool.wait_ge(x_ready, turn)
                        pool.wait_ge(z_ready, turn)
                        nc.gpsimd.tensor_tensor(zx[:, s % 2], z[:, s % 2], x_par[:, s % 2], ALU.mult).then_inc(zx_ready, 1)
                        alone(pool, consts["identity_in"])
                        pool.wait_ge(zx_ready, turn)
                        nc.gpsimd.tensor_tensor(kept[:, s % 2], zx[:, s % 2], old(block, s), ALU.subtract).then_inc(kept_ready, 1)
                        if s and s + 2 < S:
                            rows = slice(p * S + s + 2, (p + 1) * S)
                            nc.gpsimd.tensor_tensor(sums[:, rows], sums[:, rows], far[:, s + 2:S], ALU.add).then_inc(far_added, 1)
                        if s == S - 1:
                            alone(pool, consts["identity_in"])
                            pool.wait_ge(delta_ready, turn - 1)
                            nc.gpsimd.tensor_tensor(h_new[:, 0:s], delta[:, 0:s], old(block, 0, s), ALU.add).then_inc(h_ready, 1)
                            alone(pool, consts["identity_in"])
                            pool.wait_ge(delta_ready, turn)
                            nc.gpsimd.tensor_tensor(h_new[:, s], delta[:, s], old(block, s), ALU.add).then_inc(h_ready, 1)
                for p in range(BLOCKS):
                    block = span * BLOCKS + p
                    pool.wait_ge(moments_ready, block + 1)
                    nc.gpsimd.tensor_tensor(mv[:, p, :, 1], mv[:, p, :, 1], consts["eps"][:, 0:NG],
                                            ALU.add).then_inc(var_eps, 1)
                    pool.wait_ge(var_eps, block + 1)
                    nc.gpsimd.tensor_tensor(rstd[:, p], mv[:, p, :, 1], consts["minus_half"][:, 0:NG],
                                            ALU.pow).then_inc(rstd_ready, 1)

        @block_of_engines.vector
        def _(dve):
            dve.wait_ge(diag_in, 48)
            nc.vector.tensor_tensor(inverse_8[:], inverse[:].unsqueeze(2).broadcast_to([P, B, S]),
                                    eye_8[:].unsqueeze(1).broadcast_to([P, B, S]), ALU.mult).then_inc(diagonal_ready, 1)
            dve.wait_ge(small_in, 48)
            nc.vector.tensor_tensor(bias[:], bias_x[:], bias_h[:], ALU.add).then_inc(bias_ready, 1)
            dve.wait_ge(inverse_done, 1)
            nc.vector.tensor_tensor(diag[:], diag[:], ps[:, SPREAD, :].rearrange("p (b i) -> p b i", i=S),
                                    ALU.mult).then_inc(split, 1)
            for k in range(3):
                rest, part = diag if k == 0 else low, parts_nm[:, k].rearrange("p i b -> p b i")
                dve.wait_ge(split, 2 * k + 1)
                nc.vector.tensor_copy(part, rest[:]).then_inc(split, 1)
                if k < 2:
                    dve.wait_ge(split, 2 * k + 2)
                    nc.vector.tensor_tensor(low[:], rest[:], part, ALU.subtract).then_inc(split, 1)
            dve.wait_ge(between_in, 16 * (S + 1))
            for pair, (_, target) in enumerate(BLOCK_PAIRS):
                columns = inverse_group[:].rearrange("p g (m i) -> p m g i", i=SPAN)[:, :, :, target * S:(target + 1) * S]
                nc.vector.tensor_tensor(between[:, :, pair], between[:, :, pair], columns, ALU.mult).then_inc(between_ready, 1)

            def coefficients(s):
                return ps[:, COEF[s % 2], :].rearrange("p (i b) -> p i b", b=B)

            def after_tanh(block, s):
                turn = block * S + s + 1
                dve.wait_ge(hc_ready, turn)
                if s + 1 < S:
                    step = block * (S - 1) + s + 1
                    dve.wait_ge(near_z_ready, step)
                    nc.vector.tensor_tensor(late[:], near_z[:], hc[:, s % 2], ALU.mult).then_inc(late_ready, 1)
                nc.vector.scalar_tensor_tensor(out=fresh[:], in0=z[:, s % 2], scalar=1.0, in1=hc[:, s % 2],
                                               op0=ALU.subtract, op1=ALU.mult, reverse0=True).then_inc(fresh_ready, 1)
                if s + 1 < S:
                    dve.wait_ge(early_ready, step)
                    dve.wait_ge(late_ready, step)
                    nc.vector.tensor_tensor(x_par[:, (s + 1) % 2], early[:], late[:], ALU.add).then_inc(x_ready, 1)
                dve.wait_ge(fresh_ready, turn)
                dve.wait_ge(kept_ready, turn)
                nc.vector.tensor_tensor(delta[:, s], fresh[:], kept[:, s % 2], ALU.add).then_inc(delta_ready, 1)
                if s + 2 < S:
                    if s:
                        dve.wait_ge(far_added, block * (S - 3) + s)
                    dve.wait_ge(delta_ready, turn)
                    nc.vector.tensor_tensor(far[:, s + 2:S], coefficients(s)[:, s + 2:S],
                                            delta[:, s].unsqueeze(1).broadcast_to([P, S - s - 2, B]),
                                            ALU.mult).then_inc(far_ready, 1)

            dve.sem_inc(added, 1)
            with dve.Fori(0, P // SPAN) as span:
                dve.wait_ge(inverse_in, span * 16 + 16)
                for g, bank in enumerate(BASE):
                    graphs = slice(g * GB, (g + 1) * GB)
                    dve.wait_ge(base_done, span * NG + g + 1)
                    copied = nc.vector.tensor_tensor(sums[:, :, graphs], ps[:, bank, :].rearrange("p (b i) -> p i b", i=SPAN),
                                                     inverse_fm[:, :, graphs], ALU.mult)
                copied.then_inc(sums_ready, 1)
                for p in range(BLOCKS):
                    block = span * BLOCKS + p
                    rows = slice(p * S + 1, (p + 1) * S)
                    if p == 0:
                        dve.wait_ge(sums_ready, block + 1)
                        nc.vector.tensor_copy(x_par[:, 0], sums[:, 0]).then_inc(x_ready, 1)
                    else:
                        corr = ps[:, CORR, :].rearrange("p (b i) -> p i b", i=S)
                        dve.wait_ge(pair_done, span * len(BLOCK_PAIRS) + PAIRS_UP_TO[p] + 2)
                        nc.vector.tensor_tensor(x_par[:, 0], sums[:, p * S], corr[:, 0], ALU.add).then_inc(x_ready, 1)
                        nc.vector.tensor_tensor(sums[:, rows], sums[:, rows], corr[:, 1:S], ALU.add).then_inc(sums_ready, 1)
                    for s in range(S):
                        turn, step = block * S + s + 1, block * (S - 1) + s + 1
                        if s:
                            after_tanh(block, s - 1)
                        dve.wait_ge(r_ready, turn)
                        dve.wait_ge(x_ready, turn)
                        nc.vector.tensor_tensor(xr[:], x_par[:, s % 2], r[:], ALU.mult).then_inc(xr_ready, 1)
                        if s + 1 < S:
                            near = coefficients(s)[:, s + 1]
                            dve.wait_ge(coef_done, step)
                            nc.vector.tensor_tensor(near_x[:], x_par[:, s % 2], near, ALU.mult).then_inc(near_x_ready, 1)
                            dve.wait_ge(z_ready, turn)
                            dve.wait_ge(near_x_ready, step)
                            nc.vector.tensor_tensor(z_near_x[:], z[:, s % 2], near_x[:], ALU.mult).then_inc(z_near_x_ready, 1)
                            nc.vector.scalar_tensor_tensor(out=near_z[:], in0=z[:, s % 2], scalar=1.0, in1=near,
                                                           op0=ALU.subtract, op1=ALU.mult, reverse0=True).then_inc(near_z_ready, 1)
                            dve.wait_ge(sums_ready, block + 1)
                            if s:
                                dve.wait_ge(near_added, block * (S - 2) + s)
                            dve.wait_ge(z_near_x_ready, step)
                            nc.vector.tensor_tensor(early[:], sums[:, p * S + s + 1], z_near_x[:], ALU.add).then_inc(early_ready, 1)
                    after_tanh(block, S - 1)
                    if p + 1 < BLOCKS:
                        dve.wait_ge(delta_turned, (span * (BLOCKS - 1) + p) * 2 + 1)
                        nc.vector.tensor_copy(delta_nm[:, p, 0:2].rearrange("p g d -> p (g d)"),
                                              ps[:, TURN_DELTA[0], 0:2 * P]).then_inc(delta_nm_ready, 1)
                for p in range(BLOCKS):
                    block = span * BLOCKS + p
                    dve.wait_ge(h_nm_ready, block + 1)
                    dve.wait_ge(kept_in, (span + 1) * BLOCKS * 16)
                    nc.vector.tensor_tensor(result[:, p], result[:, p], h_nm[:, p], ALU.add).then_inc(added, 1)
                    dve.wait_ge(added, block + 2)
                    for g in range(NG):
                        one = nc.vector.bn_stats(stats[:, p, g, :], result[:, p, g, :])
                    one.then_inc(stats_ready, 1)
                dve.wait_ge(stats_ready, (span + 1) * BLOCKS)
                nc.vector.memset(spare[:], 0.0)
                for p in range(BLOCKS):
                    for g in range(NG):
                        one = nc.vector.bn_aggr(mv[:, p, g, :], stats[:, p, g, :])
                    one.then_inc(moments_ready, 1)
                for p in range(BLOCKS):
                    dve.wait_ge(rstd_ready, span * BLOCKS + p + 1)
                    for g in range(NG):
                        one = nc.vector.tensor_scalar(result[:, p, g, :], result[:, p, g, :], mv[:, p, g, 0:1],
                                                      rstd[:, p, g:g + 1], ALU.subtract, ALU.mult)
                one.then_inc(normed, 1)

        @block_of_engines.tensor
        def _(pe):
            pe.sem_inc(pair_done, 2)
            pe.wait_ge(diagonal_ready, 1)
            nc.tensor.matmul(ps[:, SPREAD, :], same_block[:], inverse_8[:].rearrange("p b i -> p (b i)"), start=True,
                             stop=True).then_inc(inverse_done, 1)
            pe.wait_ge(w_in, 32)

            def gates_of_x(block, chunk, banks):
                gate, at = chunk // 4, chunk % 4
                nc.tensor.matmul(ps[:, banks[gate], at * 2 * B:(at + 1) * 2 * B], wx[:, gate, :], old(block, 2 * at, 2),
                                 start=at == 0, stop=False, skip_group_check=True)

            def tanh_of_x(block, s):
                nc.tensor.matmul(ps[:, C, 0:2 * B], wx[:, 2, :], old(block, s, 2), start=True, stop=False,
                                 skip_group_check=True)

            def keep_clock_up():
                nc.tensor.matmul(ps[:, C, 2 * B:2 * B + FILL], select[:, 0, :], select[:, 0:FILL // P, :], start=False,
                                 stop=True, skip_group_check=True)

            def spread(block, pair, g):
                k, target = BLOCK_PAIRS[pair]
                return nc.tensor.matmul(ps[:, CORR, :].rearrange("p (b g i) -> p g b i", g=NG, i=S)[:, g],
                                        delta_nm[:, k, g, :], step_mat[:, pair % 2, g], start=k == 0 and g == 0,
                                        stop=True, skip_group_check=True)

            def turn_block(slab, bank, groups):
                for at, g in enumerate(groups):
                    one = nc.tensor.transpose(ps[:, bank, at * P:(at + 1) * P],
                                              slab[:].rearrange("p n (b g) -> p g n b", g=NG)[:, g], identity[:])
                return one

            with pe.Fori(0, P // SPAN) as span:
                for chunk in range(8):
                    gates_of_x(span * BLOCKS, chunk, (R[0], Z[0]))
                pe.wait_ge(rows_in, span * BLOCKS * 16 + 16)
                for b in range(B):
                    at = b % GB
                    one = nc.tensor.matmul(ps[:, BASE[b // GB], at * SPAN:(at + 1) * SPAN], X[:, b, :],
                                           adj[:, b, bass.ds(span * SPAN, SPAN)], start=at == 0, stop=True,
                                           skip_group_check=True)
                    if at == GB - 1:
                        one.then_inc(base_done, 1)
                for p in range(BLOCKS):
                    block = span * BLOCKS + p
                    early_steps = [(pair, g) for pair, (k, target) in enumerate(BLOCK_PAIRS) if target == p + 1 and k < p
                                   for g in range(NG)]
                    for s in range(S):
                        turn, step = block * S + s + 1, block * (S - 1) + s + 1
                        column = slice(s * B, (s + 1) * B)
                        if s:
                            pe.wait_ge(early_ready, step - 1)
                            nc.tensor.matmul(ps[:, R[p % 2], column], wh[:, 0, :], early[:], start=False, stop=False,
                                             skip_group_check=True)
                            pe.wait_ge(late_ready, step - 1)
                            nc.tensor.matmul(ps[:, R[p % 2], column], wh[:, 0, :], late[:], start=False, stop=True,
                                             skip_group_check=True).then_inc(r_done, 1)
                            pe.wait_ge(x_ready, turn)
                        else:
                            pe.wait_ge(x_ready, turn)
                            nc.tensor.matmul(ps[:, R[p % 2], column], wh[:, 0, :], x_par[:, 0], start=False, stop=True,
                                             skip_group_check=True).then_inc(r_done, 1)
                        nc.tensor.matmul(ps[:, Z[p % 2], s * B:(s + 1) * B], wh[:, 1, :], x_par[:, s % 2], start=False,
                                         stop=True, skip_group_check=True).then_inc(z_done, 1)
                        if s + 1 < S:
                            if s > 1:
                                pe.wait_ge(far_ready, block * (S - 2) + s - 1)
                            if s == 0 and p == 0:
                                pe.wait_ge(select_ready, 1)
                                pe.wait_ge(parts_in, 16 * len(PARTS))
                            if s == 0 and p:
                                pe.wait_ge(h_nm_ready, block)
                            nc.tensor.matmul(ps[:, COEF[s % 2], (s + 1) * B:S * B], select[:, s, :],
                                             parts[:, bass.ds(block, 1), s + 1:S, :].squeeze(1), start=True,
                                             stop=True).then_inc(coef_done, 1)
                        if s == 0:
                            tanh_of_x(block, 0)
                        keep_clock_up()
                        pe.wait_ge(xr_ready, turn)
                        nc.tensor.matmul(ps[:, C, s % 2 * B:(s % 2 + 1) * B], wh[:, 2, :], xr[:], start=False, stop=True,
                                         skip_group_check=True).then_inc(c_done, 1)
                        if p + 1 < BLOCKS:
                            gates_of_x(block + 1, s, (R[(p + 1) % 2], Z[(p + 1) % 2]))
                        if s < len(early_steps):
                            pair, g = early_steps[s]
                            if s == 0:
                                pe.wait_ge(sums_ready, block + 1)
                            if g == 0:
                                pe.wait_ge(step_ready, span * len(BLOCK_PAIRS) + pair + 1)
                            one = spread(block, pair, g)
                            if g == NG - 1:
                                one.then_inc(pair_done, 1)
                        if s % 2 and s + 1 < S:
                            pe.wait_ge(hc_ready, turn)
                            tanh_of_x(block, s + 1)
                    if p + 1 < BLOCKS:
                        pe.wait_ge(delta_ready, (block + 1) * S)
                        turn_block(delta, TURN_DELTA[0], range(2)).then_inc(delta_turned, 1)
                        turn_block(delta, TURN_DELTA[1], range(2, NG)).then_inc(delta_turned, 1)
                        pair = BLOCK_PAIRS.index((p, p + 1))
                        pe.wait_ge(step_ready, span * len(BLOCK_PAIRS) + pair + 1)
                        pe.wait_ge(delta_nm_ready, span * (BLOCKS - 1) + p + 1)
                        for g in range(NG):
                            if g == 2:
                                pe.wait_ge(delta_nm_late, span * (BLOCKS - 1) + p + 1)
                            one = spread(block, pair, g)
                        one.then_inc(pair_done, 1)
                    pe.wait_ge(h_ready, (block + 1) * 2)
                    turn_block(h_new, TURN_H, range(NG)).then_inc(h_turned, 1)


def graph_layers(nc, dram, out):
    with ExitStack() as ctx:
        def sb(name, shape):
            return ctx.enter_context(nc.sbuf_tensor(name, shape, F32))

        def sem(name):
            return ctx.enter_context(nc.semaphore(name))

        X = sb("X", [P, B, P])
        adj = sb("adj", [P, B, P])
        node_degree = sb("node_degree", [P, B])
        degrees_ready = sem("degrees_ready")
        inverse_stored = sem("inverse_stored")
        consts = {"identity": sb("identity", [P, P]), "minus_half": sb("minus_half", [P, B]), "eps": sb("eps", [P, B]),
                  "identity_in": sem("identity_in")}
        with ExitStack() as groups:
            norm_t = groups.enter_context(nc.sbuf_tensor("norm_t", [Q, B, Q], F32))
            root_diag = groups.enter_context(nc.sbuf_tensor("root_diag", [Q, B, Q], F32))
            groups_ready = groups.enter_context(nc.semaphore("groups_ready"))
            gated_convolution(nc, dram, X, adj, consts, norm_t, root_diag, groups_ready, node_degree,
                              degrees_ready)
            group_convolution(nc, dram, X, consts, norm_t, root_diag, groups_ready, node_degree,
                              dram["inverse_t"], inverse_stored)
        x_fm = ctx.enter_context(nc.sbuf_tensor("x_fm", [P, P, B], F32))
        with ExitStack() as attention:
            hn = attention.enter_context(nc.sbuf_tensor("hn", [P, B, P], F32))
            graph_attention(nc, dram, X, adj, hn, consts)
            finish_attention(nc, X, hn, x_fm, consts, dram["x_kept"])
        gated_scan(nc, dram, X, adj, x_fm, consts, dram["inverse_t"], node_degree, dram["x_kept"], out)


def kernel(**inputs):
    import numpy as np
    import concourse.bacc as bacc
    from concourse.bass_utils import run_bass_kernel_spmd

    def lay(a):
        return np.ascontiguousarray(a)

    a = {k: np.asarray(v) for k, v in inputs.items()}
    x, adj = a["x"], a["adj"]
    group_of = [g for g, nodes in enumerate(GROUPS) for _ in nodes]
    blocks = np.zeros((Q, B, Q), adj.dtype)
    blocks_t = np.zeros((Q, B, Q), adj.dtype)
    for q, n in enumerate(ROWS):
        for p, m in enumerate(ROWS):
            if group_of[p] == group_of[q]:
                blocks[q, :, p] = adj[:, n, m]
                blocks_t[q, :, p] = adj[:, m, n]
    G = len(GROUPS)
    blocks_of = P // S
    by_block = adj.reshape(B, blocks_of, S, blocks_of, S)
    own = np.stack([by_block[:, m, :, m] for m in range(blocks_of)])
    spans, in_span = P // SPAN, SPAN // S
    between = np.stack([np.stack([by_block[:, m * in_span + k, :, m * in_span + target] for k, target in BLOCK_PAIRS])
                        for m in range(spans)])
    select = np.zeros((PARTS[-1] + S, S, P), np.float32)
    for s in range(S):
        for at in PARTS:
            select[at + s, s] = 1.0
    node = np.arange(P)
    gate = a["L3_gnn_W_ioux"].reshape(2, P, P).transpose(2, 0, 1), a["L3_gnn_W_iouh"].reshape(2, P, P).transpose(2, 0, 1)
    wide = (P, P)
    arrays = {
        "adj_diag": lay(own.transpose(0, 2, 1, 3).reshape(P, B, S)),
        "adj_between": lay(between.reshape(spans, len(BLOCK_PAIRS), P // S, B * S // P, S, S).transpose(
            4, 2, 0, 1, 3, 5).reshape(P, spans, len(BLOCK_PAIRS), B * S // P, S)),
        "not_next": (1 - ((node[:, None] + 1 == node) & (node % S != 0))).astype(np.float32),
        "eye_8": (node[:, None] % S == np.arange(S)).astype(np.float32),
        "same_block": (node[:, None] // S == node // S).astype(np.float32),
        "same_graph": lay(np.broadcast_to((node[:, None] % (P // S) == np.arange(P // S))[:, :, None],
                                          (P, P // S, S)).astype(np.float32)),
        "select": select,
        "L3_wx": lay(np.concatenate([gate[0], a["L3_gnn_W_coux"].T[:, None]], axis=1)),
        "L3_wh": lay(np.concatenate([gate[1], a["L3_gnn_W_couh"].T[:, None]], axis=1)),
        "L3_bx": lay(np.stack([*a["L3_gnn_b_ioux"].reshape(2, P), a["L3_gnn_b_coux"]], axis=1)),
        "L3_bh": lay(np.stack([*a["L3_gnn_b_iouh"].reshape(2, P), a["L3_gnn_b_couh"]], axis=1)),
        "L2_W": a["L2_gnn_W"],
        "L2_W_t": lay(a["L2_gnn_W"].T),
        "L2_a1": lay(np.broadcast_to(a["L2_gnn_a"][:P], wide)),
        "L2_a2": lay(np.broadcast_to(a["L2_gnn_a"][P:], wide)),
        "L2_gamma": lay(np.broadcast_to(a["L2_gnn_gamma"], wide)),
        "L2_beta": lay(np.broadcast_to(a["L2_gnn_beta"], wide)),
        "adj_groups": blocks,
        "adj_groups_t": blocks_t,
        "L1_W1": lay(a["L1_gnn_W1"].reshape(G, P, HALVES, P).transpose(1, 0, 2, 3)),
        "L1_W2": lay(a["L1_gnn_W2"].reshape(G, HALVES, P, P).transpose(2, 0, 1, 3)),
        "L1_b1": lay(a["L1_gnn_b1"].reshape(G, HALVES, P).transpose(2, 0, 1)),
        "L1_b2": lay(a["L1_gnn_b2"].T),
        "L1_fusion_w": lay(np.broadcast_to(a["L1_gnn_fusion_w"], (P, G))),
        "x_nm": lay(x.transpose(1, 0, 2)),
        "x_fm": lay(x.transpose(2, 0, 1).reshape(P, B * P)),
        "adj_nm": lay(adj.transpose(1, 0, 2)),
        "mask": lay(a["nodemask"].T),
        "identity": np.eye(P, dtype=np.float32),
        "L0_weight": lay(a["L0_gnn_weight"].transpose(1, 0, 2)),
        "L0_w_ih": lay(a["L0_gnn_w_ih"].reshape(3, P, P).transpose(2, 0, 1)),
        "L0_w_hh": lay(a["L0_gnn_w_hh"].reshape(3, P, P).transpose(2, 0, 1)),
        "L0_b_ih": lay(a["L0_gnn_b_ih"].reshape(3, P).T),
        "L0_b_hh": lay(a["L0_gnn_b_hh"].reshape(3, P).T),
    }
    nc = bacc.Bacc("TRN2", target_bir_lowering=False, num_devices=1)
    dram = {name: nc.dram_tensor(f"in_{name}", v.shape, F32, kind="ExternalInput").ap() for name, v in arrays.items()}
    dram["inverse_t"] = nc.dram_tensor("inverse_t", (B, P), F32, kind="Internal").ap()
    dram["inverse_n"] = nc.dram_tensor("inverse_by_node", (P, B), F32, kind="Internal").ap()
    dram["x_kept"] = nc.dram_tensor("x_kept_scratch", (P, B, P), F32, kind="Internal").ap()
    dram["parts"] = nc.dram_tensor("parts_scratch", (P, 3, S * B), BF16, kind="Internal").ap()
    out = nc.dram_tensor("out_nm", (P, B, P), F32, kind="ExternalOutput").ap()
    graph_layers(nc, dram, out)
    result = run_bass_kernel_spmd(nc, [{f"in_{name}": v for name, v in arrays.items()}], core_ids=[0])
    return lay(result.results[0]["out_nm"].transpose(1, 0, 2))
```
